# Optimizing a Trainium2 kernel written in Bass

```python
import numpy as np
import jax
import jax.numpy as jnp

def _softmax(x, axis=-1):
    return jax.nn.softmax(x, axis=axis)

def _gelu(x):
    return jax.nn.gelu(x, approximate=True)

def _silu(x):
    return jax.nn.silu(x)

def _sigmoid(x):
    return jax.nn.sigmoid(x)

def _layernorm(x, axis=-1, eps=1e-05):
    m = jnp.mean(x, axis=axis, keepdims=True)
    v = jnp.var(x, axis=axis, keepdims=True)
    return (x - m) / jnp.sqrt(v + eps)

def _scatter_add(tgt, idx, src, axis=0):
    return tgt.at[idx].add(src)

def _segment_sum(src, seg, n):
    return jax.ops.segment_sum(src, seg, n)
kernel_name = 'mk_decoder_postln_d2_seqx_r8_b80cb1'

def setup_inputs(seed: int=0):
    np.random.seed(seed)
    _w = jnp.asarray

    def _rec_inputs():
        import jax
        import jax.numpy as jnp
        _rk = jax.random.key(seed)
        x = 0.0003765 + 1 * jax.random.normal(jax.random.fold_in(_rk, 1), (8, 128, 256), jnp.float32)
        _lenS = 128 - jax.random.randint(jax.random.fold_in(_rk, 7), (8,), 0, max(1, 128 // 4) + 1, jnp.int32)
        _lenS2 = 128 - jax.random.randint(jax.random.fold_in(_rk, 8), (8,), 0, max(1, 128 // 4) + 1, jnp.int32)
        _ctx_2048P = jax.random.normal(jax.random.fold_in(_rk, 11), (8, 16, 256), jnp.float32)
        _ctx_2048c = jax.random.dirichlet(jax.random.fold_in(_rk, 511), 0.3 * jnp.ones((16,), jnp.float32), (8, 128))
        _ctx_2048t = jnp.einsum('bsk,bkd->bsd', _ctx_2048c, _ctx_2048P)
        _ctx_2048t = _ctx_2048t * jax.lax.rsqrt(jnp.mean(jnp.square(_ctx_2048t)) + 1e-12) * 0.953939
        ctx_2048 = -0.000292821 + 1.00034 * (_ctx_2048t + 0.3 * jax.random.normal(jax.random.fold_in(_rk, 611), (8, 128, 256), jnp.float32))
        return (x, ctx_2048)
    x, ctx_2048 = _rec_inputs()

    def _L0_attn_setup():
        import jax, jax.numpy as jnp
        import numpy as np
        NUM_HEADS = 16
        CHUNK = 128

        def _bitlinear(x, w, b):
            w_scale = jnp.maximum(jnp.mean(jnp.abs(w)), 1e-05)
            w_norm = w / w_scale
            w_q = jax.lax.stop_gradient(jnp.sign(w_norm) - w_norm) + w_norm
            x_scale = jnp.maximum(jnp.max(jnp.abs(x), axis=-1, keepdims=True), 1e-05)
            x_norm = x / x_scale * 127.0
            x_q = jax.lax.stop_gradient(jnp.round(x_norm) - x_norm) + x_norm
            return jnp.einsum('...i,oi->...o', x_q, w_q) * (x_scale * w_scale / 127.0) + b

        def _rmsnorm(x, w, eps=1e-06):
            return x * jax.lax.rsqrt(jnp.mean(x * x, axis=-1, keepdims=True) + eps) * w
        key = jax.random.key(seed)
        ks = jax.random.split(key, 8)
        B, N, C = (2, 512, 256)

        def w(k, shape):
            return jax.random.normal(k, shape, jnp.float32) * 0.02
        return {'x': jax.random.normal(ks[0], (B, N, C), jnp.float32), 'qkv_w': w(ks[1], (3 * C, C)), 'qkv_b': w(ks[2], (3 * C,)), 'gate_w': w(ks[3], (C, C)), 'gate_b': w(ks[4], (C,)), 'proj_w': w(ks[5], (C, C)), 'proj_b': w(ks[6], (C,)), 'norm_w': jnp.ones((C,), jnp.float32)}
    _L0_attn_all = _L0_attn_setup()
    _L0_attn_in = {k: v for k, v in _L0_attn_all.items() if k in ('qkv_w', 'qkv_b', 'gate_w', 'gate_b', 'proj_w', 'proj_b', 'norm_w')}
    del _L0_attn_all

    def _L0_xattn_setup():
        import jax, jax.numpy as jnp
        import numpy as np
        key = jax.random.key(seed)
        k1, k2, k3, k4, k5 = jax.random.split(key, 5)
        B, D_MODEL, L = (2, 128, 256)
        HEAD_DIM = 8
        H = D_MODEL // HEAD_DIM
        return {'k': jax.random.normal(k1, (B, D_MODEL, L), dtype=jnp.float32), 'v': jax.random.normal(k2, (B, D_MODEL, L), dtype=jnp.float32), 'q': jax.random.normal(k3, (B, D_MODEL, L), dtype=jnp.float32), 'ssm_kernel': jax.random.normal(k4, (H, L), dtype=jnp.float32), 'D': jax.random.normal(k5, (H,), dtype=jnp.float32), 'head_dim': HEAD_DIM}
    _L0_xattn_all = _L0_xattn_setup()
    _L0_xattn_in = {k: v for k, v in _L0_xattn_all.items() if k in ('ssm_kernel', 'D')}
    del _L0_xattn_all

    def _L0_ffn_setup():
        import jax, jax.numpy as jnp
        import numpy as np
        TOP_K = 2
        key = jax.random.key(seed)
        ks = jax.random.split(key, 6)
        B, S, H, F, E = (1, 256, 256, 176, 8)
        Fs = 2 * F
        std = jnp.float32(0.02)
        return {'hidden_states': jax.random.normal(ks[0], (B, S, H), jnp.float32), 'gate_weight': jax.random.normal(ks[1], (E, H), jnp.float32) * std, 'gate_up_weights': jax.random.normal(ks[2], (E, 2 * F, H), jnp.float32) * std, 'down_weights': jax.random.normal(ks[3], (E, H, F), jnp.float32) * std, 'shared_gate_up': jax.random.normal(ks[4], (2 * Fs, H), jnp.float32) * std, 'shared_down': jax.random.normal(ks[5], (H, Fs), jnp.float32) * std}
    _L0_ffn_all = _L0_ffn_setup()
    _L0_ffn_in = {k: v for k, v in _L0_ffn_all.items() if k in ('gate_weight', 'gate_up_weights', 'down_weights', 'shared_gate_up', 'shared_down')}
    del _L0_ffn_all

    def _L1_attn_setup():
        import jax, jax.numpy as jnp
        import numpy as np
        B, S, E, H, D = (2, 256, 256, 16, 128)
        ROPE_THETA = 10000.0

        def apply_rope(t, start_pos=0):
            d = t.shape[-1]
            s = t.shape[-2]
            inv_freq = 1.0 / ROPE_THETA ** (jnp.arange(0, d, 2, dtype=jnp.float32) / d)
            pos = jnp.arange(start_pos, start_pos + s, dtype=jnp.float32)
            ang = pos[:, None] * inv_freq[None, :]
            cos, sin = (jnp.cos(ang), jnp.sin(ang))
            x1 = t[..., 0::2]
            x2 = t[..., 1::2]
            r1 = x1 * cos - x2 * sin
            r2 = x1 * sin + x2 * cos
            return jnp.stack([r1, r2], axis=-1).reshape(t.shape)
        key = jax.random.key(seed)
        ks = jax.random.split(key, 5)
        sc = lambda fan_in: 1.0 / np.sqrt(fan_in)
        return {'x': jax.random.normal(ks[0], (B, S, E), dtype=jnp.float32), 'Wq': jax.random.normal(ks[1], (E, H * D), dtype=jnp.float32) * sc(E), 'bq': jnp.zeros((H * D,), dtype=jnp.float32), 'Wk': jax.random.normal(ks[2], (E, D), dtype=jnp.float32) * sc(E), 'bk': jnp.zeros((D,), dtype=jnp.float32), 'Wv': jax.random.normal(ks[3], (E, D), dtype=jnp.float32) * sc(E), 'bv': jnp.zeros((D,), dtype=jnp.float32), 'Wo': jax.random.normal(ks[4], (H * D, E), dtype=jnp.float32) * sc(H * D), 'bo': jnp.zeros((E,), dtype=jnp.float32)}
    _L1_attn_all = _L1_attn_setup()
    _L1_attn_in = {k: v for k, v in _L1_attn_all.items() if k in ('Wq', 'bq', 'Wk', 'bk', 'Wv', 'bv', 'Wo', 'bo')}
    del _L1_attn_all

    def _L1_xattn_setup():
        import jax, jax.numpy as jnp
        import numpy as np
        DIM = 256
        NHEADS = 32
        HEAD_DIM = DIM // NHEADS
        EPS = 1e-06

        def _rmsnorm(t):
            return t * jax.lax.rsqrt(jnp.mean(t * t, axis=-1, keepdims=True) + EPS)
        key = jax.random.key(seed)
        kx, kc, kq, kk, kv = jax.random.split(key, 5)
        x = jax.random.normal(kx, (2, 512, DIM), dtype=jnp.float32)
        context = jax.random.normal(kc, (2, 64, DIM), dtype=jnp.float32)
        std = 0.02
        Wq = jax.random.normal(kq, (DIM, DIM), dtype=jnp.float32) * std
        Wk = jax.random.normal(kk, (DIM, DIM), dtype=jnp.float32) * std
        Wv = jax.random.normal(kv, (DIM, DIM), dtype=jnp.float32) * std
        return {'x': x, 'context': context, 'Wq': Wq, 'Wk': Wk, 'Wv': Wv}
    _L1_xattn_all = _L1_xattn_setup()
    _L1_xattn_in = {k: v for k, v in _L1_xattn_all.items() if k in ('Wq', 'Wk', 'Wv')}
    del _L1_xattn_all

    def _L1_ffn_setup():
        import jax, jax.numpy as jnp
        import numpy as np
        B, S, D = (4, 512, 256)
        DFF = 4 * D
        SKIP = 0.125
        key = jax.random.key(seed)
        ks = jax.random.split(key, 4)
        s_in = 1.0 / np.sqrt(D).astype(np.float32)
        s_ff = 1.0 / np.sqrt(DFF).astype(np.float32)
        return {'x': jax.random.normal(ks[0], (B, S, D), jnp.float32), 'Wr': jax.random.normal(ks[1], (D, 1), jnp.float32) * s_in, 'br': jnp.zeros((1,), jnp.float32), 'W1': jax.random.normal(ks[2], (D, DFF), jnp.float32) * s_in, 'b1': jnp.zeros((DFF,), jnp.float32), 'W2': jax.random.normal(ks[3], (DFF, D), jnp.float32) * s_ff, 'b2': jnp.zeros((D,), jnp.float32)}
    _L1_ffn_all = _L1_ffn_setup()
    _L1_ffn_in = {k: v for k, v in _L1_ffn_all.items() if k in ('Wr', 'br', 'W1', 'b1', 'W2', 'b2')}
    del _L1_ffn_all
    return {'x': x, 'ctx_2048': ctx_2048, 'L0_attn_qkv_w': _L0_attn_in['qkv_w'], 'L0_attn_qkv_b': _L0_attn_in['qkv_b'], 'L0_attn_gate_w': _L0_attn_in['gate_w'], 'L0_attn_gate_b': _L0_attn_in['gate_b'], 'L0_attn_proj_w': _L0_attn_in['proj_w'], 'L0_attn_proj_b': _L0_attn_in['proj_b'], 'L0_attn_norm_w': _L0_attn_in['norm_w'], 'L0_xattn_ssm_kernel': _L0_xattn_in['ssm_kernel'], 'L0_xattn_D': _L0_xattn_in['D'], 'L0_ffn_gate_weight': _L0_ffn_in['gate_weight'], 'L0_ffn_gate_up_weights': _L0_ffn_in['gate_up_weights'], 'L0_ffn_down_weights': _L0_ffn_in['down_weights'], 'L0_ffn_shared_gate_up': _L0_ffn_in['shared_gate_up'], 'L0_ffn_shared_down': _L0_ffn_in['shared_down'], 'L1_attn_Wq': _L1_attn_in['Wq'], 'L1_attn_bq': _L1_attn_in['bq'], 'L1_attn_Wk': _L1_attn_in['Wk'], 'L1_attn_bk': _L1_attn_in['bk'], 'L1_attn_Wv': _L1_attn_in['Wv'], 'L1_attn_bv': _L1_attn_in['bv'], 'L1_attn_Wo': _L1_attn_in['Wo'], 'L1_attn_bo': _L1_attn_in['bo'], 'L1_xattn_Wq': _L1_xattn_in['Wq'], 'L1_xattn_Wk': _L1_xattn_in['Wk'], 'L1_xattn_Wv': _L1_xattn_in['Wv'], 'L1_ffn_Wr': _L1_ffn_in['Wr'], 'L1_ffn_br': _L1_ffn_in['br'], 'L1_ffn_W1': _L1_ffn_in['W1'], 'L1_ffn_b1': _L1_ffn_in['b1'], 'L1_ffn_W2': _L1_ffn_in['W2'], 'L1_ffn_b2': _L1_ffn_in['b2']}

def reference(x, ctx_2048, L0_attn_qkv_w, L0_attn_qkv_b, L0_attn_gate_w, L0_attn_gate_b, L0_attn_proj_w, L0_attn_proj_b, L0_attn_norm_w, L0_xattn_ssm_kernel, L0_xattn_D, L0_ffn_gate_weight, L0_ffn_gate_up_weights, L0_ffn_down_weights, L0_ffn_shared_gate_up, L0_ffn_shared_down, L1_attn_Wq, L1_attn_bq, L1_attn_Wk, L1_attn_bk, L1_attn_Wv, L1_attn_bv, L1_attn_Wo, L1_attn_bo, L1_xattn_Wq, L1_xattn_Wk, L1_xattn_Wv, L1_ffn_Wr, L1_ffn_br, L1_ffn_W1, L1_ffn_b1, L1_ffn_W2, L1_ffn_b2):
    import jax
    import jax.numpy as jnp

    def _L0_attn_ref(x, qkv_w, qkv_b, gate_w, gate_b, proj_w, proj_b, norm_w):
        import jax, jax.numpy as jnp
        import numpy as np
        NUM_HEADS = 16
        CHUNK = 128

        def _bitlinear(x, w, b):
            w_scale = jnp.maximum(jnp.mean(jnp.abs(w)), 1e-05)
            w_norm = w / w_scale
            w_q = jax.lax.stop_gradient(jnp.sign(w_norm) - w_norm) + w_norm
            x_scale = jnp.maximum(jnp.max(jnp.abs(x), axis=-1, keepdims=True), 1e-05)
            x_norm = x / x_scale * 127.0
            x_q = jax.lax.stop_gradient(jnp.round(x_norm) - x_norm) + x_norm
            return jnp.einsum('...i,oi->...o', x_q, w_q) * (x_scale * w_scale / 127.0) + b

        def _rmsnorm(x, w, eps=1e-06):
            return x * jax.lax.rsqrt(jnp.mean(x * x, axis=-1, keepdims=True) + eps) * w
        B, N, C = x.shape
        H, L = (NUM_HEADS, CHUNK)
        D = C // H
        scale = D ** (-0.5)
        qkv = _bitlinear(x, qkv_w, qkv_b).reshape(B, N, 3, H, D)
        q, k, v = (qkv[:, :, 0], qkv[:, :, 1], qkv[:, :, 2])
        g = jax.nn.sigmoid(_bitlinear(x, gate_w, gate_b)).reshape(B, N, H, D)
        nc = N // L

        def chunks(t):
            return t.reshape(B, nc, L, H, D).transpose(1, 0, 2, 3, 4)
        qc, kc, vc, gc = map(chunks, (q, k, v, g))

        def step(kv_state, inp):
            qi, ki, vi, gi = inp
            attn = jax.nn.softmax(jnp.einsum('blhd,blgd->blhg', qi, ki) * scale, axis=-1)
            local = jnp.einsum('blhg,blgd->blhd', attn, vi)
            recur = jnp.einsum('blhd,bhde->blhe', qi, kv_state)
            decay = jnp.mean(gi, axis=1)[..., None]
            kv_update = jnp.einsum('blhd,blhe->bhde', ki, vi)
            return (kv_state * decay + kv_update, local + recur)
        kv0 = jnp.zeros((B, H, D, D), x.dtype)
        _, out = jax.lax.scan(step, kv0, (qc, kc, vc, gc))
        out = out.transpose(1, 0, 2, 3, 4).reshape(B, N, C)
        return _bitlinear(_rmsnorm(out, norm_w), proj_w, proj_b)

    def _L0_xattn_ref(k, v, q, ssm_kernel, D, head_dim):
        import jax, jax.numpy as jnp
        import numpy as np
        B, HD, L = k.shape
        H = HD // head_dim
        fft_size = 2 * L
        k_ = k.reshape(B, H, head_dim, L)
        v_ = v.reshape(B, H, head_dim, L)
        q_ = q.reshape(B, H, head_dim, L)
        kv = jnp.einsum('bhil,bhjl->bijhl', k_, v_)
        kv_f = jnp.fft.rfft(kv, n=fft_size)
        kernel_f = jnp.fft.rfft(ssm_kernel, n=fft_size)
        y = jnp.fft.irfft(kv_f * kernel_f, n=fft_size)[..., :L]
        out = y + kv * D[None, None, None, :, None]
        out = jnp.einsum('bijhl,bhil->bjhl', out, q_)
        out = jnp.transpose(out, (0, 2, 1, 3)).reshape(B, H * head_dim, L)
        return out.astype(k.dtype)

    def _L0_ffn_ref(hidden_states, gate_weight, gate_up_weights, down_weights, shared_gate_up, shared_down):
        import jax, jax.numpy as jnp
        import numpy as np
        TOP_K = 2
        B, S, H = hidden_states.shape
        E, twoF, _ = gate_up_weights.shape
        F = twoF // 2
        T = B * S
        x = hidden_states.reshape(T, H)
        logits = x @ gate_weight.T
        scores = jax.nn.softmax(logits, axis=-1)
        topk_w, topk_idx = jax.lax.top_k(scores, TOP_K)
        combine = jnp.zeros((T, E), x.dtype).at[jnp.arange(T)[:, None], topk_idx].add(topk_w)
        gu = jnp.einsum('th,efh->tef', x, gate_up_weights)
        act = jax.nn.silu(gu[..., :F]) * gu[..., F:]
        y = jnp.einsum('tef,te,ehf->th', act, combine, down_weights)
        Fs = shared_gate_up.shape[0] // 2
        sgu = x @ shared_gate_up.T
        sact = jax.nn.silu(sgu[:, :Fs]) * sgu[:, Fs:]
        y = y + sact @ shared_down.T
        return y.reshape(B, S, H)

    def _L1_attn_ref(x, Wq, bq, Wk, bk, Wv, bv, Wo, bo):
        import jax, jax.numpy as jnp
        import numpy as np
        B, S, E, H, D = (2, 256, 256, 16, 128)
        ROPE_THETA = 10000.0

        def apply_rope(t, start_pos=0):
            d = t.shape[-1]
            s = t.shape[-2]
            inv_freq = 1.0 / ROPE_THETA ** (jnp.arange(0, d, 2, dtype=jnp.float32) / d)
            pos = jnp.arange(start_pos, start_pos + s, dtype=jnp.float32)
            ang = pos[:, None] * inv_freq[None, :]
            cos, sin = (jnp.cos(ang), jnp.sin(ang))
            x1 = t[..., 0::2]
            x2 = t[..., 1::2]
            r1 = x1 * cos - x2 * sin
            r2 = x1 * sin + x2 * cos
            return jnp.stack([r1, r2], axis=-1).reshape(t.shape)
        b, s, _ = x.shape
        q = (x @ Wq + bq).reshape(b, s, H, D).transpose(0, 2, 1, 3)
        k = (x @ Wk + bk).reshape(b, s, 1, D).transpose(0, 2, 1, 3)
        v = (x @ Wv + bv).reshape(b, s, 1, D).transpose(0, 2, 1, 3)
        q = apply_rope(q)
        k = apply_rope(k)
        scores = jnp.einsum('bhqd,bxkd->bhqk', q, k) / jnp.sqrt(jnp.float32(D))
        causal = jnp.tril(jnp.ones((s, s), dtype=bool))
        scores = jnp.where(causal, scores, -jnp.inf)
        attn = jax.nn.softmax(scores, axis=-1)
        out = jnp.einsum('bhqk,bxkd->bhqd', attn, v)
        out = out.transpose(0, 2, 1, 3).reshape(b, s, H * D)
        return out @ Wo + bo

    def _L1_xattn_ref(x, context, Wq, Wk, Wv):
        import jax, jax.numpy as jnp
        import numpy as np
        DIM = 256
        NHEADS = 32
        HEAD_DIM = DIM // NHEADS
        EPS = 1e-06

        def _rmsnorm(t):
            return t * jax.lax.rsqrt(jnp.mean(t * t, axis=-1, keepdims=True) + EPS)
        b, n, _ = x.shape
        m = context.shape[1]
        q = x @ Wq.T
        k_raw = context @ Wk.T
        v_raw = context @ Wv.T
        q = q.reshape(b, n, NHEADS, HEAD_DIM).transpose(0, 2, 1, 3)
        kv = jnp.concatenate([k_raw, v_raw], axis=-1)
        kv = kv.reshape(b, m, NHEADS, HEAD_DIM, 2)
        k = kv[..., 0].transpose(0, 2, 1, 3)
        v = kv[..., 1].transpose(0, 2, 1, 3)
        q = _rmsnorm(q)
        k = _rmsnorm(k)
        scale = HEAD_DIM ** (-0.5)
        scores = jnp.einsum('bhnd,bhmd->bhnm', q, k) * scale
        attn = jax.nn.softmax(scores, axis=-1)
        out = jnp.einsum('bhnm,bhmd->bhnd', attn, v)
        return out.transpose(0, 2, 1, 3).reshape(b, n, NHEADS * HEAD_DIM)

    def _L1_ffn_ref(x, Wr, br, W1, b1, W2, b2):
        import jax, jax.numpy as jnp
        import numpy as np
        B, S, D = (4, 512, 256)
        DFF = 4 * D
        SKIP = 0.125
        Bs, Ss, Ds = x.shape
        k = max(int(Ss * SKIP), 1)
        logits = (x @ Wr + br)[..., 0]
        weights, idx = jax.lax.top_k(logits, k)
        perm = jnp.argsort(idx, axis=1)
        tokens = jnp.take_along_axis(idx, perm, axis=1)
        fx = jnp.take_along_axis(x, tokens[..., None], axis=1)
        h = jax.nn.gelu(fx @ W1 + b1, approximate=False)
        out_l = h @ W2 + b2
        tw = jax.nn.softmax(weights, axis=1)
        rw = jnp.take_along_axis(tw, perm, axis=1)
        xw = rw[..., None] * out_l
        bidx = jnp.arange(Bs)[:, None]
        return x.at[bidx, tokens].add(xw)
    x = _layernorm(x + _L0_attn_ref(x, L0_attn_qkv_w, L0_attn_qkv_b, L0_attn_gate_w, L0_attn_gate_b, L0_attn_proj_w, L0_attn_proj_b, L0_attn_norm_w), axis=-1)
    x = _layernorm(x + _L0_xattn_ref(ctx_2048, ctx_2048, x, L0_xattn_ssm_kernel, L0_xattn_D, 8), axis=-1)
    x = _layernorm(x + _L0_ffn_ref(x, L0_ffn_gate_weight, L0_ffn_gate_up_weights, L0_ffn_down_weights, L0_ffn_shared_gate_up, L0_ffn_shared_down), axis=-1)
    x = _layernorm(x + _L1_attn_ref(x, L1_attn_Wq, L1_attn_bq, L1_attn_Wk, L1_attn_bk, L1_attn_Wv, L1_attn_bv, L1_attn_Wo, L1_attn_bo), axis=-1)
    x = _layernorm(x + _L1_xattn_ref(x, ctx_2048, L1_xattn_Wq, L1_xattn_Wk, L1_xattn_Wv), axis=-1)
    x = _layernorm(x + _L1_ffn_ref(x, L1_ffn_Wr, L1_ffn_br, L1_ffn_W1, L1_ffn_b1, L1_ffn_W2, L1_ffn_b2), axis=-1)
    return x

_drawn_inputs = setup_inputs


def setup_inputs(seed=0):
    import zlib

    import numpy as np

    out = dict(_drawn_inputs(seed))
    spreads = {'L0_attn_norm_w': (1.0, 0.2),
     'L1_attn_bq': (0.0, 0.4),
     'L1_attn_bk': (0.0, 0.649),
     'L1_attn_bv': (0.0, 0.1),
     'L1_attn_bo': (0.0, 0.1),
     'L1_ffn_b1': (0.0, 2.0),
     'L1_ffn_b2': (0.0, 2.0)}
    factors = {'L0_ffn_gate_weight': 8.0,
     'L0_ffn_gate_up_weights': 8.0,
     'L0_ffn_down_weights': 8.0,
     'L0_ffn_shared_gate_up': 2.831,
     'L0_ffn_shared_down': 2.827,
     'L1_ffn_Wr': 7.241,
     'L1_ffn_W1': 8.0,
     'L1_ffn_W2': 7.35}
    for name, (base, spread) in spreads.items():
        noise = np.random.default_rng([zlib.crc32(name.encode()), seed]).standard_normal(out[name].shape)
        drawn = base * np.exp(spread * noise) if base else spread * noise
        out[name] = jnp.asarray(drawn.astype(out[name].dtype))
    for name, factor in factors.items():
        out[name] = (out[name] * factor).astype(out[name].dtype)
    return out
```

```python
from contextlib import ExitStack

import numpy as np

import concourse.bass as bass
from concourse import mybir

ALU = mybir.AluOpType
ACT = mybir.ActivationFunctionType
AX = mybir.AxisListType
F32 = mybir.dt.float32
BF16 = mybir.dt.bfloat16
U32 = mybir.dt.uint32

P = 128
B, T, C = 8, 128, 256
KC = C // P
PAIRS = B // 2
LN_EPS = 1e-5
RMS_EPS = 1e-6
QMAX = 127.0
TINY = 1e-5
ROUND = 12582912.0

H0, D0 = 16, 16
HS, DS = 16, 8
NE, FE = 8, 176
FSH = 352
NF = NE * FE + FSH
NFT = -(-NF // P)
H1, D1 = 16, 128
H2, D2 = 32, 8
DFF = 1024
NFF = DFF // P
TOPK = 16
PAD = 32

CONSTS = {"ident": 128, "ones": 128, "before": 128, "iota": 128, "causal": 128, "cos": 128,
          "sin": 128, "minus_half": 64, "rms_eps": 64, "ln_eps": 1,
          "euler": 8, "first_slot": 8}
CONST_AT = {}
_at = 0
for _name, _width in CONSTS.items():
    CONST_AT[_name] = (_at, _at + _width)
    _at += _width
NCONST = _at


def build(nc, a):
    ctx = ExitStack()
    with ctx:
        def sb(name, shape, dt=F32):
            return ctx.enter_context(nc.sbuf_tensor(name, shape, dt))

        def sem(name):
            return ctx.enter_context(nc.semaphore(name))

        def rows(name, n):
            return a[name].rearrange("(o n) -> o n", o=1).broadcast_to([P, n])

        PS = ctx.enter_context(nc.psum_tensor("PS", [P, 8, 512], F32))

        def bank(p, k):
            return PS[:, 4 * p + k, :]

        X = sb("X", [P, B, C])
        const = sb("const", [P, NCONST])
        ident_bf = sb("ident_bf", [P, P], BF16)
        causal_bf = sb("causal_bf", [P, P], BF16)
        w0 = sb("w0", [P, KC * 4 * C])
        qkv_w = w0[:, 0:KC * 3 * C].rearrange("p (k n) -> p k n", k=KC)
        proj_w = w0[:, KC * 3 * C:].rearrange("p (k n) -> p k n", k=KC)
        w2 = w0[:, :].rearrange("p (k n) -> p k n", k=NFF)
        signs = sb("signs", [P, KC * 2 * C])
        qkv_sign = signs[:, 0:KC * 3 * C // 2].bitcast(BF16).rearrange("p (k n) -> p k n", k=KC)
        proj_sign = signs[:, KC * 3 * C // 2:].bitcast(BF16).rearrange("p (k n) -> p k n", k=KC)
        ETX = signs[:, :].rearrange("p (a n) -> p a n", a=2)
        CT = sb("CT", [P, 2, KC, P])
        proj_b = CT[:, 0, :, :].rearrange("p k t -> p (k t)")
        norm_w = CT[:, 1, :, :].rearrange("p k t -> p (k t)")
        router_w = sb("router_w", [P, KC, NE])
        gu_w = sb("gu_w", [P, KC, 2 * NF])
        down = sb("down", [P, NFT * C])
        down_w = down[:, :].rearrange("p (k n) -> p k n", k=NFT)
        ctxT = down[:, 0:B * C].rearrange("p (b k t) -> p b k t", b=B, k=KC)
        qkv_b = down[:, B * C:B * C + 3 * C]
        big = sb("big", [P, 2 * B * HS * DS * DS])
        Y = big[:, :].rearrange("p (l b n) -> p l b n", l=2, b=B)
        off = [0]

        def late(n):
            off[0] += n
            return big[:, off[0] - n:off[0]]

        wq = late(KC * H1 * D1).rearrange("p (k n) -> p k n", k=KC)
        wkv = late(KC * 2 * D1).rearrange("p (k n) -> p k n", k=KC)
        wo = late(H1 * C).rearrange("p (k n) -> p k n", k=H1)
        bq = late(H1 * D1)
        bkv = late(2 * D1)
        bo = late(C)
        xwq = late(KC * C).rearrange("p (k n) -> p k n", k=KC)
        xwkv = late(KC * 2 * C).rearrange("p (k n) -> p k n", k=KC)
        wr = late(C)
        br = late(1)
        b1 = late(NFF)
        w1 = late(KC * DFF).rearrange("p (k n) -> p k n", k=KC)
        b2 = late(C)
        assert off[0] <= 16384

        Xc = sb("Xc", [P, 2, C])
        R = sb("R", [P, 2, C])
        XT = sb("XT", [P, 2, KC, P])
        WK = [sb(f"WK{i}", [P, 2, 2048]) for i in range(4)]
        xq = sb("xq", [P, 2, C], BF16)
        xqT = sb("xqT", [P, 2, KC, P], BF16)
        st = sb("st", [P, 2, 6])
        mv = sb("mv", [P, 2, 2])
        ve = sb("ve", [P, 2, 1])
        rstd = sb("rstd", [P, 2, 1])
        sm = sb("sm", [P, 2, 16])
        mx = sb("mx", [P, 2, 16])
        nmx = sb("nmx", [P, 2, 16])
        rec = sb("rec", [P, 2, 64])
        msq = sb("msq", [P, 2, 64])
        rms = sb("rms", [P, 2, 64])
        wsc = sb("wsc", [P, 4])
        d_skip = sb("d_skip", [P, HS])
        toep = X[:, 0:2, :]
        lg = sb("lg", [P, 2, NE])
        top = sb("top", [P, 2, 8])
        topi = sb("topi", [P, 2, 8], U32)
        topf = sb("topf", [P, 2, 8])
        dl = sb("dl", [P, 2, NE])
        ex = sb("ex", [P, 2, NE])
        chosen = sb("chosen", [P, 2, NE])
        cw = sb("cw", [P, 2, NE])

        def cst(name, n=None):
            lo, hi = CONST_AT[name]
            return const[:, lo:hi if n is None else lo + n]

        ident = cst("ident")
        ones = cst("ones")

        const_in = sem("const_in")
        w0_in, w1_in, w2_in, w3_in, w4_in, w5_in = (sem(f"w{i}_in") for i in range(6))
        bf_made = sem("bf_made")
        pads_clear = sem("pads_clear")
        w_abs, w_abs_sum, w_scaled, w_signed = (sem(n) for n in ("w_abs", "w_abs_sum", "w_scaled", "w_signed"))
        x_in = [sem(f"x_in{p}") for p in range(2)]
        x_free = [sem(f"x_free{p}") for p in range(2)]
        stats = sem("stats")
        normed = sem("normed")
        ctx_in = [sem(f"ctx_in{p}") for p in range(2)]
        toep_in = [sem(f"toep_in{p}") for p in range(2)]
        conv_w, conv_k0, conv_k1, conv_mm, conv_out = (sem(n) for n in ("conv_w", "conv_k0", "conv_k1", "conv_mm", "conv_out"))
        names = {
            "A": "xq xqT xqT_sb qkv deq qk_hi sub exp pv_hi ss rms xq2 xq2T xq2T_sb y",
            "B": "xT g o",
            "C": "xT xT_sb lg dl ex cw gu silu act aT aT_sb y",
            "D": "xT xT_sb kv kvb q qb rot half qkT qkT_sb s max exp rsum pn pT pT_sa pT_sv o o_sa o_sv y",
            "E": "xT xT_sb qkv sq ms rms pad qkT qkT_sb s exp o",
            "F": "rest logit diag row rank keep ew esum w pick gath gath_sb up gelu down ol pickT pickT_sb back resid stats rstd out",
        }
        S = {f"{stage}_{n}": sem(f"{stage}_{n}") for stage, text in names.items() for n in text.split()}

        def nth(j, p, per=1, k=1, before=0):
            return j * (2 * per) + (p * per + k + before)

        w = WK[0][:, :, :].rearrange("p a b -> p (a b)")
        F = {"diag": w[:, 0:1024].rearrange("p (b n) -> p b n", b=B),
             "tmp": w[:, 1024:2048].rearrange("p (b n) -> p b n", b=B),
             "pick": w[:, 2048:3072].rearrange("p (b n) -> p b n", b=B),
             "pickT": w[:, 3072:4096].rearrange("p (b n) -> p b n", b=B)}
        w = WK[1][:, :, :].rearrange("p a b -> p (a b)")
        F["R"] = w[:, 0:2048].rearrange("p (b n) -> p b n", b=B)
        F["gath"] = w[:, 2048:2304].rearrange("p (k n) -> p k n", k=KC)
        F["hid"] = w[:, 2304:3328].rearrange("p (k n) -> p k n", k=NFF)
        F["ol"] = w[:, 3328:3584]
        F["junk"] = w[:, 3584:3840]
        w = WK[2][:, 0, :]
        for i, n in enumerate(("logit", "max", "above", "tied", "rank", "keep", "e", "esum", "w", "ve", "rstd", "slot", "far")):
            F[n] = w[:, 8 * i:8 * i + 8]
        F["st"] = w[:, 128:176].rearrange("p (b n) -> p b n", b=B)
        F["mv"] = w[:, 192:208].rearrange("p (b n) -> p b n", b=B)

        def conv_products(eng, j, p, l):
            h = ctxT[:, :, l, :].rearrange("p b (h i) -> p b h i", i=DS)[:, :, j * 2 + p, :]
            out = WK[l][:, p, 0:512].rearrange("p (b i k) -> p b i k", b=B, i=DS)
            return eng.tensor_tensor(out, h.unsqueeze(3).broadcast_to([P, B, DS, DS]),
                                     h.unsqueeze(2).broadcast_to([P, B, DS, DS]), ALU.mult)

        def qk_products(eng, p, half):
            qkv = WK[0][:, p, 0:3 * C].rearrange("p (n h d) -> p n h d", n=3, h=H0)
            hs = slice(half * H0 // 2, (half + 1) * H0 // 2)
            return eng.tensor_tensor(WK[1 + half][:, p, :].rearrange("p (h g d) -> p h g d", h=H0 // 2, g=H0),
                                     qkv[:, 0, hs, :].unsqueeze(2).broadcast_to([P, H0 // 2, H0, D0]),
                                     qkv[:, 1, :, :].unsqueeze(1).broadcast_to([P, H0 // 2, H0, D0]), ALU.mult)

        def pv_products(eng, p, half):
            e = probs(p).rearrange("p (h g) -> p h g", h=H0)
            v = WK[0][:, p, 2 * C:3 * C].rearrange("p (g d) -> p d g", g=H0)
            hs = slice(half * H0 // 2, (half + 1) * H0 // 2)
            return eng.tensor_tensor(WK[1 + half][:, p, :].rearrange("p (h d g) -> p h d g", h=H0 // 2, d=D0),
                                     e[:, hs, :].unsqueeze(2).broadcast_to([P, H0 // 2, D0, H0]),
                                     v.unsqueeze(1).broadcast_to([P, H0 // 2, D0, H0]), ALU.mult)

        def probs(p):
            return WK[3][:, p, 0:H0 * H0]

        def PT3(p, i):
            return WK[2][:, p, i * 512:(i + 1) * 512]

        def ET(p, i):
            return WK[3][:, p, 512 + i * 512:1024 + i * 512] if i < 3 else ETX[:, p, :]

        block = ctx.enter_context(nc.Block())

        @block.sync
        def _(sp):
            sp.dma_start(const[:, :], a["const"]).then_inc(const_in, 16)
            sp.dma_start(ctxT, a["ctxT"]).then_inc(const_in, 16)
            sp.dma_start(d_skip[:, :], rows("d_skip", HS)).then_inc(const_in, 16)
            for dst, src in ((qkv_w, a["qkv_w"]), (proj_w, a["proj_w"]),
                             (qkv_b, rows("qkv_b", 3 * C)), (proj_b, rows("proj_b", C)),
                             (norm_w, rows("norm_w", C))):
                sp.dma_start(dst, src).then_inc(w0_in, 16)
            for p in range(2):
                sp.sem_inc(x_free[p], 1)
            with sp.Fori(0, HS // 2) as j:
                for p in range(2):
                    sp.wait_ge(conv_mm, nth(j, p))
                    sp.dma_start(toep[:, p, :], a["toep"][j * 2 + p, :, :]).then_inc(toep_in[p], 16)
            sp.wait_ge(conv_k0, HS)
            sp.wait_ge(conv_k1, HS)
            sp.wait_ge(w_signed, 1)
            for dst, src in ((router_w[:, :, :], a["router_w"]), (gu_w[:, :, :], a["gu_w"]),
                             (w2, a["w2"])):
                sp.dma_start(dst, src).then_inc(w2_in, 16)
            for s in range(5):
                if s == 1:
                    sp.wait_ge(S["A_deq"], B)
                    sp.dma_start(down_w, a["down_w"]).then_inc(w2_in, 16)
                if s == 2:
                    sp.wait_ge(S["B_g"], B)
                    for dst, src in ((wq, a["wq"]), (wkv, a["wkv"]), (wo, a["wo"]), (bq, rows("bq", H1 * D1)),
                                     (bkv, rows("bkv", 2 * D1)), (bo, rows("bo", C))):
                        sp.dma_start(dst, src).then_inc(w3_in, 16)
                    for dst, src in ((xwq, a["xwq"]), (xwkv, a["xwkv"])):
                        sp.dma_start(dst, src).then_inc(w4_in, 16)
                    for dst, src in ((wr, rows("wr", C)), (br, rows("br", 1)), (b1, a["b1"]),
                                     (w1, a["w1"]), (b2, rows("b2", C))):
                        sp.dma_start(dst, src).then_inc(w5_in, 16)
                with sp.Fori(PAIRS * s + 1, PAIRS * (s + 1) + 1) as n:
                    for p in range(2):
                        b = n * 2 + (p - 2 * PAIRS * s - 2)
                        if s:
                            sp.wait_ge(normed, n * 2 + (p - 2 * PAIRS * s - 2 + 1 + B * (s - 1) + 2))
                            src = X[:, b, :]
                        else:
                            src = a["x"][b, :, :]
                        sp.wait_ge(x_free[p], n)
                        sp.dma_start(Xc[:, p, :], src).then_inc(x_in[p], 16)
                        if s == 4:
                            sp.wait_ge(S["E_qkv"], n * 2 + (p - 2 * PAIRS * s - 2 + 1))
                            sp.dma_start(CT[:, p, :, :], a["ctxT"][:, b, :, :]).then_inc(ctx_in[p], 16)
            for b in range(B):
                sp.wait_ge(S["F_out"], b + 1)
                sp.dma_start(a["out"][b, :, :], X[:, b, :]).then_inc(S["F_rest"], 16)
            sp.wait_ge(S["F_rest"], 16 * B)

        @block.gpsimd
        def _(pool):
            pool.sem_inc(normed, 2)

            def norm_tail(j, p, s):
                pool.wait_ge(stats, nth(j, p, before=B * s))
                pool.tensor_tensor(ve[:, p, :], mv[:, p, 1:2], cst("ln_eps"), ALU.add)
                pool.drain()
                pool.tensor_tensor(rstd[:, p, :], ve[:, p, :], cst("minus_half", 1), ALU.pow)
                pool.drain()
                pool.tensor_scalar(R[:, p, :], R[:, p, :], mv[:, p, 0:1], rstd[:, p, :], ALU.subtract, ALU.mult)
                pool.drain()
                pool.tensor_copy(X[:, j * 2 + p, :], R[:, p, :]).then_inc(normed, 1)

            pool.wait_ge(const_in, 48)
            with pool.Fori(0, HS // 2) as j:
                for p in range(2):
                    pool.wait_ge(conv_mm, nth(j, p))
                    conv_products(pool, j, p, 1).then_inc(conv_k1, 1)
            with pool.Fori(0, PAIRS) as j:
                for p in range(2):
                    pool.wait_ge(S["A_deq"], nth(j, p))
                    qk_products(pool, p, 1).then_inc(S["A_qk_hi"], 1)
                for p in range(2):
                    pool.wait_ge(S["A_exp"], nth(j, p))
                    pv_products(pool, p, 1).then_inc(S["A_pv_hi"], 1)
                for p in range(2):
                    pool.wait_ge(S["A_ss"], nth(j, p))
                    pool.tensor_tensor(rms[:, p, 0:1], sm[:, p, 4:5], cst("minus_half", 1), ALU.pow).then_inc(S["A_rms"], 1)
                for p in range(2):
                    norm_tail(j, p, 0)
            with pool.Fori(0, PAIRS) as j:
                for p in range(2):
                    norm_tail(j, p, 1)
            with pool.Fori(0, PAIRS) as j:
                for p in range(2):
                    pool.wait_ge(S["C_dl"], nth(j, p))
                    pool.tensor_tensor(ex[:, p, :], cst("euler"), dl[:, p, :], ALU.pow).then_inc(S["C_ex"], 1)
                for p in range(2):
                    norm_tail(j, p, 2)
            with pool.Fori(0, PAIRS) as j:
                for p in range(2):
                    pool.wait_ge(S["D_qb"], nth(j, p))
                    q = WK[0][:, p, :].rearrange("p (h t d) -> p h t d", h=H1, t=2)
                    o = WK[1][:, p, :].rearrange("p (h t d) -> p h t d", h=H1, t=2)
                    sin = cst("sin").rearrange("p (t d) -> p t d", t=2)
                    for t in range(2):
                        i = pool.tensor_tensor(o[:, :, t, :], q[:, :, 1 - t, :],
                                               sin[:, t:t + 1, :].broadcast_to([P, H1, D1 // 2]), ALU.mult)
                    i.then_inc(S["D_half"], 1)
                for p in range(2):
                    pool.wait_ge(S["D_rsum"], nth(j, p))
                    e = WK[1][:, p, :].rearrange("p (h k) -> p h k", h=H1)
                    pool.tensor_tensor(e, e, rec[:, p, 0:H1].unsqueeze(2).broadcast_to([P, H1, T]), ALU.mult)\
                        .then_inc(S["D_pn"], 1)
                for p in range(2):
                    norm_tail(j, p, 3)
            with pool.Fori(0, PAIRS) as j:
                for p in range(2):
                    pool.wait_ge(S["E_ms"], nth(j, p))
                    pool.tensor_tensor(msq[:, p, :], msq[:, p, :], cst("rms_eps"), ALU.add)
                    pool.drain()
                    pool.tensor_tensor(rms[:, p, :], msq[:, p, :], cst("minus_half"), ALU.pow).then_inc(S["E_rms"], 1)
                for p in range(2):
                    norm_tail(j, p, 4)
            pool.wait_ge(S["F_stats"], B)
            pool.tensor_scalar(F["ve"], F["mv"][:, :, 1], LN_EPS, None, ALU.add)
            pool.drain()
            pool.tensor_tensor(F["rstd"], F["ve"], cst("minus_half", B), ALU.pow).then_inc(S["F_rstd"], 1)

        @block.vector
        def _(dve):
            def ln_stats(j, p, s):
                dve.drain()
                dve.bn_stats(st[:, p, :], R[:, p, :])
                dve.drain()
                dve.bn_aggr(mv[:, p, :], st[:, p, :]).then_inc(stats, 1)

            def r_free(j, p, s):
                dve.wait_ge(normed, nth(j, p, before=B * s))

            def quantise(j, p, src, scale, wcol):
                dve.tensor_reduce(sm[:, p, scale:scale + 1], src, AX.X, ALU.max, apply_absolute_value=True)
                dve.drain()
                dve.tensor_scalar(sm[:, p, scale:scale + 1], sm[:, p, scale:scale + 1], TINY, None, ALU.max)
                dve.drain()
                dve.reciprocal(sm[:, p, 3:4], sm[:, p, scale:scale + 1])
                dve.tensor_scalar(sm[:, p, scale + 1:scale + 2], sm[:, p, scale:scale + 1], wsc[:, wcol:wcol + 1],
                                  1.0 / QMAX, ALU.mult, ALU.mult)
                dve.drain()
                dve.tensor_scalar(XN_q[:, p, :], src, sm[:, p, 3:4], QMAX, ALU.mult, ALU.mult)
                dve.drain()
                return dve.tensor_scalar(xq[:, p, :], XN_q[:, p, :], ROUND, -ROUND, ALU.add, ALU.add)

            XN_q = WK[3][:, :, 1024:1280]

            dve.wait_ge(const_in, 48)
            dve.tensor_copy(ident_bf[:, :], ident)
            dve.tensor_copy(causal_bf[:, :], cst("causal")).then_inc(bf_made, 1)
            dve.wait_ge(w0_in, 80)
            dve.tensor_reduce(wsc[:, 0:1], qkv_w, AX.XY, ALU.add, apply_absolute_value=True)
            dve.tensor_reduce(wsc[:, 1:2], proj_w, AX.XY, ALU.add, apply_absolute_value=True).then_inc(w_abs, 1)
            dve.wait_ge(w_abs_sum, 1)
            dve.tensor_scalar(wsc[:, 2:3], bank(1, 3)[:, 0:1], 1.0 / (3 * C * C), TINY, ALU.mult, ALU.max)
            dve.tensor_scalar(wsc[:, 3:4], bank(1, 3)[:, 1:2], 1.0 / (C * C), TINY, ALU.mult, ALU.max)
            dve.drain()

            with dve.Fori(0, HS // 2) as j:
                for p in range(2):
                    dve.wait_ge(toep_in[p], j * 16 + 16)
                    dve.scalar_tensor_tensor(toep[:, p, 0:P], ident, d_skip[:, bass.ds(j * 2 + p, 1)],
                                             toep[:, p, 0:P], ALU.mult, ALU.add).then_inc(conv_w, 1)
                    dve.wait_ge(conv_mm, nth(j, p))
                    conv_products(dve, j, p, 0).then_inc(conv_k0, 1)

            dve.wait_ge(conv_mm, 2 + HS)
            with dve.Fori(0, PAIRS) as j:
                for p in range(2):
                    dve.wait_ge(x_in[p], j * 16 + 16)
                    quantise(j, p, Xc[:, p, :], 0, 2).then_inc(S["A_xq"], 1)
                for p in range(2):
                    dve.wait_ge(S["A_qkv"], nth(j, p))
                    dve.scalar_tensor_tensor(WK[0][:, p, 0:2 * C], bank(p, 1), sm[:, p, 1:2], qkv_b[:, 0:2 * C],
                                             ALU.mult, ALU.add)
                    dve.scalar_tensor_tensor(WK[0][:, p, 2 * C:3 * C], bank(p, 2)[:, 0:C], sm[:, p, 1:2],
                                             qkv_b[:, 2 * C:3 * C], ALU.mult, ALU.add).then_inc(S["A_deq"], 1)
                dve.drain()
                for p in range(2):
                    e = probs(p)
                    qk_products(dve, p, 0)
                    dve.drain()
                    for half in range(2):
                        if half:
                            dve.wait_ge(S["A_qk_hi"], nth(j, p))
                        dve.tensor_reduce(e[:, half * 128:half * 128 + 128],
                                          WK[1 + half][:, p, :].rearrange("p (n d) -> p n d", d=D0), AX.X, ALU.add)
                    dve.drain()
                    dve.tensor_reduce(mx[:, p, :], e.rearrange("p (h g) -> p h g", h=H0), AX.X, ALU.max)
                    dve.drain()
                    dve.tensor_tensor(e.rearrange("p (h g) -> p h g", h=H0), e.rearrange("p (h g) -> p h g", h=H0),
                                      mx[:, p, :].unsqueeze(2).broadcast_to([P, H0, H0]), ALU.subtract)\
                        .then_inc(S["A_sub"], 1)
                for p in range(2):
                    att = WK[3][:, p, 512:512 + C]
                    dve.wait_ge(S["A_exp"], nth(j, p))
                    dve.tensor_reduce(nmx[:, p, :], probs(p).rearrange("p (h g) -> p h g", h=H0), AX.X, ALU.add)
                    pv_products(dve, p, 0)
                    dve.drain()
                    dve.reciprocal(rec[:, p, 0:H0], nmx[:, p, :])
                    for half in range(2):
                        if half:
                            dve.wait_ge(S["A_pv_hi"], nth(j, p))
                        dve.tensor_reduce(att[:, half * 128:half * 128 + 128],
                                          WK[1 + half][:, p, :].rearrange("p (n g) -> p n g", g=H0), AX.X, ALU.add)
                    dve.drain()
                    dve.tensor_tensor(att.rearrange("p (h d) -> p h d", d=D0), att.rearrange("p (h d) -> p h d", d=D0),
                                      rec[:, p, 0:H0].unsqueeze(2).broadcast_to([P, H0, D0]), ALU.mult)
                    dve.drain()
                    dve.tensor_tensor_reduce(XN_q[:, p, :], att, att, 1.0 / C, RMS_EPS, ALU.mult, ALU.add, sm[:, p, 4:5])\
                        .then_inc(S["A_ss"], 1)
                for p in range(2):
                    att = WK[3][:, p, 512:512 + C]
                    dve.wait_ge(S["A_rms"], nth(j, p))
                    dve.scalar_tensor_tensor(att, att, rms[:, p, 0:1], norm_w, ALU.mult, ALU.mult)
                    dve.drain()
                    quantise(j, p, att, 5, 3).then_inc(S["A_xq2"], 1)
                for p in range(2):
                    dve.wait_ge(S["A_y"], nth(j, p))
                    r_free(j, p, 0)
                    dve.scalar_tensor_tensor(R[:, p, :], bank(p, 2)[:, 0:C], sm[:, p, 6:7], proj_b, ALU.mult, ALU.add)
                    dve.drain()
                    dve.tensor_tensor(R[:, p, :], R[:, p, :], Xc[:, p, :], ALU.add).then_inc(x_free[p], 1)
                    ln_stats(j, p, 0)

            dve.wait_ge(conv_out, 2 + HS)
            with dve.Fori(0, PAIRS) as j:
                for p in range(2):
                    dve.wait_ge(S["B_xT"], nth(j, p))
                    for l in range(2):
                        dve.tensor_tensor(WK[0][:, p, l * 1024:(l + 1) * 1024].rearrange("p (n j) -> p n j", j=DS),
                                          Y[:, l, j * 2 + p, :].rearrange("p (n j) -> p n j", j=DS),
                                          bank(p, 0)[:, l * P:(l + 1) * P].unsqueeze(2).broadcast_to([P, P, DS]), ALU.mult)
                    dve.drain()
                    dve.tensor_reduce(WK[1][:, p, 0:2 * P].rearrange("p (n j) -> p n j", j=DS),
                                      WK[0][:, p, :].rearrange("p (n i j) -> p n j i", i=DS, j=DS),
                                      AX.X, ALU.add).then_inc(S["B_g"], 1)
                for p in range(2):
                    dve.wait_ge(S["B_o"], nth(j, p))
                    r_free(j, p, 1)
                    dve.tensor_tensor(R[:, p, :], bank(p, 1)[:, 0:C], Xc[:, p, :], ALU.add).then_inc(x_free[p], 1)
                    ln_stats(j, p, 1)

            NU = NE + 1
            with dve.Fori(0, PAIRS) as j:
                for p in range(2):
                    dve.wait_ge(S["C_lg"], nth(j, p))
                    dve.tensor_copy(lg[:, p, :], bank(p, 1)[:, 0:NE])
                    dve.drain()
                    dve.max(top[:, p, :], lg[:, p, :])
                    dve.drain()
                    dve.tensor_scalar(dl[:, p, :], lg[:, p, :], top[:, p, 0:1], None, ALU.subtract).then_inc(S["C_dl"], 1)
                    dve.max_index(topi[:, p, :], top[:, p, :], lg[:, p, :])
                    dve.drain()
                    dve.tensor_copy(topf[:, p, :], topi[:, p, :])
                    dve.drain()
                    dve.tensor_scalar(chosen[:, p, :], cst("iota", NE), topf[:, p, 0:1], None, ALU.is_equal)
                    dve.drain()
                    dve.scalar_tensor_tensor(chosen[:, p, :], cst("iota", NE), topf[:, p, 1:2], chosen[:, p, :],
                                             ALU.is_equal, ALU.add)
                for p in range(2):
                    dve.wait_ge(S["C_ex"], nth(j, p))
                    dve.reduce_sum(sm[:, p, 0:1], ex[:, p, :], axis=AX.X)
                    dve.drain()
                    dve.reciprocal(sm[:, p, 1:2], sm[:, p, 0:1])
                    dve.drain()
                    dve.scalar_tensor_tensor(cw[:, p, :], ex[:, p, :], sm[:, p, 1:2], chosen[:, p, :], ALU.mult, ALU.mult)
                dve.drain()
                for p in range(2):
                    for e in range(NU):
                        dve.wait_ge(S["C_silu"], nth(j, p, NU, e + 1))
                        if e < NE:
                            i = dve.scalar_tensor_tensor(WK[1][:, p, e * FE:(e + 1) * FE], WK[0][:, p, e * FE:(e + 1) * FE],
                                                         cw[:, p, e:e + 1], bank(p, e % 4)[:, FE:2 * FE], ALU.mult, ALU.mult)
                        else:
                            i = dve.tensor_tensor(WK[1][:, p, NE * FE:NF], WK[0][:, p, NE * FE:NF],
                                                  bank(p, 1)[:, 0:FSH], ALU.mult)
                        i.then_inc(S["C_act"], 1)
                for p in range(2):
                    dve.wait_ge(S["C_y"], nth(j, p))
                    r_free(j, p, 2)
                    dve.tensor_tensor(R[:, p, :], bank(p, 0)[:, 0:C], Xc[:, p, :], ALU.add).then_inc(x_free[p], 1)
                    ln_stats(j, p, 2)

            dve.wait_ge(w3_in, 96)
            with dve.Fori(0, PAIRS) as j:
                for p in range(2):
                    q = WK[0][:, p, :]
                    k = WK[3][:, p, 0:2 * D1]
                    kt = WK[3][:, p, 2 * D1:3 * D1]
                    sin = cst("sin")
                    cos = cst("cos")
                    dve.wait_ge(S["D_kv"], nth(j, p))
                    dve.tensor_tensor(k, bank(p, 0)[:, 0:2 * D1], bkv, ALU.add).then_inc(S["D_kvb"], 1)
                    dve.drain()
                    for t in range(2):
                        dve.tensor_tensor(kt[:, t * 64:t * 64 + 64], k[:, 64 - t * 64:128 - t * 64], sin[:, t * 64:t * 64 + 64], ALU.mult)
                    dve.drain()
                    dve.tensor_tensor(k[:, 0:D1], k[:, 0:D1], cos, ALU.mult)
                    dve.drain()
                    dve.tensor_tensor(k[:, 0:D1], k[:, 0:D1], kt, ALU.add)
                    for i in range(4):
                        dve.wait_ge(S["D_q"], nth(j, p, 4, i + 1))
                        last = dve.tensor_tensor(q[:, i * 512:(i + 1) * 512], bank(p, (i + 1) % 4), bq[:, i * 512:(i + 1) * 512], ALU.add)
                    last.then_inc(S["D_qb"], 1)
                for p in range(2):
                    q = WK[0][:, p, :]
                    dve.wait_ge(S["D_half"], nth(j, p))
                    dve.tensor_tensor(q.rearrange("p (h d) -> p h d", d=D1), q.rearrange("p (h d) -> p h d", d=D1),
                                      cst("cos").unsqueeze(1).broadcast_to([P, H1, D1]), ALU.mult)
                    dve.drain()
                    dve.tensor_tensor(q, q, WK[1][:, p, :], ALU.add).then_inc(S["D_rot"], 1)
                for p in range(2):
                    dve.wait_ge(S["D_s"], nth(j, p))
                    dve.tensor_reduce(mx[:, p, :], PS[:, 4 * p:4 * p + 4, :].rearrange("p k (g t) -> p (k g) t", g=4), AX.X, ALU.max)
                    dve.drain()
                    dve.tensor_scalar(nmx[:, p, :], mx[:, p, :], -(D1 ** -0.5), None, ALU.mult).then_inc(S["D_max"], 1)
                for p in range(2):
                    dve.wait_ge(S["D_exp"], nth(j, p))
                    dve.reciprocal(rec[:, p, 0:H1], msq[:, p, 0:H1]).then_inc(S["D_rsum"], 1)
                for p in range(2):
                    for i in range(2, 4):
                        dve.wait_ge(S["D_pT"], nth(j, p, 4, i + 1))
                        last = dve.tensor_copy(PT3(p, i), bank(p, i))
                    last.then_inc(S["D_pT_sv"], 1)
                for p in range(2):
                    for i in range(2, 4):
                        dve.wait_ge(S["D_o"], nth(j, p, 4, i + 1))
                        last = dve.tensor_copy(WK[0][:, p, i * 512:(i + 1) * 512], bank(p, i))
                    last.then_inc(S["D_o_sv"], 1)
                for p in range(2):
                    r_free(j, p, 3)
                    dve.tensor_tensor(R[:, p, :], Xc[:, p, :], bo, ALU.add)
                    dve.drain()
                    dve.wait_ge(S["D_y"], nth(j, p))
                    dve.tensor_tensor(R[:, p, :], bank(p, 0)[:, 0:C], R[:, p, :], ALU.add).then_inc(x_free[p], 1)
                    ln_stats(j, p, 3)

            dve.memset(WK[0][:, :, :], 0.0)
            dve.memset(WK[3][:, :, 0:512], 1.0).then_inc(pads_clear, 1)
            with dve.Fori(0, PAIRS) as j:
                for p in range(2):
                    dve.wait_ge(S["E_sq"], nth(j, p))
                    dve.tensor_reduce(msq[:, p, :], WK[2][:, p, 0:512].rearrange("p (h d) -> p h d", d=D2), AX.X, ALU.add)\
                        .then_inc(S["E_ms"], 1)
                for p in range(2):
                    dve.wait_ge(S["E_rms"], nth(j, p))
                    dve.tensor_tensor(WK[0][:, p, :].rearrange("p (h d) -> p h d", d=PAD)[:, :, 0:D2],
                                      bank(p, 1).rearrange("p (h d) -> p h d", d=D2),
                                      rms[:, p, :].unsqueeze(2).broadcast_to([P, 2 * H2, D2]), ALU.mult)\
                        .then_inc(S["E_pad"], 1)
                for p in range(2):
                    dve.wait_ge(S["E_o"], nth(j, p))
                    r_free(j, p, 4)
                    o = bank(p, 0)[:, 0:H2 * (D2 + 1)].rearrange("p (h d) -> p h d", d=D2 + 1)
                    dve.reciprocal(rec[:, p, 0:H2], o[:, :, D2])
                    dve.drain()
                    dve.tensor_tensor(R[:, p, :].rearrange("p (h d) -> p h d", d=D2), o[:, :, 0:D2],
                                      rec[:, p, 0:H2].unsqueeze(2).broadcast_to([P, H2, D2]), ALU.mult)
                    dve.drain()
                    dve.tensor_tensor(R[:, p, :], R[:, p, :], Xc[:, p, :], ALU.add).then_inc(x_free[p], 1)
                    ln_stats(j, p, 4)

            dve.wait_ge(w5_in, 80)
            for b in range(B):
                dve.wait_ge(normed, 2 + 4 * B + b + 1)
                dve.tensor_tensor_reduce(F["junk"], X[:, b, :], wr, 1.0, 0.0, ALU.mult, ALU.add, F["logit"][:, b:b + 1])
                dve.drain()
            dve.tensor_scalar(F["logit"], F["logit"], br, None, ALU.add)
            dve.drain()
            for b in range(B):
                last = dve.tensor_scalar(F["diag"][:, b, :], ident, F["logit"][:, b:b + 1], None, ALU.mult)
            last.then_inc(S["F_diag"], 1)
            row = PS[:, 0:2, :].rearrange("p k (b t) -> p (k b) t", b=4)
            dve.wait_ge(S["F_row"], 1)
            dve.tensor_reduce(F["max"], row, AX.X, ALU.max)
            for b in range(B):
                dve.tensor_scalar(F["tmp"][:, b, :], row[:, b, :], F["logit"][:, b:b + 1], 0.0, ALU.is_gt, ALU.add,
                                  accum_out=F["above"][:, b:b + 1])
            dve.drain()
            for b in range(B):
                dve.scalar_tensor_tensor(F["tmp"][:, b, :], row[:, b, :], F["logit"][:, b:b + 1], cst("before"),
                                         ALU.is_equal, ALU.mult, accum_out=F["tied"][:, b:b + 1])
            dve.drain()
            dve.tensor_tensor(F["rank"], F["above"], F["tied"], ALU.add)
            dve.tensor_tensor(F["e"], F["logit"], F["max"], ALU.subtract).then_inc(S["F_rank"], 1)
            dve.drain()
            dve.tensor_scalar(F["keep"], F["rank"], float(TOPK), None, ALU.is_lt)
            dve.tensor_scalar(F["far"], F["rank"], float(TOPK), 1000.0, ALU.is_ge, ALU.mult)
            dve.tensor_tensor(F["slot"], F["rank"], cst("first_slot"), ALU.add)
            dve.drain()
            dve.tensor_tensor(F["slot"], F["slot"], F["far"], ALU.add)
            dve.drain()
            for b in range(B):
                last = dve.tensor_scalar(F["pick"][:, b, :], cst("iota"), F["slot"][:, b:b + 1], None, ALU.is_equal)
            last.then_inc(S["F_pick"], 1)
            dve.wait_ge(S["F_ew"], 1)
            dve.tensor_tensor(F["e"], F["e"], F["keep"], ALU.mult).then_inc(S["F_keep"], 1)
            dve.wait_ge(S["F_esum"], 1)
            dve.reciprocal(F["esum"], PS[:, 7, 0:B])
            dve.drain()
            dve.tensor_tensor(F["w"], F["e"], F["esum"], ALU.mult)
            dve.tensor_scalar(F["R"], X[:, :, :], 2.0, None, ALU.mult)
            dve.wait_ge(S["F_pickT"], 1)
            dve.tensor_copy(F["pickT"].rearrange("p b n -> p (b n)"), PS[:, 4:6, :].rearrange("p k n -> p (k n)"))\
                .then_inc(S["F_pickT_sb"], 1)
            dve.wait_ge(S["F_down"], 1)
            dve.tensor_tensor(F["ol"], PS[:, 6, 0:C], b2, ALU.add).then_inc(S["F_ol"], 1)
            for b in range(B):
                dve.wait_ge(S["F_back"], b + 1)
                dve.scalar_tensor_tensor(F["R"][:, b, :], PS[:, b % 4, 0:C], F["w"][:, b:b + 1],
                                         F["R"][:, b, :], ALU.mult, ALU.add)
                dve.drain()
                dve.bn_stats(F["st"][:, b, :], F["R"][:, b, :])
                dve.drain()
                dve.bn_aggr(F["mv"][:, b, :], F["st"][:, b, :]).then_inc(S["F_stats"], 1)
            dve.wait_ge(S["F_rstd"], 1)
            for b in range(B):
                dve.tensor_scalar(X[:, b, :], F["R"][:, b, :], F["mv"][:, b, 0:1], F["rstd"][:, b:b + 1],
                                  ALU.subtract, ALU.mult).then_inc(S["F_out"], 1)

        @block.scalar
        def _(act):
            def copy(dst, src):
                return act.activation(dst, src, ACT.Copy)

            act.sem_inc(conv_out, 2)
            with act.Fori(0, HS // 2) as j:
                for p in range(2):
                    act.wait_ge(conv_mm, nth(j, p, before=2))
                    for l in range(2):
                        last = copy(Y[:, l, :, :].rearrange("p b (h n) -> p b h n", h=HS)[:, :, j * 2 + p, :],
                                    bank(p, l).rearrange("p (b n) -> p b n", b=B))
                    last.then_inc(conv_out, 1)
            act.wait_ge(w0_in, 80)
            act.activation(qkv_sign, qkv_w, ACT.Sign)
            act.activation(proj_sign, proj_w, ACT.Sign).then_inc(w_signed, 1)
            with act.Fori(0, PAIRS) as j:
                for p in range(2):
                    act.wait_ge(S["A_xqT"], nth(j, p))
                    copy(xqT[:, p, :, :].rearrange("p k t -> p (k t)"), bank(p, 0)[:, 0:P].bitcast(BF16)).then_inc(S["A_xqT_sb"], 1)
                for p in range(2):
                    act.wait_ge(S["A_sub"], nth(j, p))
                    act.activation(probs(p), probs(p), ACT.Exp, scale=D0 ** -0.5).then_inc(S["A_exp"], 1)
                for p in range(2):
                    act.wait_ge(S["A_xq2T"], nth(j, p))
                    copy(xqT[:, p, :, :].rearrange("p k t -> p (k t)"), bank(p, 1)[:, 0:P].bitcast(BF16)).then_inc(S["A_xq2T_sb"], 1)

            def xt_copy(j, p, stage):
                act.wait_ge(S[f"{stage}_xT"], nth(j, p))
                copy(XT[:, p, :, :].rearrange("p k t -> p (k t)"), bank(p, 0)[:, 0:C]).then_inc(S[f"{stage}_xT_sb"], 1)

            NU = NE + 1
            with act.Fori(0, PAIRS) as j:
                for p in range(2):
                    xt_copy(j, p, "C")
                for p in range(2):
                    for e in range(NU):
                        act.wait_ge(S["C_gu"], nth(j, p, NU, e + 1))
                        n = FE if e < NE else FSH
                        act.activation(WK[0][:, p, e * FE:e * FE + n], bank(p, e % 4)[:, 0:n], ACT.Silu).then_inc(S["C_silu"], 1)
                for p in range(2):
                    for i in range(4):
                        act.wait_ge(S["C_aT"], nth(j, p, 4, i + 1))
                        if i < 3:
                            last = copy(WK[2][:, p, i * 512:(i + 1) * 512], bank(p, i))
                        else:
                            copy(WK[2][:, p, 1536:1664], bank(p, 3)[:, 0:P])
                            last = copy(WK[2][0:NF - 13 * P, p, 1664:1792], bank(p, 3)[0:NF - 13 * P, P:2 * P])
                    last.then_inc(S["C_aT_sb"], 1)
            with act.Fori(0, PAIRS) as j:
                for p in range(2):
                    xt_copy(j, p, "D")
                for p in range(2):
                    act.wait_ge(S["D_qkT"], nth(j, p, 5, 1))
                    copy(WK[3][:, p, 512:512 + P], bank(p, 0)[:, 0:P]).then_inc(S["D_qkT_sb"], 1)
                    for i in range(4):
                        act.wait_ge(S["D_qkT"], nth(j, p, 5, i + 2))
                        copy(WK[2][:, p, i * 512:(i + 1) * 512], bank(p, (i + 1) % 4)).then_inc(S["D_qkT_sb"], 1)
                for p in range(2):
                    act.wait_ge(S["D_max"], nth(j, p))
                    for h in range(H1):
                        last = act.activation(WK[1][:, p, h * T:(h + 1) * T], bank(p, h // 4)[:, (h % 4) * T:(h % 4 + 1) * T],
                                              ACT.Exp, bias=nmx[:, p, h:h + 1], scale=D1 ** -0.5,
                                              accum_out=msq[:, p, h:h + 1])
                    last.then_inc(S["D_exp"], 1)
                for p in range(2):
                    for i in range(2):
                        act.wait_ge(S["D_pT"], nth(j, p, 4, i + 1))
                        last = copy(PT3(p, i), bank(p, i))
                    last.then_inc(S["D_pT_sa"], 1)
                for p in range(2):
                    for i in range(2):
                        act.wait_ge(S["D_o"], nth(j, p, 4, i + 1))
                        last = copy(WK[0][:, p, i * 512:(i + 1) * 512], bank(p, i))
                    last.then_inc(S["D_o_sa"], 1)
            act.wait_ge(pads_clear, 1)
            with act.Fori(0, PAIRS) as j:
                for p in range(2):
                    xt_copy(j, p, "E")
                for p in range(2):
                    act.wait_ge(S["E_qkv"], nth(j, p, before=2))
                    act.activation(WK[2][:, p, 0:512], bank(p, 1), ACT.Square, scale=D2 ** -0.5)
                    copy(WK[3][:, p, 0:H2 * (D2 + 1)].rearrange("p (h d) -> p h d", d=D2 + 1)[:, :, 0:D2],
                         bank(p, 2)[:, 0:C].rearrange("p (h d) -> p h d", d=D2)).then_inc(S["E_sq"], 1)
                for p in range(2):
                    for i in range(4):
                        act.wait_ge(S["E_qkT"], nth(j, p, 4, i + 1))
                        last = copy(ET(p, i), bank(p, i))
                    last.then_inc(S["E_qkT_sb"], 1)
                for p in range(2):
                    for n in range(8):
                        act.wait_ge(S["E_s"], nth(j, p, 8, n + 1))
                        act.activation(WK[1 + n // 4][:, p, (n % 4) * 512:(n % 4 + 1) * 512], bank(p, n % 4), ACT.Exp,
                                       scale=D2 ** -0.5).then_inc(S["E_exp"], 1)
            act.wait_ge(S["F_rank"], 1)
            act.activation(F["e"], F["e"], ACT.Exp).then_inc(S["F_ew"], 1)
            act.wait_ge(S["F_gath"], 1)
            for k in range(KC):
                last = copy(F["gath"][:, k, :], PS[:, 2 + k, 0:P])
            last.then_inc(S["F_gath_sb"], 1)
            act.wait_ge(w5_in, 80)
            for f in range(NFF):
                act.wait_ge(S["F_up"], f + 1)
                act.activation(F["hid"][:, f, :], PS[:, f % 4, 0:P], ACT.Gelu,
                               bias=b1[:, f:f + 1]).then_inc(S["F_gelu"], 1)

        @block.tensor
        def _(pe):
            def turn_x(j, p, s, stage):
                pe.wait_ge(x_in[p], j * 16 + (s * 64 + 16))
                for k in range(KC):
                    last = pe.transpose(bank(p, 0)[:, k * P:(k + 1) * P], Xc[:, p, k * P:(k + 1) * P], ident)
                last.then_inc(S[f"{stage}_xT"], 1)

            pe.sem_inc(conv_mm, 2)
            pe.sem_inc(S["E_qkv"], 2)
            pe.wait_ge(const_in, 48)
            pe.wait_ge(bf_made, 1)
            pe.wait_ge(w_abs, 1)
            pe.matmul(bank(1, 3)[:, 0:2], ones, wsc[:, 0:2], start=True, stop=True).then_inc(w_abs_sum, 1)
            with pe.Fori(0, HS // 2) as j:
                for p in range(2):
                    pe.wait_ge(conv_w, nth(j, p))
                    pe.wait_ge(conv_k0, nth(j, p))
                    pe.wait_ge(conv_k1, nth(j, p))
                    pe.wait_ge(conv_out, nth(j, p))
                    near, far = toep[:, p, 0:P], toep[:, p, P:2 * P]
                    pe.matmul(bank(p, 0), near, WK[0][:, p, 0:512], start=True, stop=True)
                    pe.matmul(bank(p, 1), near, WK[1][:, p, 0:512], start=True, stop=False)
                    pe.matmul(bank(p, 1), far, WK[0][:, p, 0:512], start=False, stop=True).then_inc(conv_mm, 1)
            pe.wait_ge(w_signed, 1)
            pe.wait_ge(conv_out, 2 + HS)
            with pe.Fori(0, PAIRS) as j:
                for p in range(2):
                    pe.wait_ge(S["A_xq"], nth(j, p))
                    for k in range(KC):
                        last = pe.transpose(bank(p, 0)[:, 0:P].bitcast(BF16)[:, k * P:(k + 1) * P], xq[:, p, k * P:(k + 1) * P], ident_bf[:, :])
                    last.then_inc(S["A_xqT"], 1)
                for p in range(2):
                    pe.wait_ge(S["A_xqT_sb"], nth(j, p))
                    for n, (lo, hi) in enumerate(((0, 512), (512, 768))):
                        for k in range(KC):
                            last = pe.matmul(bank(p, 1 + n)[:, 0:hi - lo], xqT[:, p, k, :], qkv_sign[:, k, lo:hi],
                                             start=(k == 0), stop=(k == KC - 1))
                    last.then_inc(S["A_qkv"], 1)
                for p in range(2):
                    pe.wait_ge(S["A_xq2"], nth(j, p))
                    for k in range(KC):
                        last = pe.transpose(bank(p, 1)[:, 0:P].bitcast(BF16)[:, k * P:(k + 1) * P], xq[:, p, k * P:(k + 1) * P], ident_bf[:, :])
                    last.then_inc(S["A_xq2T"], 1)
                for p in range(2):
                    pe.wait_ge(S["A_xq2T_sb"], nth(j, p))
                    for k in range(KC):
                        last = pe.matmul(bank(p, 2)[:, 0:C], xqT[:, p, k, :], proj_sign[:, k, :], start=(k == 0), stop=(k == KC - 1))
                    last.then_inc(S["A_y"], 1)
            with pe.Fori(0, PAIRS) as j:
                for p in range(2):
                    turn_x(j, p, 1, "B")
                for p in range(2):
                    pe.wait_ge(S["B_g"], nth(j, p))
                    for l in range(2):
                        last = pe.transpose(bank(p, 1)[:, l * P:(l + 1) * P], WK[1][:, p, l * P:(l + 1) * P], ident)
                    last.then_inc(S["B_o"], 1)
            NU = NE + 1
            pe.wait_ge(w2_in, 64)
            with pe.Fori(0, PAIRS) as j:
                for p in range(2):
                    turn_x(j, p, 2, "C")
                for p in range(2):
                    pe.wait_ge(S["C_xT_sb"], nth(j, p))
                    for k in range(KC):
                        last = pe.matmul(bank(p, 1)[:, 0:NE], XT[:, p, k, :], router_w[:, k, :], start=(k == 0), stop=(k == KC - 1))
                    last.then_inc(S["C_lg"], 1)
                for p in range(2):
                    pe.wait_ge(S["C_dl"], nth(j, p))
                    for e in range(NE):
                        if e >= 4:
                            pe.wait_ge(S["C_act"], nth(j, p, NU, e - 3))
                        for k in range(KC):
                            last = pe.matmul(bank(p, e % 4)[:, 0:2 * FE], XT[:, p, k, :], gu_w[:, k, e * 2 * FE:(e + 1) * 2 * FE],
                                             start=(k == 0), stop=(k == KC - 1))
                        last.then_inc(S["C_gu"], 1)
                    pe.wait_ge(S["C_act"], nth(j, p, NU, 6))
                    for n in range(2):
                        c = 2 * FE * NE + n * FSH
                        for k in range(KC):
                            last = pe.matmul(bank(p, n)[:, 0:FSH], XT[:, p, k, :], gu_w[:, k, c:c + FSH],
                                             start=(k == 0), stop=(k == KC - 1))
                    last.then_inc(S["C_gu"], 1)
                for p in range(2):
                    pe.wait_ge(S["C_act"], nth(j, p, NU, NU))
                    for i in range(4):
                        for f in range(4 * i, min(4 * i + 4, NFT)):
                            w = min(P, NF - f * P)
                            last = pe.transpose(bank(p, i)[0:w, (f % 4) * P:(f % 4 + 1) * P], WK[1][:, p, f * P:f * P + w], ident)
                        last.then_inc(S["C_aT"], 1)
                for p in range(2):
                    pe.wait_ge(S["C_aT_sb"], nth(j, p))
                    for f in range(NFT):
                        w = min(P, NF - f * P)
                        last = pe.matmul(bank(p, 0)[:, 0:C], WK[2][0:w, p, f * P:(f + 1) * P], down_w[0:w, f, :],
                                         start=(f == 0), stop=(f == NFT - 1))
                    last.then_inc(S["C_y"], 1)
            pe.wait_ge(w3_in, 96)
            with pe.Fori(0, PAIRS) as j:
                for p in range(2):
                    turn_x(j, p, 3, "D")
                for p in range(2):
                    pe.wait_ge(S["D_xT_sb"], nth(j, p))
                    for k in range(KC):
                        last = pe.matmul(bank(p, 0)[:, 0:2 * D1], XT[:, p, k, :], wkv[:, k, :], start=(k == 0), stop=(k == KC - 1))
                    last.then_inc(S["D_kv"], 1)
                    for i in range(4):
                        if i == 3:
                            pe.wait_ge(S["D_kvb"], nth(j, p))
                        for k in range(KC):
                            last = pe.matmul(bank(p, (i + 1) % 4), XT[:, p, k, :], wq[:, k, i * 512:(i + 1) * 512],
                                             start=(k == 0), stop=(k == KC - 1))
                        last.then_inc(S["D_q"], 1)
                for p in range(2):
                    pe.wait_ge(S["D_rot"], nth(j, p))
                    pe.transpose(bank(p, 0)[:, 0:P], WK[3][:, p, 0:D1], ident).then_inc(S["D_qkT"], 1)
                    for i in range(4):
                        if i == 3:
                            pe.wait_ge(S["D_qkT_sb"], nth(j, p, 5, 1))
                        for n in range(4):
                            c = (4 * i + n) * D1
                            last = pe.transpose(bank(p, (i + 1) % 4)[:, n * T:(n + 1) * T], WK[0][:, p, c:c + D1], ident)
                        last.then_inc(S["D_qkT"], 1)
                for p in range(2):
                    pe.wait_ge(S["D_qkT_sb"], nth(j, p, 5, 5))
                    for i in range(4):
                        pe.matmul(bank(p, i), ident_bf[:, :], causal_bf[:, :].unsqueeze(1).broadcast_to([P, 4, P]), start=True, stop=True)
                        for n in range(4):
                            c = (4 * i + n) * T
                            last = pe.matmul(bank(p, i)[:, n * T:(n + 1) * T], WK[2][:, p, c:c + T], WK[3][:, p, 512:512 + P],
                                             start=False, stop=True, skip_group_check=True)
                    last.then_inc(S["D_s"], 1)
                for p in range(2):
                    pe.wait_ge(S["D_pn"], nth(j, p))
                    for i in range(4):
                        for n in range(4):
                            c = (4 * i + n) * T
                            last = pe.transpose(bank(p, i)[:, n * T:(n + 1) * T], WK[1][:, p, c:c + T], ident)
                        last.then_inc(S["D_pT"], 1)
                for p in range(2):
                    pe.wait_ge(S["D_pT_sa"], nth(j, p))
                    pe.wait_ge(S["D_pT_sv"], nth(j, p))
                    for i in range(4):
                        pe.matmul(bank(p, i), WK[3][:, p, D1:2 * D1], PT3(p, i), start=True, stop=True).then_inc(S["D_o"], 1)
                for p in range(2):
                    pe.wait_ge(S["D_o_sa"], nth(j, p))
                    pe.wait_ge(S["D_o_sv"], nth(j, p))
                    for h in range(H1):
                        last = pe.matmul(bank(p, 0)[:, 0:C], WK[0][:, p, h * T:(h + 1) * T], wo[:, h, :], start=(h == 0), stop=(h == H1 - 1))
                    last.then_inc(S["D_y"], 1)
            pe.wait_ge(w4_in, 32)
            with pe.Fori(0, PAIRS) as j:
                for p in range(2):
                    turn_x(j, p, 4, "E")
                for p in range(2):
                    pe.wait_ge(ctx_in[p], j * 16 + 16)
                    for k in range(KC):
                        pe.matmul(bank(p, 1)[:, C:2 * C], CT[:, p, k, :], xwkv[:, k, 0:C], start=(k == 0), stop=(k == KC - 1))
                    for k in range(KC):
                        pe.matmul(bank(p, 2)[:, 0:C], CT[:, p, k, :], xwkv[:, k, C:2 * C], start=(k == 0), stop=(k == KC - 1))
                    pe.wait_ge(S["E_xT_sb"], nth(j, p))
                    for k in range(KC):
                        last = pe.matmul(bank(p, 1)[:, 0:C], XT[:, p, k, :], xwq[:, k, :], start=(k == 0), stop=(k == KC - 1))
                    last.then_inc(S["E_qkv"], 1)
                for p in range(2):
                    pe.wait_ge(S["E_pad"], nth(j, p))
                    for i in range(4):
                        for n in range(4):
                            c = (4 * i + n) * P
                            last = pe.transpose(bank(p, i)[:, n * P:(n + 1) * P], WK[0][:, p, c:c + P], ident)
                        last.then_inc(S["E_qkT"], 1)
                for p in range(2):
                    pe.wait_ge(S["E_qkT_sb"], nth(j, p))
                    for n in range(8):
                        rd, r = n // 4, n % 4
                        if rd:
                            pe.wait_ge(S["E_exp"], nth(j, p, 8, r + 1))
                        at = slice(PAD * r, PAD * r + D2)
                        for g in range(4):
                            last = pe.matmul(bank(p, r)[:, g * P:(g + 1) * P], ET(p, 2 + rd)[at, g * P:(g + 1) * P],
                                             ET(p, rd)[at, g * P:(g + 1) * P], start=True, stop=True)
                        last.then_inc(S["E_s"], 1)
                for p in range(2):
                    pe.wait_ge(S["E_exp"], nth(j, p, 8, 8))
                    for n in range(8):
                        for g in range(4):
                            h = 16 * (n // 4) + 4 * g + n % 4
                            last = pe.matmul(bank(p, 0)[:, h * (D2 + 1):(h + 1) * (D2 + 1)],
                                             WK[1 + n // 4][:, p, ((n % 4) * 4 + g) * P:((n % 4) * 4 + g + 1) * P],
                                             WK[3][:, p, h * (D2 + 1):(h + 1) * (D2 + 1)], start=True, stop=True)
                    last.then_inc(S["E_o"], 1)
            pe.wait_ge(S["F_diag"], 1)
            for b in range(B):
                last = pe.matmul(PS[:, b // 4, (b % 4) * P:(b % 4 + 1) * P], ones, F["diag"][:, b, :], start=True, stop=True)
            last.then_inc(S["F_row"], 1)
            pe.wait_ge(S["F_pick"], 1)
            for k in range(KC):
                for b in range(B):
                    last = pe.matmul(PS[:, 2 + k, 0:P], X[:, b, k * P:(k + 1) * P], F["pick"][:, b, :], start=(b == 0), stop=(b == B - 1))
            last.then_inc(S["F_gath"], 1)
            for b in range(B):
                last = pe.transpose(PS[:, 4 + b // 4, (b % 4) * P:(b % 4 + 1) * P], F["pick"][:, b, :], ident)
            last.then_inc(S["F_pickT"], 1)
            pe.wait_ge(S["F_keep"], 1)
            pe.matmul(PS[:, 7, 0:B], ones, F["e"], start=True, stop=True).then_inc(S["F_esum"], 1)
            pe.wait_ge(S["F_gath_sb"], 1)
            pe.wait_ge(w5_in, 80)
            for f in range(NFF):
                if f >= 4:
                    pe.wait_ge(S["F_gelu"], f - 3)
                for k in range(KC):
                    last = pe.matmul(PS[:, f % 4, 0:P], w1[:, k, f * P:(f + 1) * P], F["gath"][:, k, :],
                                     start=(k == 0), stop=(k == KC - 1))
                last.then_inc(S["F_up"], 1)
            for f in range(NFF):
                pe.wait_ge(S["F_gelu"], f + 1)
                last = pe.matmul(PS[:, 6, 0:C], F["hid"][:, f, :], w2[:, f, :], start=(f == 0), stop=(f == NFF - 1))
            last.then_inc(S["F_down"], 1)
            pe.wait_ge(S["F_pickT_sb"], 1)
            pe.wait_ge(S["F_ol"], 1)
            for b in range(B):
                if b >= 4:
                    pe.wait_ge(S["F_stats"], b - 3)
                pe.matmul(PS[:, b % 4, 0:C], F["pickT"][:, b, :], F["ol"], start=True, stop=True)\
                    .then_inc(S["F_back"], 1)


def constants():
    c = np.zeros((P, NCONST), np.float32)

    def put(name, value):
        c[:, CONST_AT[name][0]:CONST_AT[name][1]] = value

    t = np.arange(P)
    put("ident", np.eye(P))
    put("ones", 1.0)
    put("before", t[None, :] < t[:, None])
    put("iota", t[None, :])
    put("causal", np.where(t[None, :] <= t[:, None], 0.0, -1e30))
    inv_freq = (1.0 / np.float32(10000.0) ** (np.arange(0, D1, 2, dtype=np.float32) / np.float32(D1))).astype(np.float32)
    ang = (t.astype(np.float32)[:, None] * inv_freq[None, :]).astype(np.float32)
    put("cos", np.tile(np.cos(ang), (1, 2)))
    put("sin", np.concatenate([-np.sin(ang), np.sin(ang)], axis=1))
    put("minus_half", -0.5)
    put("rms_eps", RMS_EPS)
    put("ln_eps", LN_EPS)
    put("euler", np.e)
    put("first_slot", TOPK * np.arange(B)[None, :])
    return c


def kernel(**inputs):
    import concourse.bacc as _bacc
    from concourse.bass_utils import run_bass_kernel_spmd as _run

    g = {k: np.asarray(v) for k, v in inputs.items()}

    def tiles(w):
        n = -(-w.shape[0] // P)
        if n * P != w.shape[0]:
            w = np.concatenate([w, np.zeros((n * P - w.shape[0], w.shape[1]), w.dtype)])
        return w.reshape(n, P, -1).transpose(1, 0, 2)

    halves = np.concatenate([np.arange(0, D1, 2), np.arange(1, D1, 2)])
    qcols = (np.arange(H1)[:, None] * D1 + halves[None, :]).ravel()
    xkv = np.concatenate([g["L1_xattn_Wk"], g["L1_xattn_Wv"]])
    taps = g["L0_xattn_ssm_kernel"]
    taps = np.concatenate([np.zeros((HS, P - 1), taps.dtype), taps], axis=1)
    toep = np.lib.stride_tricks.sliding_window_view(taps, C, axis=1)[:, ::-1, :]
    down = g["L0_ffn_down_weights"].transpose(0, 2, 1).reshape(NE * FE, C)
    gu = g["L0_ffn_gate_up_weights"].reshape(NE * 2 * FE, C)
    arrays = {
        "x": g["x"],
        "const": constants(),
        "ctxT": g["ctx_2048"].reshape(B, T, KC, P).transpose(3, 0, 2, 1),
        "d_skip": g["L0_xattn_D"],
        "toep": toep,
        "qkv_w": tiles(g["L0_attn_qkv_w"].T), "qkv_b": g["L0_attn_qkv_b"],
        "proj_w": tiles(g["L0_attn_proj_w"].T), "proj_b": g["L0_attn_proj_b"],
        "norm_w": g["L0_attn_norm_w"],
        "router_w": tiles(g["L0_ffn_gate_weight"].T),
        "gu_w": tiles(np.concatenate([gu, g["L0_ffn_shared_gate_up"]]).T),
        "down_w": tiles(np.concatenate([down, g["L0_ffn_shared_down"].T])),
        "wq": tiles(g["L1_attn_Wq"][:, qcols]), "bq": g["L1_attn_bq"][qcols],
        "wkv": tiles(np.concatenate([g["L1_attn_Wk"][:, halves], g["L1_attn_Wv"]], axis=1)),
        "bkv": np.concatenate([g["L1_attn_bk"][halves], g["L1_attn_bv"]]),
        "wo": tiles(g["L1_attn_Wo"]), "bo": g["L1_attn_bo"],
        "xwq": tiles(g["L1_xattn_Wq"].T),
        "xwkv": tiles(np.concatenate([xkv[0::2], xkv[1::2]]).T),
        "wr": g["L1_ffn_Wr"][:, 0], "br": g["L1_ffn_br"],
        "w1": tiles(g["L1_ffn_W1"]), "b1": g["L1_ffn_b1"].reshape(NFF, P).T,
        "w2": tiles(g["L1_ffn_W2"]), "b2": g["L1_ffn_b2"],
    }
    arrays = {f"in_{k}": np.ascontiguousarray(v) for k, v in arrays.items()}
    nc = _bacc.Bacc("TRN2", target_bir_lowering=False, num_devices=1)
    a = {k[3:]: nc.dram_tensor(k, v.shape, F32, kind="ExternalInput").ap() for k, v in arrays.items()}
    a["out"] = nc.dram_tensor("out_0", (B, T, C), F32, kind="ExternalOutput").ap()
    build(nc, a)
    r = _run(nc, [arrays], core_ids=[0])
    return r.results[0]["out_0"]
```

```python
from contextlib import ExitStack

import numpy as np

import concourse.bass as bass
from concourse import mybir

ALU = mybir.AluOpType
ACT = mybir.ActivationFunctionType
AX = mybir.AxisListType
F32 = mybir.dt.float32
BF16 = mybir.dt.bfloat16
U32 = mybir.dt.uint32
I32 = mybir.dt.int32

P = 128
B, T, C = 8, 128, 256
KC = C // P
PAIRS = B // 2
LN_EPS = 1e-5
RMS_EPS = 1e-6
QMAX = 127.0
TINY = 1e-5
ROUND = 12582912.0

H0, D0 = 16, 16
HS, DS = 16, 8
NE, FE = 8, 176
FSH = 352
NF = NE * FE + FSH
NFT = -(-NF // P)
H1, D1 = 16, 128
H2, D2 = 32, 8
DFF = 1024
NFF = DFF // P
TOPK = 16
PAD = 32

CONSTS = {"ident": 128, "ones": 128, "before": 128, "iota": 128, "causal": 128, "cos": 128,
          "sin": 128, "minus_half": 64, "rms_eps": 64, "ln_eps": 1,
          "euler": 8, "first_slot": 8}
CONST_AT = {}
_at = 0
for _name, _width in CONSTS.items():
    CONST_AT[_name] = (_at, _at + _width)
    _at += _width
NCONST = _at


def build(nc, a):
    ctx = ExitStack()
    with ctx:
        def sb(name, shape, dt=F32):
            return ctx.enter_context(nc.sbuf_tensor(name, shape, dt))

        def sem(name):
            return ctx.enter_context(nc.semaphore(name))

        def rows(name, n):
            return a[name].rearrange("(o n) -> o n", o=1).broadcast_to([P, n])

        PS = ctx.enter_context(nc.psum_tensor("PS", [P, 8, 512], F32))

        def bank(p, k):
            return PS[:, 4 * p + k, :]

        X = sb("X", [P, B, C])
        const = sb("const", [P, NCONST])
        ident_bf = sb("ident_bf", [P, P], BF16)
        causal_bf = sb("causal_bf", [P, P], BF16)
        w0 = sb("w0", [P, KC * 4 * C])
        qkv_w = w0[:, 0:KC * 3 * C].rearrange("p (k n) -> p k n", k=KC)
        proj_w = w0[:, KC * 3 * C:].rearrange("p (k n) -> p k n", k=KC)
        w2 = w0[:, :].rearrange("p (k n) -> p k n", k=NFF)
        signs = sb("signs", [P, KC * 2 * C])
        qkv_sign = signs[:, 0:KC * 3 * C // 2].bitcast(BF16).rearrange("p (k n) -> p k n", k=KC)
        proj_sign = signs[:, KC * 3 * C // 2:].bitcast(BF16).rearrange("p (k n) -> p k n", k=KC)
        CT = sb("CT", [P, 2, KC, P])
        proj_b = CT[:, 0, :, :].rearrange("p k t -> p (k t)")
        norm_w = CT[:, 1, :, :].rearrange("p k t -> p (k t)")
        router_w = sb("router_w", [P, KC, NE])
        gu_w = sb("gu_w", [P, KC, 2 * NF])
        down = sb("down", [P, NFT * C])
        down_w = down[:, :].rearrange("p (k n) -> p k n", k=NFT)
        ctxT = down[:, 0:B * C].rearrange("p (b k t) -> p b k t", b=B, k=KC)
        qkv_b = down[:, B * C:B * C + 3 * C]
        big = sb("big", [P, 2 * B * HS * DS * DS])
        Y = big[:, :].rearrange("p (l b n) -> p l b n", l=2, b=B)
        off = [0]

        def late(n):
            off[0] += n
            return big[:, off[0] - n:off[0]]

        wq = late(KC * H1 * D1).rearrange("p (k n) -> p k n", k=KC)
        wkv = late(KC * 2 * D1).rearrange("p (k n) -> p k n", k=KC)
        wo = late(H1 * C).rearrange("p (k n) -> p k n", k=H1)
        bq = late(H1 * D1)
        bkv = late(2 * D1)
        bo = late(C)
        xwq = late(KC * C).rearrange("p (k n) -> p k n", k=KC)
        xwkv = late(KC * 2 * C).rearrange("p (k n) -> p k n", k=KC)
        wr = late(C)
        br = late(1)
        b1 = late(NFF)
        w1 = late(KC * DFF).rearrange("p (k n) -> p k n", k=KC)
        b2 = late(C)
        assert off[0] <= 16384

        Xc = sb("Xc", [P, 2, C])
        R = sb("R", [P, 2, C])
        XT = sb("XT", [P, 2, KC, P])
        WK = [sb(f"WK{i}", [P, 2, 2048]) for i in range(4)]
        xq = sb("xq", [P, 2, C], BF16)
        xqT = sb("xqT", [P, 2, KC, P], BF16)
        st = sb("st", [P, 2, 6])
        mv = sb("mv", [P, 2, 2])
        ve = sb("ve", [P, 2, 1])
        rstd = sb("rstd", [P, 2, 1])
        sm = sb("sm", [P, 2, 16])
        mx = sb("mx", [P, 2, 16])
        nmx = sb("nmx", [P, 2, 16])
        rec = sb("rec", [P, 2, 64])
        msq = sb("msq", [P, 2, 64])
        rms = sb("rms", [P, 2, 64])
        wsc = sb("wsc", [P, 4])
        d_skip = sb("d_skip", [P, HS])
        lg = sb("lg", [P, 2, NE])
        top = sb("top", [P, 2, 8])
        topi = sb("topi", [P, 2, 8], U32)
        topf = sb("topf", [P, 2, 8])
        dl = sb("dl", [P, 2, NE])
        ex = sb("ex", [P, 2, NE])
        chosen = sb("chosen", [P, 2, NE])
        cw = sb("cw", [P, 2, NE])

        def cst(name, n=None):
            lo, hi = CONST_AT[name]
            return const[:, lo:hi if n is None else lo + n]

        ident = cst("ident")
        ones = cst("ones")

        const_in = sem("const_in")
        w0_in, w1_in, w2_in, w3_in, w4_in, w5_in = (sem(f"w{i}_in") for i in range(6))
        bf_made = sem("bf_made")
        pads_clear = sem("pads_clear")
        w_abs, w_abs_sum, w_scaled, w_signed = (sem(n) for n in ("w_abs", "w_abs_sum", "w_scaled", "w_signed"))
        x_in = [sem(f"x_in{p}") for p in range(2)]
        x_free = [sem(f"x_free{p}") for p in range(2)]
        stats = sem("stats")
        normed = sem("normed")
        ctx_in = [sem(f"ctx_in{p}") for p in range(2)]
        toep_in = [sem(f"toep_in{p}") for p in range(2)]
        conv_w, conv_kv, conv_half, conv_mm, conv_out = (sem(n) for n in ("conv_w", "conv_kv", "conv_half", "conv_mm", "conv_out"))
        names = {
            "A": "xq xqT xqT_sb qkv deq qk_hi sub exp pv_hi ss rms xq2 xq2T xq2T_sb y",
            "B": "xT g o",
            "C": "xT xT_sb lg dl ex cw gu silu act aT aT_sb y",
            "D": "xT xT_sb kv kvb q qb rot half qkT qkT_sb s max exp rsum pn pT pT_sa pT_sv o o_sa o_sv y",
            "E": "xT xT_sb qkv sq pad qkT qkT_sb s exp oT oT_sb o",
            "F": "rest logit diag row rank keep ew esum w pick gath gath_sb up gelu down ol pickT pickT_sb back resid stats rstd out",
        }
        S = {f"{stage}_{n}": sem(f"{stage}_{n}") for stage, text in names.items() for n in text.split()}

        def nth(j, p, per=1, k=1, before=0):
            return j * (2 * per) + (p * per + k + before)

        w = WK[0][:, :, :].rearrange("p a b -> p (a b)")
        F = {"diag": w[:, 0:1024].rearrange("p (b n) -> p b n", b=B),
             "tmp": w[:, 1024:2048].rearrange("p (b n) -> p b n", b=B),
             "pick": w[:, 2048:3072].rearrange("p (b n) -> p b n", b=B),
             "pickT": w[:, 3072:4096].rearrange("p (b n) -> p b n", b=B)}
        w = WK[1][:, :, :].rearrange("p a b -> p (a b)")
        F["R"] = w[:, 0:2048].rearrange("p (b n) -> p b n", b=B)
        F["gath"] = w[:, 2048:2304].rearrange("p (k n) -> p k n", k=KC)
        F["hid"] = w[:, 2304:3328].rearrange("p (k n) -> p k n", k=NFF)
        F["ol"] = w[:, 3328:3584]
        F["junk"] = w[:, 3584:3840]
        w = WK[2][:, 0, :]
        for i, n in enumerate(("logit", "max", "above", "tied", "rank", "keep", "e", "esum", "w", "ve", "rstd", "slot", "far")):
            F[n] = w[:, 8 * i:8 * i + 8]
        F["st"] = w[:, 128:176].rearrange("p (b n) -> p b n", b=B)
        F["mv"] = w[:, 192:208].rearrange("p (b n) -> p b n", b=B)

        HEADS_A_TURN = HS // PAIRS
        toep = WK[3][:, :, 1280:1536]

        def conv_kv_tile(c, l):
            return WK[0][:, c % 2, 1024 + l * 512:1536 + l * 512]

        def head(j, c, before=0):
            return j * HEADS_A_TURN + (c + 1 + before)

        def conv_products(eng, j, c, l):
            h = ctxT[:, :, l, :].rearrange("p b (h i) -> p b h i", i=DS)[:, :, j * HEADS_A_TURN + c, :]
            out = conv_kv_tile(c, l).rearrange("p (b i k) -> p b i k", b=B, i=DS)
            return eng.tensor_tensor(out, h.unsqueeze(3).broadcast_to([P, B, DS, DS]),
                                     h.unsqueeze(2).broadcast_to([P, B, DS, DS]), ALU.mult)

        def qk_products(eng, p, half):
            qkv = WK[0][:, p, 0:3 * C].rearrange("p (n h d) -> p n h d", n=3, h=H0)
            hs = slice(half * H0 // 2, (half + 1) * H0 // 2)
            return eng.tensor_tensor(WK[1 + half][:, p, :].rearrange("p (h g d) -> p h g d", h=H0 // 2, g=H0),
                                     qkv[:, 0, hs, :].unsqueeze(2).broadcast_to([P, H0 // 2, H0, D0]),
                                     qkv[:, 1, :, :].unsqueeze(1).broadcast_to([P, H0 // 2, H0, D0]), ALU.mult)

        def pv_products(eng, p, half):
            e = probs(p).rearrange("p (h g) -> p h g", h=H0)
            v = WK[0][:, p, 2 * C:3 * C].rearrange("p (g d) -> p d g", g=H0)
            hs = slice(half * H0 // 2, (half + 1) * H0 // 2)
            return eng.tensor_tensor(WK[1 + half][:, p, :].rearrange("p (h d g) -> p h d g", h=H0 // 2, d=D0),
                                     e[:, hs, :].unsqueeze(2).broadcast_to([P, H0 // 2, D0, H0]),
                                     v.unsqueeze(1).broadcast_to([P, H0 // 2, D0, H0]), ALU.mult)

        def probs(p):
            return WK[3][:, p, 0:H0 * H0]

        def PT3(p, i):
            return WK[2][:, p, i * 512:(i + 1) * 512]

        late2 = gu_w[:, :, :].rearrange("p k n -> p (k n)")

        def ET(p, i):
            return late2[:, (4 * p + i) * 512:(4 * p + i + 1) * 512]

        def OT(p):
            return late2[:, 4096 + p * 1024:4096 + (p + 1) * 1024]

        def VP(p):
            return WK[3][:, p, 0:H2 * PAD].rearrange("p (h d) -> p h d", d=PAD)

        block = ctx.enter_context(nc.Block())

        @block.sync
        def _(sp):
            sp.dma_start(const[:, :], a["const"]).then_inc(const_in, 16)
            sp.dma_start(ctxT, a["ctxT"]).then_inc(const_in, 16)
            sp.dma_start(d_skip[:, :], rows("d_skip", HS)).then_inc(const_in, 16)
            for dst, src in ((qkv_w, a["qkv_w"]), (proj_w, a["proj_w"]),
                             (qkv_b, rows("qkv_b", 3 * C)), (proj_b, rows("proj_b", C)),
                             (norm_w, rows("norm_w", C))):
                sp.dma_start(dst, src).then_inc(w0_in, 16)
            for p in range(2):
                sp.sem_inc(x_free[p], 1)
            for s in range(5):
                if s == 1:
                    for dst, src in ((router_w[:, :, :], a["router_w"]), (gu_w[:, :, :], a["gu_w"]), (w2, a["w2"])):
                        sp.dma_start(dst, src).then_inc(w2_in, 16)
                    sp.wait_ge(S["A_deq"], B)
                    sp.wait_ge(conv_kv, HS)
                    sp.dma_start(down_w, a["down_w"]).then_inc(w2_in, 16)
                if s == 2:
                    sp.wait_ge(S["B_g"], B)
                    for dst, src in ((wq, a["wq"]), (wkv, a["wkv"]), (wo, a["wo"]), (bq, rows("bq", H1 * D1)),
                                     (bkv, rows("bkv", 2 * D1)), (bo, rows("bo", C))):
                        sp.dma_start(dst, src).then_inc(w3_in, 16)
                    for dst, src in ((xwq, a["xwq"]), (xwkv, a["xwkv"])):
                        sp.dma_start(dst, src).then_inc(w4_in, 16)
                    for dst, src in ((wr, rows("wr", C)), (br, rows("br", 1)), (b1, a["b1"]),
                                     (w1, a["w1"]), (b2, rows("b2", C))):
                        sp.dma_start(dst, src).then_inc(w5_in, 16)
                with sp.Fori(PAIRS * s + 1, PAIRS * (s + 1) + 1) as n:
                    for p in range(2):
                        b = n * 2 + (p - 2 * PAIRS * s - 2)
                        if s:
                            sp.wait_ge(normed, n * 2 + (p - 2 * PAIRS * s - 2 + 1 + B * (s - 1) + 2))
                            src = X[:, b, :]
                        else:
                            src = a["x"][b, :, :]
                        sp.wait_ge(x_free[p], n)
                        sp.dma_start(Xc[:, p, :], src).then_inc(x_in[p], 16)
                        if s == 0 and p == 1:
                            for c in range(HEADS_A_TURN):
                                h = n * HEADS_A_TURN + (c - HEADS_A_TURN)
                                sp.wait_ge(conv_mm, n * HEADS_A_TURN + (c + 1 - HEADS_A_TURN))
                                sp.dma_start(toep[:, c % 2, :], a["toep"][h, :, :]).then_inc(toep_in[c % 2], 16)
                        if s == 4:
                            sp.wait_ge(S["E_qkv"], n * 2 + (p - 2 * PAIRS * s - 2 + 1))
                            sp.dma_start(CT[:, p, :, :], a["ctxT"][:, b, :, :]).then_inc(ctx_in[p], 16)
            for b in range(B):
                sp.wait_ge(S["F_out"], b + 1)
                sp.dma_start(a["out"][b, :, :], X[:, b, :]).then_inc(S["F_rest"], 16)
            sp.wait_ge(S["F_rest"], 16 * B)

        @block.gpsimd
        def _(pool):
            pool.sem_inc(normed, 2)

            def norm_tail(j, p, s):
                pool.wait_ge(stats, nth(j, p, before=B * s))
                pool.tensor_tensor(ve[:, p, :], mv[:, p, 1:2], cst("ln_eps"), ALU.add)
                pool.drain()
                pool.tensor_tensor(rstd[:, p, :], ve[:, p, :], cst("minus_half", 1), ALU.pow)
                pool.drain()
                pool.tensor_scalar(R[:, p, :], R[:, p, :], mv[:, p, 0:1], rstd[:, p, :], ALU.subtract, ALU.mult)
                pool.drain()
                pool.tensor_copy(X[:, j * 2 + p, :], R[:, p, :]).then_inc(normed, 1)

            pool.wait_ge(const_in, 48)
            def conv_heads(j, cs):
                for c in cs:
                    pool.wait_ge(conv_mm, head(j, c))
                    conv_products(pool, j, c, 0)
                    conv_products(pool, j, c, 1).then_inc(conv_kv, 1)

            with pool.Fori(0, PAIRS) as j:
                conv_heads(j, (0, 1))
                for p in range(2):
                    pool.wait_ge(S["A_deq"], nth(j, p))
                    qk_products(pool, p, 1).then_inc(S["A_qk_hi"], 1)
                conv_heads(j, (2, 3))
                for p in range(2):
                    pool.wait_ge(S["A_exp"], nth(j, p))
                    pv_products(pool, p, 1).then_inc(S["A_pv_hi"], 1)
                for p in range(2):
                    pool.wait_ge(S["A_ss"], nth(j, p))
                    pool.tensor_tensor(rms[:, p, 0:1], sm[:, p, 4:5], cst("minus_half", 1), ALU.pow).then_inc(S["A_rms"], 1)
                for p in range(2):
                    norm_tail(j, p, 0)
            with pool.Fori(0, PAIRS) as j:
                for p in range(2):
                    norm_tail(j, p, 1)
            with pool.Fori(0, PAIRS) as j:
                for p in range(2):
                    pool.wait_ge(S["C_dl"], nth(j, p))
                    pool.tensor_tensor(ex[:, p, :], cst("euler"), dl[:, p, :], ALU.pow).then_inc(S["C_ex"], 1)
                for p in range(2):
                    norm_tail(j, p, 2)
            with pool.Fori(0, PAIRS) as j:
                for p in range(2):
                    q = WK[0][:, p, :].rearrange("p (h t d) -> p h t d", h=H1, t=2)
                    o = WK[1][:, p, :].rearrange("p (h t d) -> p h t d", h=H1, t=2)
                    sin = cst("sin").rearrange("p (t d) -> p t d", t=2)
                    for i in range(4):
                        pool.wait_ge(S["D_qb"], nth(j, p, 4, i + 1))
                        hs = slice(4 * i, 4 * i + 4)
                        for t in range(2):
                            last = pool.tensor_tensor(o[:, hs, t, :], q[:, hs, 1 - t, :],
                                                      sin[:, t:t + 1, :].broadcast_to([P, 4, D1 // 2]), ALU.mult)
                        last.then_inc(S["D_half"], 1)
                for p in range(2):
                    e = WK[1][:, p, :].rearrange("p (h k) -> p h k", h=H1)
                    for i in range(4):
                        hs = slice(4 * i, 4 * i + 4)
                        pool.wait_ge(S["D_rsum"], nth(j, p, 4, i + 1))
                        pool.tensor_tensor(e[:, hs, :], e[:, hs, :], rec[:, p, hs].unsqueeze(2).broadcast_to([P, 4, T]), ALU.mult)\
                            .then_inc(S["D_pn"], 1)
                for p in range(2):
                    norm_tail(j, p, 3)
            with pool.Fori(0, PAIRS) as j:
                for p in range(2):
                    norm_tail(j, p, 4)
            pool.wait_ge(S["F_stats"], B)
            pool.tensor_scalar(F["ve"], F["mv"][:, :, 1], LN_EPS, None, ALU.add)
            pool.drain()
            pool.tensor_tensor(F["rstd"], F["ve"], cst("minus_half", B), ALU.pow).then_inc(S["F_rstd"], 1)

        @block.vector
        def _(dve):
            def ln_stats(j, p, s):
                dve.drain()
                dve.bn_stats(st[:, p, :], R[:, p, :])
                dve.drain()
                dve.bn_aggr(mv[:, p, :], st[:, p, :]).then_inc(stats, 1)

            def r_free(j, p, s):
                dve.wait_ge(normed, nth(j, p, before=B * s))

            def quantise(j, p, src, scale, wcol):
                dve.tensor_reduce(sm[:, p, scale:scale + 1], src, AX.X, ALU.max, apply_absolute_value=True)
                dve.drain()
                dve.tensor_scalar(sm[:, p, scale:scale + 1], sm[:, p, scale:scale + 1], TINY, None, ALU.max)
                dve.drain()
                dve.reciprocal(sm[:, p, 3:4], sm[:, p, scale:scale + 1])
                dve.tensor_scalar(sm[:, p, scale + 1:scale + 2], sm[:, p, scale:scale + 1], wsc[:, wcol:wcol + 1],
                                  1.0 / QMAX, ALU.mult, ALU.mult)
                dve.drain()
                dve.tensor_scalar(XN_q[:, p, :], src, sm[:, p, 3:4], QMAX, ALU.mult, ALU.mult)
                dve.drain()
                return dve.tensor_scalar(xq[:, p, :], XN_q[:, p, :], ROUND, -ROUND, ALU.add, ALU.add)

            XN_q = WK[3][:, :, 1024:1280]

            dve.wait_ge(const_in, 48)
            dve.tensor_copy(ident_bf[:, :], ident)
            dve.tensor_copy(causal_bf[:, :], cst("causal")).then_inc(bf_made, 1)
            dve.wait_ge(w0_in, 80)
            dve.tensor_reduce(wsc[:, 0:1], qkv_w, AX.XY, ALU.add, apply_absolute_value=True)
            dve.tensor_reduce(wsc[:, 1:2], proj_w, AX.XY, ALU.add, apply_absolute_value=True).then_inc(w_abs, 1)
            dve.wait_ge(w_abs_sum, 1)
            dve.tensor_scalar(wsc[:, 2:3], bank(1, 3)[:, 0:1], 1.0 / (3 * C * C), TINY, ALU.mult, ALU.max)
            dve.tensor_scalar(wsc[:, 3:4], bank(1, 3)[:, 1:2], 1.0 / (C * C), TINY, ALU.mult, ALU.max)
            dve.drain()

            def conv_taps(j, cs):
                for c in cs:
                    dve.wait_ge(toep_in[c % 2], j * 32 + (16 * (c // 2) + 16))
                    dve.scalar_tensor_tensor(toep[:, c % 2, 0:P], ident, d_skip[:, bass.ds(j * HEADS_A_TURN + c, 1)],
                                             toep[:, c % 2, 0:P], ALU.mult, ALU.add).then_inc(conv_w, 1)

            with dve.Fori(0, PAIRS) as j:
                for p in range(2):
                    dve.wait_ge(x_in[p], j * 16 + 16)
                    quantise(j, p, Xc[:, p, :], 0, 2).then_inc(S["A_xq"], 1)
                for p in range(2):
                    dve.wait_ge(S["A_qkv"], nth(j, p))
                    dve.scalar_tensor_tensor(WK[0][:, p, 0:2 * C], bank(p, 1), sm[:, p, 1:2], qkv_b[:, 0:2 * C],
                                             ALU.mult, ALU.add)
                    dve.scalar_tensor_tensor(WK[0][:, p, 2 * C:3 * C], bank(p, 2)[:, 0:C], sm[:, p, 1:2],
                                             qkv_b[:, 2 * C:3 * C], ALU.mult, ALU.add).then_inc(S["A_deq"], 1)
                conv_taps(j, (0, 1))
                dve.drain()
                for p in range(2):
                    e = probs(p)
                    qk_products(dve, p, 0)
                    dve.drain()
                    for half in range(2):
                        if half:
                            dve.wait_ge(S["A_qk_hi"], nth(j, p))
                        dve.tensor_reduce(e[:, half * 128:half * 128 + 128],
                                          WK[1 + half][:, p, :].rearrange("p (n d) -> p n d", d=D0), AX.X, ALU.add)
                    dve.drain()
                    dve.tensor_reduce(mx[:, p, :], e.rearrange("p (h g) -> p h g", h=H0), AX.X, ALU.max)
                    dve.drain()
                    dve.tensor_tensor(e.rearrange("p (h g) -> p h g", h=H0), e.rearrange("p (h g) -> p h g", h=H0),
                                      mx[:, p, :].unsqueeze(2).broadcast_to([P, H0, H0]), ALU.subtract)\
                        .then_inc(S["A_sub"], 1)
                conv_taps(j, (2, 3))
                for p in range(2):
                    att = WK[3][:, p, 512:512 + C]
                    dve.wait_ge(S["A_exp"], nth(j, p))
                    dve.tensor_reduce(nmx[:, p, :], probs(p).rearrange("p (h g) -> p h g", h=H0), AX.X, ALU.add)
                    pv_products(dve, p, 0)
                    dve.drain()
                    dve.reciprocal(rec[:, p, 0:H0], nmx[:, p, :])
                    for half in range(2):
                        if half:
                            dve.wait_ge(S["A_pv_hi"], nth(j, p))
                        dve.tensor_reduce(att[:, half * 128:half * 128 + 128],
                                          WK[1 + half][:, p, :].rearrange("p (n g) -> p n g", g=H0), AX.X, ALU.add)
                    dve.drain()
                    dve.tensor_tensor(att.rearrange("p (h d) -> p h d", d=D0), att.rearrange("p (h d) -> p h d", d=D0),
                                      rec[:, p, 0:H0].unsqueeze(2).broadcast_to([P, H0, D0]), ALU.mult)
                    dve.drain()
                    dve.tensor_tensor_reduce(XN_q[:, p, :], att, att, 1.0 / C, RMS_EPS, ALU.mult, ALU.add, sm[:, p, 4:5])\
                        .then_inc(S["A_ss"], 1)
                for p in range(2):
                    att = WK[3][:, p, 512:512 + C]
                    dve.wait_ge(S["A_rms"], nth(j, p))
                    dve.scalar_tensor_tensor(att, att, rms[:, p, 0:1], norm_w, ALU.mult, ALU.mult)
                    dve.drain()
                    quantise(j, p, att, 5, 3).then_inc(S["A_xq2"], 1)
                for p in range(2):
                    dve.wait_ge(S["A_y"], nth(j, p))
                    r_free(j, p, 0)
                    dve.scalar_tensor_tensor(R[:, p, :], bank(p, 2)[:, 0:C], sm[:, p, 6:7], proj_b, ALU.mult, ALU.add)
                    dve.drain()
                    dve.tensor_tensor(R[:, p, :], R[:, p, :], Xc[:, p, :], ALU.add).then_inc(x_free[p], 1)
                    ln_stats(j, p, 0)

            dve.wait_ge(conv_out, 2 + 2 * HS)
            with dve.Fori(0, PAIRS) as j:
                for p in range(2):
                    dve.wait_ge(S["B_xT"], nth(j, p))
                    for l in range(2):
                        dve.tensor_tensor(WK[0][:, p, l * 1024:(l + 1) * 1024].rearrange("p (n j) -> p n j", j=DS),
                                          Y[:, l, j * 2 + p, :].rearrange("p (n j) -> p n j", j=DS),
                                          bank(p, 0)[:, l * P:(l + 1) * P].unsqueeze(2).broadcast_to([P, P, DS]), ALU.mult)
                    dve.drain()
                    dve.tensor_reduce(WK[1][:, p, 0:2 * P].rearrange("p (n j) -> p n j", j=DS),
                                      WK[0][:, p, :].rearrange("p (n i j) -> p n j i", i=DS, j=DS),
                                      AX.X, ALU.add).then_inc(S["B_g"], 1)
                for p in range(2):
                    dve.wait_ge(S["B_o"], nth(j, p))
                    r_free(j, p, 1)
                    dve.tensor_tensor(R[:, p, :], bank(p, 1)[:, 0:C], Xc[:, p, :], ALU.add).then_inc(x_free[p], 1)
                    ln_stats(j, p, 1)

            NU = NE + 1
            with dve.Fori(0, PAIRS) as j:
                for p in range(2):
                    dve.wait_ge(S["C_lg"], nth(j, p))
                    dve.tensor_copy(lg[:, p, :], bank(p, 1)[:, 0:NE])
                    dve.drain()
                    dve.max(top[:, p, :], lg[:, p, :])
                    dve.drain()
                    dve.tensor_scalar(dl[:, p, :], lg[:, p, :], top[:, p, 0:1], None, ALU.subtract).then_inc(S["C_dl"], 1)
                    dve.max_index(topi[:, p, :], top[:, p, :], lg[:, p, :])
                    dve.drain()
                    dve.tensor_copy(topf[:, p, :], topi[:, p, :])
                    dve.drain()
                    dve.tensor_scalar(chosen[:, p, :], cst("iota", NE), topf[:, p, 0:1], None, ALU.is_equal)
                    dve.drain()
                    dve.scalar_tensor_tensor(chosen[:, p, :], cst("iota", NE), topf[:, p, 1:2], chosen[:, p, :],
                                             ALU.is_equal, ALU.add)
                for p in range(2):
                    dve.wait_ge(S["C_ex"], nth(j, p))
                    dve.reduce_sum(sm[:, p, 0:1], ex[:, p, :], axis=AX.X)
                    dve.drain()
                    dve.reciprocal(sm[:, p, 1:2], sm[:, p, 0:1])
                    dve.drain()
                    dve.scalar_tensor_tensor(cw[:, p, :], ex[:, p, :], sm[:, p, 1:2], chosen[:, p, :], ALU.mult, ALU.mult)
                dve.drain()
                for p in range(2):
                    for e in range(NU):
                        dve.wait_ge(S["C_silu"], nth(j, p, NU, e + 1))
                        if e < NE:
                            i = dve.scalar_tensor_tensor(WK[1][:, p, e * FE:(e + 1) * FE], WK[0][:, p, e * FE:(e + 1) * FE],
                                                         cw[:, p, e:e + 1], bank(p, e % 4)[:, FE:2 * FE], ALU.mult, ALU.mult)
                        else:
                            i = dve.tensor_tensor(WK[1][:, p, NE * FE:NF], WK[0][:, p, NE * FE:NF],
                                                  bank(p, 1)[:, 0:FSH], ALU.mult)
                        i.then_inc(S["C_act"], 1)
                for p in range(2):
                    dve.wait_ge(S["C_y"], nth(j, p))
                    r_free(j, p, 2)
                    dve.tensor_tensor(R[:, p, :], bank(p, 0)[:, 0:C], Xc[:, p, :], ALU.add).then_inc(x_free[p], 1)
                    ln_stats(j, p, 2)

            dve.wait_ge(w3_in, 96)
            with dve.Fori(0, PAIRS) as j:
                for p in range(2):
                    q = WK[0][:, p, :]
                    k = WK[3][:, p, 0:2 * D1]
                    kt = WK[3][:, p, 2 * D1:3 * D1]
                    sin = cst("sin")
                    cos = cst("cos")
                    dve.wait_ge(S["D_kv"], nth(j, p))
                    dve.tensor_tensor(k, bank(p, 0)[:, 0:2 * D1], bkv, ALU.add).then_inc(S["D_kvb"], 1)
                    dve.drain()
                    for t in range(2):
                        dve.tensor_tensor(kt[:, t * 64:t * 64 + 64], k[:, 64 - t * 64:128 - t * 64], sin[:, t * 64:t * 64 + 64], ALU.mult)
                    dve.drain()
                    dve.tensor_tensor(k[:, 0:D1], k[:, 0:D1], cos, ALU.mult)
                    dve.drain()
                    dve.tensor_tensor(k[:, 0:D1], k[:, 0:D1], kt, ALU.add)
                    for i in range(4):
                        dve.wait_ge(S["D_q"], nth(j, p, 4, i + 1))
                        dve.tensor_tensor(q[:, i * 512:(i + 1) * 512], bank(p, (i + 1) % 4), bq[:, i * 512:(i + 1) * 512],
                                          ALU.add).then_inc(S["D_qb"], 1)
                for p in range(2):
                    for i in range(4):
                        q = WK[0][:, p, i * 512:(i + 1) * 512]
                        dve.wait_ge(S["D_half"], nth(j, p, 4, i + 1))
                        dve.tensor_tensor(q.rearrange("p (h d) -> p h d", d=D1), q.rearrange("p (h d) -> p h d", d=D1),
                                          cst("cos").unsqueeze(1).broadcast_to([P, 4, D1]), ALU.mult)
                        dve.drain()
                        dve.tensor_tensor(q, q, WK[1][:, p, i * 512:(i + 1) * 512], ALU.add).then_inc(S["D_rot"], 1)
                for p in range(2):
                    for i in range(4):
                        hs = slice(4 * i, 4 * i + 4)
                        dve.wait_ge(S["D_s"], nth(j, p, 4, i + 1))
                        dve.tensor_reduce(mx[:, p, hs], bank(p, (i + 1) % 4).rearrange("p (g t) -> p g t", g=4), AX.X, ALU.max)
                        dve.drain()
                        dve.tensor_scalar(nmx[:, p, hs], mx[:, p, hs], -(D1 ** -0.5), None, ALU.mult).then_inc(S["D_max"], 1)
                for p in range(2):
                    for i in range(4):
                        hs = slice(4 * i, 4 * i + 4)
                        dve.wait_ge(S["D_exp"], nth(j, p, 4, i + 1))
                        dve.reciprocal(rec[:, p, hs], msq[:, p, hs]).then_inc(S["D_rsum"], 1)
                for p in range(2):
                    for i in range(2, 4):
                        dve.wait_ge(S["D_pT"], nth(j, p, 4, i + 1))
                        dve.tensor_copy(PT3(p, i), bank(p, (i + 1) % 4)).then_inc(S["D_pT_sv"], 1)
                for p in range(2):
                    for i in range(2, 4):
                        dve.wait_ge(S["D_o"], nth(j, p, 4, i + 1))
                        dve.tensor_copy(WK[0][:, p, i * 512:(i + 1) * 512], bank(p, (i + 1) % 4)).then_inc(S["D_o_sv"], 1)
                for p in range(2):
                    r_free(j, p, 3)
                    dve.tensor_tensor(R[:, p, :], Xc[:, p, :], bo, ALU.add)
                    dve.drain()
                    dve.wait_ge(S["D_y"], nth(j, p))
                    dve.tensor_tensor(R[:, p, :], bank(p, 1)[:, 0:C], R[:, p, :], ALU.add).then_inc(x_free[p], 1)
                    ln_stats(j, p, 3)

            def inv_sqrt(x, y, t):
                dve.tensor_scalar(t.bitcast(I32), x.bitcast(I32), 1, None, ALU.logical_shift_right)
                dve.drain()
                dve.tensor_scalar(y.bitcast(I32), t.bitcast(I32), -1.0, float(0x5F3759DF), ALU.mult, ALU.add)
                for _ in range(4):
                    dve.drain()
                    dve.scalar_tensor_tensor(t, y, -0.5, y, ALU.mult, ALU.mult)
                    dve.drain()
                    dve.tensor_tensor(t, t, x, ALU.mult)
                    dve.drain()
                    dve.scalar_tensor_tensor(y, t, 1.5, y, ALU.add, ALU.mult)
                dve.drain()

            dve.memset(WK[0][:, :, :], 0.0)
            dve.memset(WK[3][:, :, 0:H2 * PAD], 0.0)
            dve.drain()
            for p in range(2):
                last = dve.memset(VP(p)[:, :, D2:D2 + 1], 1.0)
            last.then_inc(pads_clear, 1)
            with dve.Fori(0, PAIRS) as j:
                for p in range(2):
                    dve.wait_ge(S["E_sq"], nth(j, p))
                    dve.tensor_reduce(msq[:, p, :], WK[2][:, p, 0:512].rearrange("p (h d) -> p h d", d=D2), AX.X, ALU.add)
                    dve.drain()
                    dve.tensor_scalar(msq[:, p, :], msq[:, p, :], RMS_EPS, None, ALU.add)
                    dve.drain()
                    inv_sqrt(msq[:, p, :], rms[:, p, :], rec[:, p, :])
                    dve.tensor_tensor(WK[0][:, p, :].rearrange("p (h d) -> p h d", d=PAD)[:, :, 0:D2],
                                      bank(p, 1).rearrange("p (h d) -> p h d", d=D2),
                                      rms[:, p, :].unsqueeze(2).broadcast_to([P, 2 * H2, D2]), ALU.mult)\
                        .then_inc(S["E_pad"], 1)
                for p in range(2):
                    dve.wait_ge(S["E_o"], nth(j, p))
                    r_free(j, p, 4)
                    o = PS[:, 4 * p + 2:4 * p + 4, :].rearrange("p k (h d) -> p (k h) d", d=PAD)
                    dve.reciprocal(rec[:, p, 0:H2], o[:, :, D2])
                    dve.drain()
                    dve.tensor_tensor(R[:, p, :].rearrange("p (h d) -> p h d", d=D2), o[:, :, 0:D2],
                                      rec[:, p, 0:H2].unsqueeze(2).broadcast_to([P, H2, D2]), ALU.mult)
                    dve.drain()
                    dve.tensor_tensor(R[:, p, :], R[:, p, :], Xc[:, p, :], ALU.add).then_inc(x_free[p], 1)
                    ln_stats(j, p, 4)

            dve.wait_ge(w5_in, 80)
            for b in range(B):
                dve.wait_ge(normed, 2 + 4 * B + b + 1)
                dve.tensor_tensor_reduce(F["junk"], X[:, b, :], wr, 1.0, 0.0, ALU.mult, ALU.add, F["logit"][:, b:b + 1])
                dve.drain()
            dve.tensor_scalar(F["logit"], F["logit"], br, None, ALU.add)
            dve.drain()
            for b in range(B):
                last = dve.tensor_scalar(F["diag"][:, b, :], ident, F["logit"][:, b:b + 1], None, ALU.mult)
            last.then_inc(S["F_diag"], 1)
            row = PS[:, 0:2, :].rearrange("p k (b t) -> p (k b) t", b=4)
            dve.wait_ge(S["F_row"], 1)
            dve.tensor_reduce(F["max"], row, AX.X, ALU.max)
            for b in range(B):
                dve.tensor_scalar(F["tmp"][:, b, :], row[:, b, :], F["logit"][:, b:b + 1], 0.0, ALU.is_gt, ALU.add,
                                  accum_out=F["above"][:, b:b + 1])
            dve.drain()
            for b in range(B):
                dve.scalar_tensor_tensor(F["tmp"][:, b, :], row[:, b, :], F["logit"][:, b:b + 1], cst("before"),
                                         ALU.is_equal, ALU.mult, accum_out=F["tied"][:, b:b + 1])
            dve.drain()
            dve.tensor_tensor(F["rank"], F["above"], F["tied"], ALU.add)
            dve.tensor_tensor(F["e"], F["logit"], F["max"], ALU.subtract).then_inc(S["F_rank"], 1)
            dve.drain()
            dve.tensor_scalar(F["keep"], F["rank"], float(TOPK), None, ALU.is_lt)
            dve.tensor_scalar(F["far"], F["rank"], float(TOPK), 1000.0, ALU.is_ge, ALU.mult)
            dve.tensor_tensor(F["slot"], F["rank"], cst("first_slot"), ALU.add)
            dve.drain()
            dve.tensor_tensor(F["slot"], F["slot"], F["far"], ALU.add)
            dve.drain()
            for b in range(B):
                last = dve.tensor_scalar(F["pick"][:, b, :], cst("iota"), F["slot"][:, b:b + 1], None, ALU.is_equal)
            last.then_inc(S["F_pick"], 1)
            dve.wait_ge(S["F_ew"], 1)
            dve.tensor_tensor(F["e"], F["e"], F["keep"], ALU.mult).then_inc(S["F_keep"], 1)
            dve.wait_ge(S["F_esum"], 1)
            dve.reciprocal(F["esum"], PS[:, 7, 0:B])
            dve.drain()
            dve.tensor_tensor(F["w"], F["e"], F["esum"], ALU.mult)
            dve.tensor_scalar(F["R"], X[:, :, :], 2.0, None, ALU.mult)
            dve.wait_ge(S["F_pickT"], 1)
            dve.tensor_copy(F["pickT"].rearrange("p b n -> p (b n)"), PS[:, 4:6, :].rearrange("p k n -> p (k n)"))\
                .then_inc(S["F_pickT_sb"], 1)
            dve.wait_ge(S["F_down"], 1)
            dve.tensor_tensor(F["ol"], PS[:, 6, 0:C], b2, ALU.add).then_inc(S["F_ol"], 1)
            for b in range(B):
                dve.wait_ge(S["F_back"], b + 1)
                dve.scalar_tensor_tensor(F["R"][:, b, :], PS[:, b % 4, 0:C], F["w"][:, b:b + 1],
                                         F["R"][:, b, :], ALU.mult, ALU.add)
                dve.drain()
                dve.bn_stats(F["st"][:, b, :], F["R"][:, b, :])
                dve.drain()
                dve.bn_aggr(F["mv"][:, b, :], F["st"][:, b, :]).then_inc(S["F_stats"], 1)
            dve.wait_ge(S["F_rstd"], 1)
            for b in range(B):
                dve.tensor_scalar(X[:, b, :], F["R"][:, b, :], F["mv"][:, b, 0:1], F["rstd"][:, b:b + 1],
                                  ALU.subtract, ALU.mult).then_inc(S["F_out"], 1)

        @block.scalar
        def _(act):
            def copy(dst, src):
                return act.activation(dst, src, ACT.Copy)

            act.sem_inc(conv_out, 2)

            def conv_copies(j, cs):
                for c in cs:
                    for l in range(2):
                        act.wait_ge(conv_half if l == 0 else conv_mm, head(j, c, before=2 * l))
                        copy(Y[:, l, :, :].rearrange("p b (h n) -> p b h n", h=HS)[:, :, j * HEADS_A_TURN + c, :],
                             bank(l, 3).rearrange("p (b n) -> p b n", b=B)).then_inc(conv_out, 1)

            act.wait_ge(w0_in, 80)
            act.activation(qkv_sign, qkv_w, ACT.Sign)
            act.activation(proj_sign, proj_w, ACT.Sign).then_inc(w_signed, 1)
            with act.Fori(0, PAIRS) as j:
                for p in range(2):
                    act.wait_ge(S["A_xqT"], nth(j, p))
                    copy(xqT[:, p, :, :].rearrange("p k t -> p (k t)"), bank(p, 0)[:, 0:P].bitcast(BF16)).then_inc(S["A_xqT_sb"], 1)
                conv_copies(j, (0, 1))
                for p in range(2):
                    act.wait_ge(S["A_sub"], nth(j, p))
                    act.activation(probs(p), probs(p), ACT.Exp, scale=D0 ** -0.5).then_inc(S["A_exp"], 1)
                conv_copies(j, (2, 3))
                for p in range(2):
                    act.wait_ge(S["A_xq2T"], nth(j, p))
                    copy(xqT[:, p, :, :].rearrange("p k t -> p (k t)"), bank(p, 1)[:, 0:P].bitcast(BF16)).then_inc(S["A_xq2T_sb"], 1)

            def xt_copy(j, p, stage):
                act.wait_ge(S[f"{stage}_xT"], nth(j, p))
                copy(XT[:, p, :, :].rearrange("p k t -> p (k t)"), bank(p, 0)[:, 0:C]).then_inc(S[f"{stage}_xT_sb"], 1)

            NU = NE + 1
            with act.Fori(0, PAIRS) as j:
                for p in range(2):
                    xt_copy(j, p, "C")
                for p in range(2):
                    for e in range(NU):
                        act.wait_ge(S["C_gu"], nth(j, p, NU, e + 1))
                        n = FE if e < NE else FSH
                        act.activation(WK[0][:, p, e * FE:e * FE + n], bank(p, e % 4)[:, 0:n], ACT.Silu).then_inc(S["C_silu"], 1)
                for p in range(2):
                    for i in range(4):
                        act.wait_ge(S["C_aT"], nth(j, p, 4, i + 1))
                        if i < 3:
                            last = copy(WK[2][:, p, i * 512:(i + 1) * 512], bank(p, i))
                        else:
                            copy(WK[2][:, p, 1536:1664], bank(p, 3)[:, 0:P])
                            last = copy(WK[2][0:NF - 13 * P, p, 1664:1792], bank(p, 3)[0:NF - 13 * P, P:2 * P])
                    last.then_inc(S["C_aT_sb"], 1)
            with act.Fori(0, PAIRS) as j:
                for p in range(2):
                    xt_copy(j, p, "D")
                for p in range(2):
                    act.wait_ge(S["D_qkT"], nth(j, p, 5, 1))
                    copy(WK[3][:, p, 512:512 + P], bank(p, 0)[:, 0:P]).then_inc(S["D_qkT_sb"], 1)
                    for i in range(4):
                        act.wait_ge(S["D_qkT"], nth(j, p, 5, i + 2))
                        copy(WK[2][:, p, i * 512:(i + 1) * 512], bank(p, (i + 1) % 4)).then_inc(S["D_qkT_sb"], 1)
                for p in range(2):
                    for i in range(4):
                        act.wait_ge(S["D_max"], nth(j, p, 4, i + 1))
                        for n in range(4):
                            h = 4 * i + n
                            last = act.activation(WK[1][:, p, h * T:(h + 1) * T], bank(p, (i + 1) % 4)[:, n * T:(n + 1) * T],
                                                  ACT.Exp, bias=nmx[:, p, h:h + 1], scale=D1 ** -0.5,
                                                  accum_out=msq[:, p, h:h + 1])
                        last.then_inc(S["D_exp"], 1)
                for p in range(2):
                    for i in range(2):
                        act.wait_ge(S["D_pT"], nth(j, p, 4, i + 1))
                        copy(PT3(p, i), bank(p, i + 1)).then_inc(S["D_pT_sa"], 1)
                for p in range(2):
                    for i in range(2):
                        act.wait_ge(S["D_o"], nth(j, p, 4, i + 1))
                        copy(WK[0][:, p, i * 512:(i + 1) * 512], bank(p, i + 1)).then_inc(S["D_o_sa"], 1)
            act.wait_ge(pads_clear, 1)
            with act.Fori(0, PAIRS) as j:
                for p in range(2):
                    xt_copy(j, p, "E")
                for p in range(2):
                    act.wait_ge(S["E_qkv"], nth(j, p, before=2))
                    act.activation(WK[2][:, p, 0:512], bank(p, 1), ACT.Square, scale=D2 ** -0.5)
                    copy(VP(p)[:, :, 0:D2],
                         bank(p, 2)[:, 0:C].rearrange("p (h d) -> p h d", d=D2)).then_inc(S["E_sq"], 1)
                for p in range(2):
                    for i in range(4):
                        act.wait_ge(S["E_qkT"], nth(j, p, 4, i + 1))
                        last = copy(ET(p, i), bank(p, i))
                    last.then_inc(S["E_qkT_sb"], 1)
                for p in range(2):
                    for n in range(8):
                        act.wait_ge(S["E_s"], nth(j, p, 8, n + 1))
                        act.activation(WK[1 + n // 4][:, p, (n % 4) * 512:(n % 4 + 1) * 512], bank(p, n % 4), ACT.Exp,
                                       scale=D2 ** -0.5).then_inc(S["E_exp"], 1)
                for p in range(2):
                    for i in range(2):
                        act.wait_ge(S["E_oT"], nth(j, p, 2, i + 1))
                        copy(OT(p)[:, i * 512:(i + 1) * 512], bank(p, i)).then_inc(S["E_oT_sb"], 1)
            act.wait_ge(S["F_rank"], 1)
            act.activation(F["e"], F["e"], ACT.Exp).then_inc(S["F_ew"], 1)
            act.wait_ge(S["F_gath"], 1)
            for k in range(KC):
                last = copy(F["gath"][:, k, :], PS[:, 2 + k, 0:P])
            last.then_inc(S["F_gath_sb"], 1)
            act.wait_ge(w5_in, 80)
            for f in range(NFF):
                act.wait_ge(S["F_up"], f + 1)
                act.activation(F["hid"][:, f, :], PS[:, f % 4, 0:P], ACT.Gelu,
                               bias=b1[:, f:f + 1]).then_inc(S["F_gelu"], 1)

        @block.tensor
        def _(pe):
            def turn_x(j, p, s, stage):
                pe.wait_ge(x_in[p], j * 16 + (s * 64 + 16))
                for k in range(KC):
                    last = pe.transpose(bank(p, 0)[:, k * P:(k + 1) * P], Xc[:, p, k * P:(k + 1) * P], ident)
                last.then_inc(S[f"{stage}_xT"], 1)

            pe.sem_inc(conv_mm, 2)
            pe.sem_inc(S["E_qkv"], 2)
            pe.wait_ge(const_in, 48)
            pe.wait_ge(bf_made, 1)
            pe.wait_ge(w_abs, 1)
            pe.matmul(bank(1, 3)[:, 0:2], ones, wsc[:, 0:2], start=True, stop=True).then_inc(w_abs_sum, 1)
            def conv_heads(j, cs):
                for c in cs:
                    near, far = toep[:, c % 2, 0:P], toep[:, c % 2, P:2 * P]
                    pe.wait_ge(conv_w, head(j, c))
                    pe.wait_ge(conv_kv, head(j, c))
                    pe.wait_ge(conv_out, j * (2 * HEADS_A_TURN) + (2 * c + 1))
                    pe.matmul(bank(0, 3), near, conv_kv_tile(c, 0), start=True, stop=True).then_inc(conv_half, 1)
                    pe.wait_ge(conv_out, j * (2 * HEADS_A_TURN) + (2 * c + 2))
                    pe.matmul(bank(1, 3), near, conv_kv_tile(c, 1), start=True, stop=False)
                    pe.matmul(bank(1, 3), far, conv_kv_tile(c, 0), start=False, stop=True).then_inc(conv_mm, 1)

            pe.wait_ge(w_signed, 1)
            with pe.Fori(0, PAIRS) as j:
                for p in range(2):
                    pe.wait_ge(S["A_xq"], nth(j, p))
                    for k in range(KC):
                        last = pe.transpose(bank(p, 0)[:, 0:P].bitcast(BF16)[:, k * P:(k + 1) * P], xq[:, p, k * P:(k + 1) * P], ident_bf[:, :])
                    last.then_inc(S["A_xqT"], 1)
                for p in range(2):
                    pe.wait_ge(S["A_xqT_sb"], nth(j, p))
                    for n, (lo, hi) in enumerate(((0, 512), (512, 768))):
                        for k in range(KC):
                            last = pe.matmul(bank(p, 1 + n)[:, 0:hi - lo], xqT[:, p, k, :], qkv_sign[:, k, lo:hi],
                                             start=(k == 0), stop=(k == KC - 1))
                    last.then_inc(S["A_qkv"], 1)
                conv_heads(j, range(HEADS_A_TURN))
                for p in range(2):
                    pe.wait_ge(S["A_xq2"], nth(j, p))
                    for k in range(KC):
                        last = pe.transpose(bank(p, 1)[:, 0:P].bitcast(BF16)[:, k * P:(k + 1) * P], xq[:, p, k * P:(k + 1) * P], ident_bf[:, :])
                    last.then_inc(S["A_xq2T"], 1)
                for p in range(2):
                    pe.wait_ge(S["A_xq2T_sb"], nth(j, p))
                    for k in range(KC):
                        last = pe.matmul(bank(p, 2)[:, 0:C], xqT[:, p, k, :], proj_sign[:, k, :], start=(k == 0), stop=(k == KC - 1))
                    last.then_inc(S["A_y"], 1)
            with pe.Fori(0, PAIRS) as j:
                for p in range(2):
                    turn_x(j, p, 1, "B")
                for p in range(2):
                    pe.wait_ge(S["B_g"], nth(j, p))
                    for l in range(2):
                        last = pe.transpose(bank(p, 1)[:, l * P:(l + 1) * P], WK[1][:, p, l * P:(l + 1) * P], ident)
                    last.then_inc(S["B_o"], 1)
            NU = NE + 1
            pe.wait_ge(w2_in, 64)
            with pe.Fori(0, PAIRS) as j:
                for p in range(2):
                    turn_x(j, p, 2, "C")
                for p in range(2):
                    pe.wait_ge(S["C_xT_sb"], nth(j, p))
                    for k in range(KC):
                        last = pe.matmul(bank(p, 1)[:, 0:NE], XT[:, p, k, :], router_w[:, k, :], start=(k == 0), stop=(k == KC - 1))
                    last.then_inc(S["C_lg"], 1)
                for p in range(2):
                    pe.wait_ge(S["C_dl"], nth(j, p))
                    for e in range(NE):
                        if e >= 4:
                            pe.wait_ge(S["C_act"], nth(j, p, NU, e - 3))
                        for k in range(KC):
                            last = pe.matmul(bank(p, e % 4)[:, 0:2 * FE], XT[:, p, k, :], gu_w[:, k, e * 2 * FE:(e + 1) * 2 * FE],
                                             start=(k == 0), stop=(k == KC - 1))
                        last.then_inc(S["C_gu"], 1)
                    pe.wait_ge(S["C_act"], nth(j, p, NU, 6))
                    for n in range(2):
                        c = 2 * FE * NE + n * FSH
                        for k in range(KC):
                            last = pe.matmul(bank(p, n)[:, 0:FSH], XT[:, p, k, :], gu_w[:, k, c:c + FSH],
                                             start=(k == 0), stop=(k == KC - 1))
                    last.then_inc(S["C_gu"], 1)
                for p in range(2):
                    pe.wait_ge(S["C_act"], nth(j, p, NU, NU))
                    for i in range(4):
                        for f in range(4 * i, min(4 * i + 4, NFT)):
                            w = min(P, NF - f * P)
                            last = pe.transpose(bank(p, i)[0:w, (f % 4) * P:(f % 4 + 1) * P], WK[1][:, p, f * P:f * P + w], ident)
                        last.then_inc(S["C_aT"], 1)
                for p in range(2):
                    pe.wait_ge(S["C_aT_sb"], nth(j, p))
                    for f in range(NFT):
                        w = min(P, NF - f * P)
                        last = pe.matmul(bank(p, 0)[:, 0:C], WK[2][0:w, p, f * P:(f + 1) * P], down_w[0:w, f, :],
                                         start=(f == 0), stop=(f == NFT - 1))
                    last.then_inc(S["C_y"], 1)
            pe.wait_ge(w3_in, 96)
            with pe.Fori(0, PAIRS) as j:
                for p in range(2):
                    turn_x(j, p, 3, "D")
                for p in range(2):
                    pe.wait_ge(S["D_xT_sb"], nth(j, p))
                    for k in range(KC):
                        last = pe.matmul(bank(p, 0)[:, 0:2 * D1], XT[:, p, k, :], wkv[:, k, :], start=(k == 0), stop=(k == KC - 1))
                    last.then_inc(S["D_kv"], 1)
                    for i in range(4):
                        if i == 3:
                            pe.wait_ge(S["D_kvb"], nth(j, p))
                        for k in range(KC):
                            last = pe.matmul(bank(p, (i + 1) % 4), XT[:, p, k, :], wq[:, k, i * 512:(i + 1) * 512],
                                             start=(k == 0), stop=(k == KC - 1))
                        last.then_inc(S["D_q"], 1)
                for p in range(2):
                    pe.wait_ge(S["D_qb"], nth(j, p, 4, 1))
                    pe.transpose(bank(p, 0)[:, 0:P], WK[3][:, p, 0:D1], ident).then_inc(S["D_qkT"], 1)
                    for i in range(4):
                        pe.wait_ge(S["D_rot"], nth(j, p, 4, i + 1))
                        if i == 3:
                            pe.wait_ge(S["D_qkT_sb"], nth(j, p, 5, 1))
                        for n in range(4):
                            c = (4 * i + n) * D1
                            last = pe.transpose(bank(p, (i + 1) % 4)[:, n * T:(n + 1) * T], WK[0][:, p, c:c + D1], ident)
                        last.then_inc(S["D_qkT"], 1)
                for p in range(2):
                    for i in range(4):
                        b = (i + 1) % 4
                        pe.wait_ge(S["D_qkT_sb"], nth(j, p, 5, i + 2))
                        pe.matmul(bank(p, b), ident_bf[:, :], causal_bf[:, :].unsqueeze(1).broadcast_to([P, 4, P]), start=True, stop=True)
                        for n in range(4):
                            c = (4 * i + n) * T
                            last = pe.matmul(bank(p, b)[:, n * T:(n + 1) * T], WK[2][:, p, c:c + T], WK[3][:, p, 512:512 + P],
                                             start=False, stop=True, skip_group_check=True)
                        last.then_inc(S["D_s"], 1)
                for p in range(2):
                    for i in range(4):
                        pe.wait_ge(S["D_pn"], nth(j, p, 4, i + 1))
                        for n in range(4):
                            c = (4 * i + n) * T
                            last = pe.transpose(bank(p, (i + 1) % 4)[:, n * T:(n + 1) * T], WK[1][:, p, c:c + T], ident)
                        last.then_inc(S["D_pT"], 1)
                for p in range(2):
                    for i in range(4):
                        pe.wait_ge(S["D_pT_sa" if i < 2 else "D_pT_sv"], nth(j, p, 2, i % 2 + 1))
                        pe.matmul(bank(p, (i + 1) % 4), WK[3][:, p, D1:2 * D1], PT3(p, i), start=True, stop=True).then_inc(S["D_o"], 1)
                for p in range(2):
                    for i in range(4):
                        pe.wait_ge(S["D_o_sa" if i < 2 else "D_o_sv"], nth(j, p, 2, i % 2 + 1))
                        for h in range(4 * i, 4 * i + 4):
                            last = pe.matmul(bank(p, 1)[:, 0:C], WK[0][:, p, h * T:(h + 1) * T], wo[:, h, :],
                                             start=(h == 0), stop=(h == H1 - 1))
                    last.then_inc(S["D_y"], 1)
            pe.wait_ge(w4_in, 32)
            with pe.Fori(0, PAIRS) as j:
                for p in range(2):
                    turn_x(j, p, 4, "E")
                for p in range(2):
                    pe.wait_ge(ctx_in[p], j * 16 + 16)
                    for k in range(KC):
                        pe.matmul(bank(p, 1)[:, C:2 * C], CT[:, p, k, :], xwkv[:, k, 0:C], start=(k == 0), stop=(k == KC - 1))
                    for k in range(KC):
                        pe.matmul(bank(p, 2)[:, 0:C], CT[:, p, k, :], xwkv[:, k, C:2 * C], start=(k == 0), stop=(k == KC - 1))
                    pe.wait_ge(S["E_xT_sb"], nth(j, p))
                    for k in range(KC):
                        last = pe.matmul(bank(p, 1)[:, 0:C], XT[:, p, k, :], xwq[:, k, :], start=(k == 0), stop=(k == KC - 1))
                    last.then_inc(S["E_qkv"], 1)
                for p in range(2):
                    pe.wait_ge(S["E_pad"], nth(j, p))
                    for i in range(4):
                        for n in range(4):
                            c = (4 * i + n) * P
                            last = pe.transpose(bank(p, i)[:, n * P:(n + 1) * P], WK[0][:, p, c:c + P], ident)
                        last.then_inc(S["E_qkT"], 1)
                for p in range(2):
                    pe.wait_ge(S["E_qkT_sb"], nth(j, p))
                    for n in range(8):
                        rd, r = n // 4, n % 4
                        if rd:
                            pe.wait_ge(S["E_exp"], nth(j, p, 8, r + 1))
                        at = slice(PAD * r, PAD * r + D2)
                        for g in range(4):
                            last = pe.matmul(bank(p, r)[:, g * P:(g + 1) * P], ET(p, 2 + rd)[at, g * P:(g + 1) * P],
                                             ET(p, rd)[at, g * P:(g + 1) * P], start=True, stop=True)
                        last.then_inc(S["E_s"], 1)
                for p in range(2):
                    for i in range(2):
                        pe.wait_ge(S["E_exp"], nth(j, p, 8, 8))
                        for g in range(4):
                            for r in range(4):
                                h = 16 * i + 4 * g + r
                                last = pe.matmul(bank(p, i)[PAD * r:PAD * (r + 1), g * P:(g + 1) * P], VP(p)[:, h, :],
                                                 WK[1 + i][:, p, (4 * r + g) * P:(4 * r + g + 1) * P], start=True, stop=True)
                        last.then_inc(S["E_oT"], 1)
                for p in range(2):
                    for i in range(2):
                        pe.wait_ge(S["E_oT_sb"], nth(j, p, 2, i + 1))
                        for g in range(4):
                            last = pe.transpose(bank(p, 2 + i)[:, g * P:(g + 1) * P], OT(p)[:, (4 * i + g) * P:(4 * i + g + 1) * P], ident)
                    last.then_inc(S["E_o"], 1)
            pe.wait_ge(S["F_diag"], 1)
            for b in range(B):
                last = pe.matmul(PS[:, b // 4, (b % 4) * P:(b % 4 + 1) * P], ones, F["diag"][:, b, :], start=True, stop=True)
            last.then_inc(S["F_row"], 1)
            pe.wait_ge(S["F_pick"], 1)
            for k in range(KC):
                for b in range(B):
                    last = pe.matmul(PS[:, 2 + k, 0:P], X[:, b, k * P:(k + 1) * P], F["pick"][:, b, :], start=(b == 0), stop=(b == B - 1))
            last.then_inc(S["F_gath"], 1)
            for b in range(B):
                last = pe.transpose(PS[:, 4 + b // 4, (b % 4) * P:(b % 4 + 1) * P], F["pick"][:, b, :], ident)
            last.then_inc(S["F_pickT"], 1)
            pe.wait_ge(S["F_keep"], 1)
            pe.matmul(PS[:, 7, 0:B], ones, F["e"], start=True, stop=True).then_inc(S["F_esum"], 1)
            pe.wait_ge(S["F_gath_sb"], 1)
            pe.wait_ge(w5_in, 80)
            for f in range(NFF):
                if f >= 4:
                    pe.wait_ge(S["F_gelu"], f - 3)
                for k in range(KC):
                    last = pe.matmul(PS[:, f % 4, 0:P], w1[:, k, f * P:(f + 1) * P], F["gath"][:, k, :],
                                     start=(k == 0), stop=(k == KC - 1))
                last.then_inc(S["F_up"], 1)
            for f in range(NFF):
                pe.wait_ge(S["F_gelu"], f + 1)
                last = pe.matmul(PS[:, 6, 0:C], F["hid"][:, f, :], w2[:, f, :], start=(f == 0), stop=(f == NFF - 1))
            last.then_inc(S["F_down"], 1)
            pe.wait_ge(S["F_pickT_sb"], 1)
            pe.wait_ge(S["F_ol"], 1)
            for b in range(B):
                if b >= 4:
                    pe.wait_ge(S["F_stats"], b - 3)
                pe.matmul(PS[:, b % 4, 0:C], F["pickT"][:, b, :], F["ol"], start=True, stop=True)\
                    .then_inc(S["F_back"], 1)


def constants():
    c = np.zeros((P, NCONST), np.float32)

    def put(name, value):
        c[:, CONST_AT[name][0]:CONST_AT[name][1]] = value

    t = np.arange(P)
    put("ident", np.eye(P))
    put("ones", 1.0)
    put("before", t[None, :] < t[:, None])
    put("iota", t[None, :])
    put("causal", np.where(t[None, :] <= t[:, None], 0.0, -1e30))
    inv_freq = (1.0 / np.float32(10000.0) ** (np.arange(0, D1, 2, dtype=np.float32) / np.float32(D1))).astype(np.float32)
    ang = (t.astype(np.float32)[:, None] * inv_freq[None, :]).astype(np.float32)
    put("cos", np.tile(np.cos(ang), (1, 2)))
    put("sin", np.concatenate([-np.sin(ang), np.sin(ang)], axis=1))
    put("minus_half", -0.5)
    put("rms_eps", RMS_EPS)
    put("ln_eps", LN_EPS)
    put("euler", np.e)
    put("first_slot", TOPK * np.arange(B)[None, :])
    return c


def kernel(**inputs):
    import concourse.bacc as _bacc
    from concourse.bass_utils import run_bass_kernel_spmd as _run

    g = {k: np.asarray(v) for k, v in inputs.items()}

    def tiles(w):
        n = -(-w.shape[0] // P)
        if n * P != w.shape[0]:
            w = np.concatenate([w, np.zeros((n * P - w.shape[0], w.shape[1]), w.dtype)])
        return w.reshape(n, P, -1).transpose(1, 0, 2)

    halves = np.concatenate([np.arange(0, D1, 2), np.arange(1, D1, 2)])
    qcols = (np.arange(H1)[:, None] * D1 + halves[None, :]).ravel()
    xkv = np.concatenate([g["L1_xattn_Wk"], g["L1_xattn_Wv"]])
    taps = g["L0_xattn_ssm_kernel"]
    taps = np.concatenate([np.zeros((HS, P - 1), taps.dtype), taps], axis=1)
    toep = np.lib.stride_tricks.sliding_window_view(taps, C, axis=1)[:, ::-1, :]
    down = g["L0_ffn_down_weights"].transpose(0, 2, 1).reshape(NE * FE, C)
    gu = g["L0_ffn_gate_up_weights"].reshape(NE * 2 * FE, C)
    arrays = {
        "x": g["x"],
        "const": constants(),
        "ctxT": g["ctx_2048"].reshape(B, T, KC, P).transpose(3, 0, 2, 1),
        "d_skip": g["L0_xattn_D"],
        "toep": toep,
        "qkv_w": tiles(g["L0_attn_qkv_w"].T), "qkv_b": g["L0_attn_qkv_b"],
        "proj_w": tiles(g["L0_attn_proj_w"].T), "proj_b": g["L0_attn_proj_b"],
        "norm_w": g["L0_attn_norm_w"],
        "router_w": tiles(g["L0_ffn_gate_weight"].T),
        "gu_w": tiles(np.concatenate([gu, g["L0_ffn_shared_gate_up"]]).T),
        "down_w": tiles(np.concatenate([down, g["L0_ffn_shared_down"].T])),
        "wq": tiles(g["L1_attn_Wq"][:, qcols]), "bq": g["L1_attn_bq"][qcols],
        "wkv": tiles(np.concatenate([g["L1_attn_Wk"][:, halves], g["L1_attn_Wv"]], axis=1)),
        "bkv": np.concatenate([g["L1_attn_bk"][halves], g["L1_attn_bv"]]),
        "wo": tiles(g["L1_attn_Wo"]), "bo": g["L1_attn_bo"],
        "xwq": tiles(g["L1_xattn_Wq"].T),
        "xwkv": tiles(np.concatenate([xkv[0::2], xkv[1::2]]).T),
        "wr": g["L1_ffn_Wr"][:, 0], "br": g["L1_ffn_br"],
        "w1": tiles(g["L1_ffn_W1"]), "b1": g["L1_ffn_b1"].reshape(NFF, P).T,
        "w2": tiles(g["L1_ffn_W2"]), "b2": g["L1_ffn_b2"],
    }
    arrays = {f"in_{k}": np.ascontiguousarray(v) for k, v in arrays.items()}
    nc = _bacc.Bacc("TRN2", target_bir_lowering=False, num_devices=1)
    a = {k[3:]: nc.dram_tensor(k, v.shape, F32, kind="ExternalInput").ap() for k, v in arrays.items()}
    a["out"] = nc.dram_tensor("out_0", (B, T, C), F32, kind="ExternalOutput").ap()
    build(nc, a)
    r = _run(nc, [arrays], core_ids=[0])
    return r.results[0]["out_0"]
```

```python
from contextlib import ExitStack

import numpy as np

import concourse.bass as bass
from concourse import mybir

ALU = mybir.AluOpType
ACT = mybir.ActivationFunctionType
AX = mybir.AxisListType
F32 = mybir.dt.float32
BF16 = mybir.dt.bfloat16
U32 = mybir.dt.uint32
I32 = mybir.dt.int32

P = 128
B, T, C = 8, 128, 256
KC = C // P
PAIRS = B // 2
LN_EPS = 1e-5
RMS_EPS = 1e-6
QMAX = 127.0
TINY = 1e-5
ROUND = 12582912.0

H0, D0 = 16, 16
HS, DS = 16, 8
NE, FE = 8, 176
FSH = 352
NF = NE * FE + FSH
NFT = -(-NF // P)
H1, D1 = 16, 128
H2, D2 = 32, 8
DFF = 1024
NFF = DFF // P
TOPK = 16
PAD = 32

CONSTS = {"ident": 128, "ones": 128, "before": 128, "iota": 128, "causal": 128, "cos": 128,
          "sin": 128, "minus_half": 64, "ln_eps": 1, "minus_one": 1,
          "euler": 8, "first_slot": 8}
CONST_AT = {}
_at = 0
for _name, _width in CONSTS.items():
    CONST_AT[_name] = (_at, _at + _width)
    _at += _width
NCONST = _at


def build(nc, a):
    ctx = ExitStack()
    with ctx:
        def sb(name, shape, dt=F32):
            return ctx.enter_context(nc.sbuf_tensor(name, shape, dt))

        def sem(name):
            return ctx.enter_context(nc.semaphore(name))

        def rows(name, n):
            return a[name].rearrange("(o n) -> o n", o=1).broadcast_to([P, n])

        PS = ctx.enter_context(nc.psum_tensor("PS", [P, 8, 512], F32))

        def bank(p, k):
            return PS[:, 4 * p + k, :]

        X = sb("X", [P, B, C])
        const = sb("const", [P, NCONST])
        ident_bf = sb("ident_bf", [P, P], BF16)
        causal_bf = sb("causal_bf", [P, P], BF16)
        w0 = sb("w0", [P, KC * 4 * C])
        qkv_w = w0[:, 0:KC * 3 * C].rearrange("p (k n) -> p k n", k=KC)
        proj_w = w0[:, KC * 3 * C:].rearrange("p (k n) -> p k n", k=KC)
        w2 = w0[:, :].rearrange("p (k n) -> p k n", k=NFF)
        signs = sb("signs", [P, KC * 2 * C])
        qkv_sign = signs[:, 0:KC * 3 * C // 2].bitcast(BF16).rearrange("p (k n) -> p k n", k=KC)
        proj_sign = signs[:, KC * 3 * C // 2:].bitcast(BF16).rearrange("p (k n) -> p k n", k=KC)
        CT = sb("CT", [P, 2, KC, P])
        proj_b = CT[:, 0, :, :].rearrange("p k t -> p (k t)")
        norm_w = CT[:, 1, :, :].rearrange("p k t -> p (k t)")
        gu_w = sb("gu_w", [P, KC, NE + 2 * NF])
        down = sb("down", [P, NFT * C])
        down_w = down[:, :].rearrange("p (k n) -> p k n", k=NFT)
        ctxT = down[:, 0:B * C].rearrange("p (b k t) -> p b k t", b=B, k=KC)
        qkv_b = down[:, B * C:B * C + 3 * C]
        big = sb("big", [P, 2 * B * HS * DS * DS])
        Y = big[:, :].rearrange("p (l b n) -> p l b n", l=2, b=B)
        off = [0]

        def late(n):
            off[0] += n
            return big[:, off[0] - n:off[0]]

        wq = late(KC * H1 * D1).rearrange("p (k n) -> p k n", k=KC)
        wkv = late(KC * 2 * D1).rearrange("p (k n) -> p k n", k=KC)
        wo = late(H1 * C).rearrange("p (k n) -> p k n", k=H1)
        bq = late(H1 * D1)
        bkv = late(2 * D1)
        bo = late(C)
        xwq = late(KC * C).rearrange("p (k n) -> p k n", k=KC)
        xwkv = late(KC * 2 * C).rearrange("p (k n) -> p k n", k=KC)
        wr = late(C)
        br = late(1)
        b1 = late(NFF)
        w1 = late(KC * DFF).rearrange("p (k n) -> p k n", k=KC)
        b2 = late(C)
        assert off[0] <= 16384

        Xc = sb("Xc", [P, 2, C])
        R = sb("R", [P, 2, C])
        XT = sb("XT", [P, 2, KC, P])
        WK = [sb(f"WK{i}", [P, 2, 2048]) for i in range(4)]
        xq = sb("xq", [P, 2, C], BF16)
        xqT = sb("xqT", [P, 2, KC, P], BF16)
        st = sb("st", [P, 2, 6])
        mv = sb("mv", [P, 2, 2])
        ve = sb("ve", [P, 2, 1])
        rstd = sb("rstd", [P, 2, 1])
        nmean = sb("nmean", [P, 2, 1])
        shift = sb("shift", [P, 2, 1])
        sm = sb("sm", [P, 2, 16])
        mx = sb("mx", [P, 2, 16])
        nmx = sb("nmx", [P, 2, 16])
        rec = sb("rec", [P, 2, 64])
        msq = sb("msq", [P, 2, 64])
        rms = sb("rms", [P, 2, 64])
        wsc = sb("wsc", [P, 4])
        d_skip = sb("d_skip", [P, HS])
        lg = sb("lg", [P, 2, NE])
        top = sb("top", [P, 2, 8])
        topi = sb("topi", [P, 2, 8], U32)
        topf = sb("topf", [P, 2, 8])
        dl = sb("dl", [P, 2, NE])
        ex = sb("ex", [P, 2, NE])
        chosen = sb("chosen", [P, 2, NE])
        cw = sb("cw", [P, 2, NE])

        def cst(name, n=None):
            lo, hi = CONST_AT[name]
            return const[:, lo:hi if n is None else lo + n]

        ident = cst("ident")
        ones = cst("ones")

        const_in, qkv_in, d_in, ctxT_in = (sem(n) for n in ("const_in", "qkv_in", "d_in", "ctxT_in"))
        w0_in, w2_in, w3_in, w4_in, w5_in = (sem(f"w{i}_in") for i in (0, 2, 3, 4, 5))
        bf_made = sem("bf_made")
        pads_clear = sem("pads_clear")
        w_abs, w_abs_sum, w_signed = (sem(n) for n in ("w_abs", "w_abs_sum", "w_signed"))
        x_in = [sem(f"x_in{p}") for p in range(2)]
        x_free = [sem(f"x_free{p}") for p in range(2)]
        stats = sem("stats")
        ln_scale = sem("ln_scale")
        normed = sem("normed")
        ctx_in = [sem(f"ctx_in{p}") for p in range(2)]
        toep_in = [sem(f"toep_in{p}") for p in range(2)]
        conv_w, conv_kv, conv_half, conv_mm, conv_out = (sem(n) for n in ("conv_w", "conv_kv", "conv_half", "conv_mm", "conv_out"))
        names = {
            "A": "xq xqT xqT_sb qkv deq qk_hi sub exp pv_lo pv_hi att ss rms xq2 xq2T xq2T_sb y",
            "B": "xT g o",
            "C": "xT xT_sb dl ex gu silu act aT aT_sb y",
            "D": "xT xT_sb kv kvb q qb rot half qkT qkT_sb s max exp rsum pn pT pT_sa pT_sv o o_sb y",
            "E": "xT xT_sb qkv sq pad qkT qT_sb kT_sb s exp oT oT_sb o",
            "F": "stored diag row rank keep ew esum pick gath gath_sb up gelu down ol pickT pickT_sb back stats rstd out",
        }
        S = {f"{stage}_{n}": sem(f"{stage}_{n}") for stage, text in names.items() for n in text.split()}

        def nth(j, p, per=1, k=1, before=0):
            return j * (2 * per) + (p * per + k + before)

        def staggered(eng, turn):
            turn((0, 0), None)
            turn((0, 1), (0, 0))
            with eng.Fori(1, PAIRS) as j:
                turn((j, 0), (j - 1, 1))
                turn((j, 1), (j, 0))
            turn(None, (PAIRS - 1, 1))

        def staggered3(eng, turn):
            turn((0, 0), None, None)
            turn((0, 1), (0, 0), None)
            with eng.Fori(1, PAIRS) as j:
                turn((j, 0), (j - 1, 1), (j - 1, 0))
                turn((j, 1), (j, 0), (j - 1, 1))
            turn(None, (PAIRS - 1, 1), (PAIRS - 1, 0))
            turn(None, None, (PAIRS - 1, 1))

        w = WK[0][:, :, :].rearrange("p a b -> p (a b)")
        F = {"diag": w[:, 0:1024].rearrange("p (b n) -> p b n", b=B),
             "tmp": w[:, 1024:2048].rearrange("p (b n) -> p b n", b=B),
             "pick": w[:, 2048:3072].rearrange("p (b n) -> p b n", b=B),
             "pickT": w[:, 3072:4096].rearrange("p (b n) -> p b n", b=B)}
        w = WK[1][:, :, :].rearrange("p a b -> p (a b)")
        F["R"] = w[:, 0:2048].rearrange("p (b n) -> p b n", b=B)
        F["gath"] = w[:, 2048:2304].rearrange("p (k n) -> p k n", k=KC)
        F["hid"] = w[:, 2304:3328].rearrange("p (k n) -> p k n", k=NFF)
        F["ol"] = w[:, 3328:3584]
        F["junk"] = w[:, 3584:3840]
        w = WK[2][:, 0, :]
        for i, n in enumerate(("logit", "max", "above", "tied", "rank", "keep", "e", "esum", "w", "ve", "rstd", "slot", "far")):
            F[n] = w[:, 8 * i:8 * i + 8]
        F["st"] = w[:, 128:176].rearrange("p (b n) -> p b n", b=B)
        F["mv"] = w[:, 192:208].rearrange("p (b n) -> p b n", b=B)

        HEADS_A_TURN = HS // PAIRS
        toep = WK[3][:, :, 1280:1536]

        def conv_kv_tile(c, l):
            return WK[0][:, c % 2, 1024 + l * 512:1536 + l * 512]

        def head(j, c, before=0):
            return j * HEADS_A_TURN + (c + 1 + before)

        def conv_products(eng, j, c, l):
            h = ctxT[:, :, l, :].rearrange("p b (h i) -> p b h i", i=DS)[:, :, j * HEADS_A_TURN + c, :]
            out = conv_kv_tile(c, l).rearrange("p (b i k) -> p b i k", b=B, i=DS)
            return eng.tensor_tensor(out, h.unsqueeze(3).broadcast_to([P, B, DS, DS]),
                                     h.unsqueeze(2).broadcast_to([P, B, DS, DS]), ALU.mult)

        def qk_products(eng, p, half):
            qkv = WK[0][:, p, 0:3 * C].rearrange("p (n h d) -> p n h d", n=3, h=H0)
            hs = slice(half * H0 // 2, (half + 1) * H0 // 2)
            return eng.tensor_tensor(WK[1 + half][:, p, :].rearrange("p (h g d) -> p h g d", h=H0 // 2, g=H0),
                                     qkv[:, 0, hs, :].unsqueeze(2).broadcast_to([P, H0 // 2, H0, D0]),
                                     qkv[:, 1, :, :].unsqueeze(1).broadcast_to([P, H0 // 2, H0, D0]), ALU.mult)

        def pv_products(eng, p, half):
            e = probs(p).rearrange("p (h g) -> p h g", h=H0)
            v = WK[0][:, p, 2 * C:3 * C].rearrange("p (g d) -> p d g", g=H0)
            hs = slice(half * H0 // 2, (half + 1) * H0 // 2)
            return eng.tensor_tensor(WK[1 + half][:, p, :].rearrange("p (h d g) -> p h d g", h=H0 // 2, d=D0),
                                     e[:, hs, :].unsqueeze(2).broadcast_to([P, H0 // 2, D0, H0]),
                                     v.unsqueeze(1).broadcast_to([P, H0 // 2, D0, H0]), ALU.mult)

        def att_q(p):
            return WK[3][:, p, 768:768 + C // 2].bitcast(BF16)

        def probs(p):
            return WK[3][:, p, 0:H0 * H0]

        def PT3(p, i):
            return WK[2][:, p, i * 512:(i + 1) * 512]

        late2 = gu_w[:, :, :].rearrange("p k n -> p (k n)")

        def ET(p, i):
            return late2[:, (4 * p + i) * 512:(4 * p + i + 1) * 512].bitcast(BF16)

        def parts(p):
            return WK[0][:, p, :].bitcast(BF16).rearrange("p (n h s d) -> p n h s d", n=2, h=H2, d=D2)

        def OT(p):
            return late2[:, 4096 + p * 1024:4096 + (p + 1) * 1024]

        def VP(p):
            return WK[3][:, p, 0:H2 * PAD].rearrange("p (h d) -> p h d", d=PAD)

        block = ctx.enter_context(nc.Block())

        @block.sync
        def _(sp):
            sp.dma_start(qkv_w, a["qkv_w"]).then_inc(qkv_in, 16)
            for dst, src in ((proj_w, a["proj_w"]), (qkv_b, rows("qkv_b", 3 * C)), (proj_b, rows("proj_b", C)),
                             (norm_w, rows("norm_w", C))):
                sp.dma_start(dst, src).then_inc(w0_in, 16)
            sp.dma_start(d_skip[:, :], rows("d_skip", HS)).then_inc(d_in, 16)
            for p in range(2):
                sp.sem_inc(x_free[p], 1)
            def load_turn(s, n):
                for p in range(2):
                    b = n * 2 + (p - 2 * PAIRS * s - 2)
                    if s:
                        sp.wait_ge(normed, n * 2 + (p - 2 * PAIRS * s - 2 + 1 + B * (s - 1) + 2))
                        src = X[:, b, :]
                    else:
                        src = a["x"][b, :, :]
                    sp.wait_ge(x_free[p], n)
                    sp.dma_start(Xc[:, p, :], src).then_inc(x_in[p], 16)
                    if s == 0:
                        for c in (2 * p, 2 * p + 1):
                            h = n * HEADS_A_TURN + (c - HEADS_A_TURN)
                            sp.wait_ge(conv_mm, n * HEADS_A_TURN + (c + 1 - HEADS_A_TURN))
                            sp.dma_start(toep[:, c % 2, :], a["toep"][h, :, :]).then_inc(toep_in[c % 2], 16)
                    if s == 4:
                        sp.wait_ge(S["E_qkv"], n * 2 + (p - 2 * PAIRS * s - 2 + 1))
                        sp.dma_start(CT[:, p, :, :], a["ctxT"][:, b, :, :]).then_inc(ctx_in[p], 16)

            with sp.Fori(1, PAIRS + 1) as n:
                load_turn(0, n)
            sp.wait_ge(S["A_deq"], B)
            sp.wait_ge(conv_kv, HS)
            sp.dma_start(down_w, a["down_w"]).then_inc(w2_in, 16)
            with sp.Fori(PAIRS + 1, 2 * PAIRS + 1) as n:
                load_turn(1, n)
            layer1 = (((wq, a["wq"], w3_in), (wkv, a["wkv"], w3_in), (bkv, rows("bkv", 2 * D1), w3_in)),
                      ((wo, a["wo"], w3_in), (bq, rows("bq", H1 * D1), w3_in), (bo, rows("bo", C), w3_in)),
                      ((w2, a["w2"], w5_in), (xwq, a["xwq"], w4_in), (xwkv, a["xwkv"], w4_in)),
                      ((w1, a["w1"], w5_in), (b1, a["b1"], w5_in), (b2, rows("b2", C), w5_in),
                       (wr, rows("wr", C), w5_in), (br, rows("br", 1), w5_in)))
            for turn, weights in enumerate(layer1):
                load_turn(2, 2 * PAIRS + 1 + turn)
                if turn == 0:
                    sp.wait_ge(S["B_g"], 2 * B)
                for dst, src, loaded in weights:
                    sp.dma_start(dst, src).then_inc(loaded, 16)
            for s in (3, 4):
                with sp.Fori(PAIRS * s + 1, PAIRS * (s + 1) + 1) as n:
                    load_turn(s, n)
            for b in range(B):
                sp.wait_ge(S["F_out"], b + 1)
                sp.dma_start(a["out"][b, :, :], X[:, b, :]).then_inc(S["F_stored"], 16)
            sp.wait_ge(S["F_stored"], 16 * B)

        @block.gpsimd
        def _(pool):
            def norm_tail(j, p, s):
                pool.wait_ge(stats, nth(j, p, before=B * s))
                pool.tensor_tensor(ve[:, p, :], mv[:, p, 1:2], cst("ln_eps"), ALU.add)
                pool.drain()
                pool.tensor_tensor(rstd[:, p, :], ve[:, p, :], cst("minus_half", 1), ALU.pow)
                pool.drain()
                if isinstance(j, int):
                    pool.tensor_scalar(X[:, j * 2 + p, :], R[:, p, :], mv[:, p, 0:1], rstd[:, p, :], ALU.subtract, ALU.mult)\
                        .then_inc(normed, 1)
                    return
                pool.tensor_scalar(R[:, p, :], R[:, p, :], mv[:, p, 0:1], rstd[:, p, :], ALU.subtract, ALU.mult)
                pool.drain()
                pool.tensor_copy(X[:, j * 2 + p, :], R[:, p, :]).then_inc(normed, 1)

            pool.wait_ge(const_in, 16)
            pool.wait_ge(ctxT_in, 16)
            def conv_heads(j, cs):
                for c in cs:
                    pool.wait_ge(conv_mm, head(j, c))
                    conv_products(pool, j, c, 0)
                    conv_products(pool, j, c, 1).then_inc(conv_kv, 1)

            def ln_factors(j, p, s):
                pool.wait_ge(stats, nth(j, p, before=B * s))
                pool.tensor_tensor(ve[:, p, :], mv[:, p, 1:2], cst("ln_eps"), ALU.add)
                pool.tensor_tensor(nmean[:, p, :], mv[:, p, 0:1], cst("minus_one"), ALU.mult)
                pool.drain()
                pool.tensor_tensor(rstd[:, p, :], ve[:, p, :], cst("minus_half", 1), ALU.pow)
                pool.drain()
                pool.tensor_tensor(shift[:, p, :], nmean[:, p, :], rstd[:, p, :], ALU.mult).then_inc(ln_scale, 1)

            def turn(new, old, older):
                if old:
                    j, p = old
                    pool.wait_ge(S["A_exp"], nth(j, p))
                    pv_products(pool, p, 1).then_inc(S["A_pv_hi"], 1)
                if older:
                    ln_factors(*older, 0)
                if new:
                    j, p = new
                    pool.wait_ge(S["A_deq"], nth(j, p))
                    qk_products(pool, p, 1).then_inc(S["A_qk_hi"], 1)
                    conv_heads(j, (2 * p, 2 * p + 1))
                if old:
                    j, p = old
                    pool.wait_ge(S["A_ss"], nth(j, p))
                    pool.tensor_tensor(rms[:, p, 0:1], sm[:, p, 4:5], cst("minus_half", 1), ALU.pow).then_inc(S["A_rms"], 1)
            staggered3(pool, turn)

            def turn(new, old):
                if old:
                    ln_factors(*old, 1)

            staggered(pool, turn)
            pool.wait_ge(normed, 2 + 2 * B)

            def turn(new, old):
                if new:
                    p = new[1]
                    pool.wait_ge(S["C_dl"], nth(*new))
                    pool.tensor_tensor(ex[:, p, :], cst("euler"), dl[:, p, :], ALU.pow).then_inc(S["C_ex"], 1)
                if old:
                    norm_tail(*old, 2)

            staggered(pool, turn)
            def rotate_half(j, p):
                q = WK[0][:, p, :].rearrange("p (h t d) -> p h t d", h=H1, t=2)
                o = WK[1][:, p, :].rearrange("p (h t d) -> p h t d", h=H1, t=2)
                sin = cst("sin").rearrange("p (t d) -> p t d", t=2)
                for i in range(4):
                    pool.wait_ge(S["D_qb"], nth(j, p, 4, i + 1))
                    hs = slice(4 * i, 4 * i + 4)
                    for t in range(2):
                        last = pool.tensor_tensor(o[:, hs, t, :], q[:, hs, 1 - t, :],
                                                  sin[:, t:t + 1, :].broadcast_to([P, 4, D1 // 2]), ALU.mult)
                    last.then_inc(S["D_half"], 1)

            def divide(j, p):
                e = WK[1][:, p, :].rearrange("p (h k) -> p h k", h=H1)
                for i in range(4):
                    hs = slice(4 * i, 4 * i + 4)
                    pool.wait_ge(S["D_rsum"], nth(j, p, 4, i + 1))
                    pool.tensor_tensor(e[:, hs, :], e[:, hs, :], rec[:, p, hs].unsqueeze(2).broadcast_to([P, 4, T]), ALU.mult)\
                        .then_inc(S["D_pn"], 1)

            def turn(new, old):
                if old:
                    divide(*old)
                if new:
                    rotate_half(*new)
                if old:
                    norm_tail(*old, 3)

            def pads(p):
                pool.wait_ge(S["D_y"], B - 1 + p)
                pool.memset(WK[0][:, p, :].rearrange("p (h d) -> p h d", d=32)[:, :, 3 * D2:], 0.0)
                pool.memset(VP(p)[:, :, D2:D2 + 1], 1.0)
                pool.memset(VP(p)[:, :, D2 + 1:], 0.0).then_inc(pads_clear, 1)

            staggered(pool, turn)
            for p in range(2):
                pads(p)
            def turn(new, old):
                if old:
                    norm_tail(*old, 4)

            staggered(pool, turn)
            pool.wait_ge(S["F_stats"], B)
            pool.tensor_scalar(F["ve"], F["mv"][:, :, 1], LN_EPS, None, ALU.add)
            pool.drain()
            pool.tensor_tensor(F["rstd"], F["ve"], cst("minus_half", B), ALU.pow).then_inc(S["F_rstd"], 1)

        @block.vector
        def _(dve):
            def ln_stats(j, p, s):
                dve.drain()
                dve.bn_stats(st[:, p, :], R[:, p, :])
                dve.drain()
                dve.bn_aggr(mv[:, p, :], st[:, p, :]).then_inc(stats, 1)

            def r_free(j, p, s):
                dve.wait_ge(normed, nth(j, p, before=B * s))

            def quantise(j, p, src, dst, scale, wcol):
                dve.tensor_reduce(sm[:, p, scale:scale + 1], src, AX.X, ALU.max, apply_absolute_value=True)
                dve.drain()
                dve.tensor_scalar(sm[:, p, scale:scale + 1], sm[:, p, scale:scale + 1], TINY, None, ALU.max)
                dve.drain()
                dve.reciprocal(sm[:, p, 3:4], sm[:, p, scale:scale + 1])
                dve.tensor_scalar(sm[:, p, scale + 1:scale + 2], sm[:, p, scale:scale + 1], wsc[:, wcol:wcol + 1],
                                  1.0 / QMAX, ALU.mult, ALU.mult)
                dve.drain()
                dve.tensor_scalar(XN_q[:, p, :], src, sm[:, p, 3:4], QMAX, ALU.mult, ALU.mult)
                dve.drain()
                return dve.tensor_scalar(dst, XN_q[:, p, :], ROUND, -ROUND, ALU.add, ALU.add)

            XN_q = WK[3][:, :, 1024:1280]

            dve.wait_ge(const_in, 16)
            dve.tensor_copy(ident_bf[:, :], ident)
            dve.tensor_copy(causal_bf[:, :], cst("causal")).then_inc(bf_made, 1)
            dve.wait_ge(d_in, 16)
            dve.wait_ge(qkv_in, 16)
            dve.tensor_reduce(wsc[:, 0:1], qkv_w, AX.XY, ALU.add, apply_absolute_value=True)
            dve.wait_ge(w0_in, 64)
            dve.tensor_reduce(wsc[:, 1:2], proj_w, AX.XY, ALU.add, apply_absolute_value=True).then_inc(w_abs, 1)
            dve.wait_ge(w_abs_sum, 1)
            dve.tensor_scalar(wsc[:, 2:3], bank(1, 3)[:, 0:1], 1.0 / (3 * C * C), TINY, ALU.mult, ALU.max)
            dve.tensor_scalar(wsc[:, 3:4], bank(1, 3)[:, 1:2], 1.0 / (C * C), TINY, ALU.mult, ALU.max)
            dve.drain()

            def conv_taps(j, cs):
                for c in cs:
                    dve.wait_ge(toep_in[c % 2], j * 32 + (16 * (c // 2) + 16))
                    dve.scalar_tensor_tensor(toep[:, c % 2, 0:P], ident, d_skip[:, bass.ds(j * HEADS_A_TURN + c, 1)],
                                             toep[:, c % 2, 0:P], ALU.mult, ALU.add).then_inc(conv_w, 1)

            def quantise_x(j, p):
                dve.wait_ge(x_in[p], j * 16 + 16)
                quantise(j, p, Xc[:, p, :], xq[:, p, :], 0, 2).then_inc(S["A_xq"], 1)

            def dequantise(j, p):
                dve.wait_ge(S["A_qkv"], nth(j, p))
                dve.scalar_tensor_tensor(WK[0][:, p, 0:2 * C], bank(p, 1), sm[:, p, 1:2], qkv_b[:, 0:2 * C],
                                         ALU.mult, ALU.add)
                dve.scalar_tensor_tensor(WK[0][:, p, 2 * C:3 * C], bank(p, 2)[:, 0:C], sm[:, p, 1:2],
                                         qkv_b[:, 2 * C:3 * C], ALU.mult, ALU.add).then_inc(S["A_deq"], 1)
                dve.drain()

            def scores(j, p):
                e = probs(p).rearrange("p (h g) -> p h g", h=H0)
                qk_products(dve, p, 0)
                dve.drain()
                for half in range(2):
                    if half:
                        dve.wait_ge(S["A_qk_hi"], nth(j, p))
                    dve.tensor_reduce(probs(p)[:, half * P:(half + 1) * P],
                                      WK[1 + half][:, p, :].rearrange("p (n d) -> p n d", d=D0), AX.X, ALU.add)
                dve.drain()
                dve.tensor_reduce(mx[:, p, :], e, AX.X, ALU.max)
                dve.drain()
                dve.tensor_tensor(e, e, mx[:, p, :].unsqueeze(2).broadcast_to([P, H0, H0]), ALU.subtract)\
                    .then_inc(S["A_sub"], 1)

            def start_residual(j, p, bias):
                r_free(j, p, 0)
                dve.tensor_tensor(R[:, p, :], Xc[:, p, :], bias, ALU.add).then_inc(x_free[p], 1)

            def weighted_v(j, p):
                dve.wait_ge(S["A_exp"], nth(j, p))
                pv_products(dve, p, 0).then_inc(S["A_pv_lo"], 1)
                dve.tensor_reduce(nmx[:, p, :], probs(p).rearrange("p (h g) -> p h g", h=H0), AX.X, ALU.add)
                dve.drain()
                dve.reciprocal(rec[:, p, 0:H0], nmx[:, p, :])
                dve.drain()

            def attended(j, p):
                att = WK[3][:, p, 512:512 + C]
                dve.wait_ge(S["A_att"], nth(j, p))
                dve.tensor_tensor(att.rearrange("p (h d) -> p h d", d=D0),
                                  bank(p, 1)[:, 0:C].rearrange("p (h d) -> p h d", d=D0),
                                  rec[:, p, 0:H0].unsqueeze(2).broadcast_to([P, H0, D0]), ALU.mult)
                dve.drain()
                dve.tensor_tensor_reduce(XN_q[:, p, :], att, att, 1.0 / C, RMS_EPS, ALU.mult, ALU.add, sm[:, p, 4:5])\
                    .then_inc(S["A_ss"], 1)

            def quantise_att(j, p):
                att = WK[3][:, p, 512:512 + C]
                dve.wait_ge(S["A_rms"], nth(j, p))
                dve.scalar_tensor_tensor(att, att, rms[:, p, 0:1], norm_w, ALU.mult, ALU.mult)
                dve.drain()
                quantise(j, p, att, att_q(p), 5, 3).then_inc(S["A_xq2"], 1)

            def residual(j, p):
                dve.wait_ge(S["A_y"], nth(j, p))
                dve.scalar_tensor_tensor(R[:, p, :], bank(p, 2)[:, 0:C], sm[:, p, 6:7], R[:, p, :], ALU.mult, ALU.add)
                ln_stats(j, p, 0)

            def turn(new, old, older):
                if new:
                    quantise_x(*new)
                if older:
                    residual(*older)
                if old:
                    weighted_v(*old)
                if new:
                    start_residual(*new, proj_b)
                    dequantise(*new)
                    scores(*new)
                    conv_taps(new[0], (2 * new[1], 2 * new[1] + 1))
                if old:
                    attended(*old)
                    quantise_att(*old)

            staggered3(dve, turn)

            dve.wait_ge(conv_out, 2 + 2 * HS)

            def gate(j, p):
                dve.wait_ge(S["B_xT"], nth(j, p))
                for l in range(2):
                    dve.tensor_tensor(WK[0][:, p, l * 1024:(l + 1) * 1024].rearrange("p (i h j) -> p h i j", i=DS, j=DS),
                                      Y[:, l, j * 2 + p, :].rearrange("p (h i j) -> p h i j", i=DS, j=DS),
                                      bank(p, 0)[:, l * P:(l + 1) * P].rearrange("p (h i) -> p h i", i=DS)
                                      .unsqueeze(3).broadcast_to([P, HS, DS, DS]), ALU.mult)\
                        .then_inc(S["B_g"], 1)
                r_free(j, p, 1)
                dve.tensor_copy(R[:, p, :], Xc[:, p, :]).then_inc(x_free[p], 1)
                dve.drain()

            def residual(j, p):
                dve.wait_ge(S["B_o"], nth(j, p))
                dve.tensor_tensor(R[:, p, :], bank(p, 1)[:, 0:C], R[:, p, :], ALU.add)
                ln_stats(j, p, 1)

            def turn(new, old):
                if new:
                    gate(*new)
                if old:
                    residual(*old)

            staggered(dve, turn)

            NU = NE + 1
            def unit(p, e):
                n = NE + 2 * FE if e == 0 else 2 * FE
                return bank(p, e % 4)[:, n - 2 * FE:n]

            def route(j, p):
                dve.wait_ge(S["C_gu"], nth(j, p, NU, 1))
                dve.tensor_copy(lg[:, p, :], bank(p, 0)[:, 0:NE])
                dve.drain()
                dve.max(top[:, p, :], lg[:, p, :])
                dve.drain()
                dve.tensor_scalar(dl[:, p, :], lg[:, p, :], top[:, p, 0:1], None, ALU.subtract).then_inc(S["C_dl"], 1)
                dve.max_index(topi[:, p, :], top[:, p, :], lg[:, p, :])
                dve.drain()
                dve.tensor_copy(topf[:, p, :], topi[:, p, :])
                dve.drain()
                dve.tensor_scalar(chosen[:, p, :], cst("iota", NE), topf[:, p, 0:1], None, ALU.is_equal)
                dve.drain()
                dve.scalar_tensor_tensor(chosen[:, p, :], cst("iota", NE), topf[:, p, 1:2], chosen[:, p, :],
                                         ALU.is_equal, ALU.add)
                r_free(j, p, 2)
                dve.tensor_copy(R[:, p, :], Xc[:, p, :]).then_inc(x_free[p], 1)
                dve.wait_ge(S["C_ex"], nth(j, p))
                dve.reduce_sum(sm[:, p, 0:1], ex[:, p, :], axis=AX.X)
                dve.drain()
                dve.reciprocal(sm[:, p, 1:2], sm[:, p, 0:1])
                dve.drain()
                dve.scalar_tensor_tensor(cw[:, p, :], ex[:, p, :], sm[:, p, 1:2], chosen[:, p, :], ALU.mult, ALU.mult)
                dve.drain()

            def activate(j, p):
                for e in range(NU):
                    dve.wait_ge(S["C_silu"], nth(j, p, NU, e + 1))
                    if e < NE:
                        i = dve.scalar_tensor_tensor(WK[1][:, p, e * FE:(e + 1) * FE], WK[0][:, p, e * FE:(e + 1) * FE],
                                                     cw[:, p, e:e + 1], unit(p, e)[:, FE:2 * FE], ALU.mult, ALU.mult)
                    else:
                        i = dve.tensor_tensor(WK[1][:, p, NE * FE:NF], WK[0][:, p, NE * FE:NF],
                                              bank(p, 1)[:, 0:FSH], ALU.mult)
                    i.then_inc(S["C_act"], 1)

            def residual(j, p):
                dve.wait_ge(S["C_y"], nth(j, p))
                dve.tensor_tensor(R[:, p, :], bank(p, 0)[:, 0:C], R[:, p, :], ALU.add)
                ln_stats(j, p, 2)

            def turn(new, old):
                if new:
                    route(*new)
                if old:
                    residual(*old)
                if new:
                    activate(*new)

            staggered(dve, turn)

            dve.wait_ge(w3_in, 96)
            def bias_kv(j, p):
                k = WK[3][:, p, 0:2 * D1]
                kt = WK[3][:, p, 2 * D1:3 * D1]
                sin = cst("sin")
                dve.wait_ge(S["D_kv"], nth(j, p))
                dve.tensor_tensor(k, bank(p, 0)[:, 0:2 * D1], bkv, ALU.add).then_inc(S["D_kvb"], 1)
                dve.drain()
                for t in range(2):
                    dve.tensor_tensor(kt[:, t * 64:t * 64 + 64], k[:, 64 - t * 64:128 - t * 64], sin[:, t * 64:t * 64 + 64], ALU.mult)
                dve.drain()
                dve.tensor_tensor(k[:, 0:D1], k[:, 0:D1], cst("cos"), ALU.mult)
                dve.drain()
                dve.tensor_tensor(k[:, 0:D1], k[:, 0:D1], kt, ALU.add)
                r_free(j, p, 3)
                dve.tensor_tensor(R[:, p, :], Xc[:, p, :], bo, ALU.add).then_inc(x_free[p], 1)

            def bias_q(j, p, i):
                q = WK[0][:, p, :]
                dve.wait_ge(S["D_q"], nth(j, p, 4, i + 1))
                dve.tensor_tensor(q[:, i * 512:(i + 1) * 512], bank(p, (i + 1) % 4), bq[:, i * 512:(i + 1) * 512],
                                  ALU.add).then_inc(S["D_qb"], 1)

            def times_cos(j, p):
                dve.drain()
                for i in range(4):
                    dve.tensor_tensor(WK[2][:, p, i * 512:(i + 1) * 512].rearrange("p (h d) -> p h d", d=D1),
                                      WK[0][:, p, i * 512:(i + 1) * 512].rearrange("p (h d) -> p h d", d=D1),
                                      cst("cos").unsqueeze(1).broadcast_to([P, 4, D1]), ALU.mult)

            def rotate(j, p, chunks):
                for i in chunks:
                    q = WK[0][:, p, i * 512:(i + 1) * 512]
                    dve.wait_ge(S["D_half"], nth(j, p, 4, i + 1))
                    dve.tensor_tensor(q, WK[2][:, p, i * 512:(i + 1) * 512], WK[1][:, p, i * 512:(i + 1) * 512], ALU.add)\
                        .then_inc(S["D_rot"], 1)

            def row_max(j, p):
                for i in range(4):
                    hs = slice(4 * i, 4 * i + 4)
                    dve.wait_ge(S["D_s"], nth(j, p, 4, i + 1))
                    dve.tensor_reduce(mx[:, p, hs], bank(p, (i + 1) % 4).rearrange("p (g t) -> p g t", g=4), AX.X, ALU.max)
                    dve.drain()
                    dve.tensor_scalar(nmx[:, p, hs], mx[:, p, hs], -(D1 ** -0.5), None, ALU.mult).then_inc(S["D_max"], 1)

            def one_over_sum(j, p, i):
                hs = slice(4 * i, 4 * i + 4)
                dve.wait_ge(S["D_exp"], nth(j, p, 4, i + 1))
                dve.reciprocal(rec[:, p, hs], msq[:, p, hs]).then_inc(S["D_rsum"], 1)

            def copy_pT(j, p):
                for i in range(2, 4):
                    dve.wait_ge(S["D_pT"], nth(j, p, 4, i + 1))
                    dve.tensor_copy(PT3(p, i), bank(p, (i + 1) % 4)).then_inc(S["D_pT_sv"], 1)

            def residual(j, p):
                dve.wait_ge(S["D_y"], nth(j, p))
                dve.tensor_tensor(R[:, p, :], bank(p, 1)[:, 0:C], R[:, p, :], ALU.add)
                ln_stats(j, p, 3)

            def turn(new, old):
                if old:
                    row_max(*old)
                    one_over_sum(*old, 0)
                if new:
                    bias_kv(*new)
                for i in range(1, 4):
                    if old:
                        one_over_sum(*old, i)
                    if new:
                        bias_q(*new, i - 1)
                if new:
                    bias_q(*new, 3)
                    times_cos(*new)
                if old:
                    copy_pT(*old)
                if new:
                    dve.drain()
                    rotate(*new, (0, 1, 2, 3))
                if old:
                    residual(*old)

            staggered(dve, turn)

            def inv_sqrt(x, y, t):
                dve.tensor_scalar(t.bitcast(I32), x.bitcast(I32), 1, None, ALU.logical_shift_right)
                dve.drain()
                dve.tensor_scalar(y.bitcast(I32), t.bitcast(I32), -1.0, float(0x5F3759DF), ALU.mult, ALU.add)
                for _ in range(3):
                    dve.drain()
                    dve.scalar_tensor_tensor(t, y, -0.5, y, ALU.mult, ALU.mult)
                    dve.drain()
                    dve.tensor_tensor(t, t, x, ALU.mult)
                    dve.drain()
                    dve.scalar_tensor_tensor(y, t, 1.5, y, ALU.add, ALU.mult)
                dve.drain()

            def normalise_qk(j, p):
                dve.wait_ge(S["E_sq"], nth(j, p))
                dve.tensor_reduce(msq[:, p, :], WK[2][:, p, 0:512].rearrange("p (h d) -> p h d", d=D2), AX.X, ALU.add)
                dve.drain()
                dve.tensor_scalar(msq[:, p, :], msq[:, p, :], RMS_EPS, None, ALU.add)
                dve.drain()
                inv_sqrt(msq[:, p, :], rms[:, p, :], rec[:, p, :])
                x = WK[2][:, p, 0:512].rearrange("p (n h d) -> p n h d", n=2, d=D2)
                rest = WK[2][:, p, 512:1024].rearrange("p (n h d) -> p n h d", n=2, d=D2)
                qk = parts(p)
                dve.tensor_tensor(x, bank(p, 1).rearrange("p (n h d) -> p n h d", n=2, d=D2),
                                  rms[:, p, :].rearrange("p (n h) -> p n h", n=2).unsqueeze(3).broadcast_to([P, 2, H2, D2]),
                                  ALU.mult)
                dve.drain()
                for n, slots in ((0, slice(0, 3)), (1, slice(2, 5))):
                    dve.tensor_copy(qk[:, n, :, slots, :], x[:, n, :, :].unsqueeze(2).broadcast_to([P, H2, 3, D2]))
                dve.drain()
                dve.tensor_tensor(rest, x, qk[:, :, :, 2, :], ALU.subtract)
                dve.drain()
                for n, slots in ((0, slice(3, 6, 2)), (1, slice(1, 6, 4))):
                    dve.tensor_copy(qk[:, n, :, slots, :], rest[:, n, :, :].unsqueeze(2).broadcast_to([P, H2, 2, D2]))
                dve.drain()
                for n, slot in ((0, 4), (1, 0)):
                    last = dve.tensor_tensor(qk[:, n, :, slot, :], rest[:, n, :, :], qk[:, n, :, 5, :], ALU.subtract)
                last.then_inc(S["E_pad"], 1)
                r_free(j, p, 4)
                dve.tensor_copy(R[:, p, :], Xc[:, p, :]).then_inc(x_free[p], 1)

            def residual(j, p):
                dve.wait_ge(S["E_o"], nth(j, p))
                o = PS[:, 4 * p + 2:4 * p + 4, :].rearrange("p k (h d) -> p (k h) d", d=PAD)
                dve.reciprocal(rec[:, p, 0:H2], o[:, :, D2])
                dve.drain()
                att = WK[3][:, p, H2 * PAD:H2 * PAD + C]
                dve.tensor_tensor(att.rearrange("p (h d) -> p h d", d=D2), o[:, :, 0:D2],
                                  rec[:, p, 0:H2].unsqueeze(2).broadcast_to([P, H2, D2]), ALU.mult)
                dve.drain()
                dve.tensor_tensor(R[:, p, :], R[:, p, :], att, ALU.add)
                ln_stats(j, p, 4)

            def copy_kT(j, p):
                for i in range(2, 4):
                    dve.wait_ge(S["E_qkT"], nth(j, p, 4, i + 1))
                    last = dve.tensor_copy(ET(p, i), bank(p, i).bitcast(BF16))
                last.then_inc(S["E_kT_sb"], 1)

            def turn(new, old):
                if new:
                    normalise_qk(*new)
                if old:
                    residual(*old)
                if new:
                    copy_kT(*new)

            staggered(dve, turn)

            dve.wait_ge(w5_in, 96)
            for b in range(B):
                dve.wait_ge(normed, 2 + 4 * B + b + 1)
                dve.tensor_tensor_reduce(F["junk"], X[:, b, :], wr, 1.0, 0.0, ALU.mult, ALU.add, F["logit"][:, b:b + 1])
                dve.drain()
            dve.tensor_scalar(F["logit"], F["logit"], br, None, ALU.add)
            dve.drain()
            for b in range(B):
                last = dve.tensor_scalar(F["diag"][:, b, :], ident, F["logit"][:, b:b + 1], None, ALU.mult)
            last.then_inc(S["F_diag"], 1)
            row = PS[:, 0:2, :].rearrange("p k (b t) -> p (k b) t", b=4)
            dve.wait_ge(S["F_row"], 1)
            dve.tensor_reduce(F["max"], row, AX.X, ALU.max)
            for b in range(B):
                dve.tensor_scalar(F["tmp"][:, b, :], row[:, b, :], F["logit"][:, b:b + 1], 0.0, ALU.is_gt, ALU.add,
                                  accum_out=F["above"][:, b:b + 1])
            dve.drain()
            for b in range(B):
                dve.scalar_tensor_tensor(F["tmp"][:, b, :], row[:, b, :], F["logit"][:, b:b + 1], cst("before"),
                                         ALU.is_equal, ALU.mult, accum_out=F["tied"][:, b:b + 1])
            dve.drain()
            dve.tensor_tensor(F["rank"], F["above"], F["tied"], ALU.add)
            dve.tensor_tensor(F["e"], F["logit"], F["max"], ALU.subtract).then_inc(S["F_rank"], 1)
            dve.drain()
            dve.tensor_scalar(F["keep"], F["rank"], float(TOPK), None, ALU.is_lt)
            dve.tensor_scalar(F["far"], F["rank"], float(TOPK), 1000.0, ALU.is_ge, ALU.mult)
            dve.tensor_tensor(F["slot"], F["rank"], cst("first_slot"), ALU.add)
            dve.drain()
            dve.tensor_tensor(F["slot"], F["slot"], F["far"], ALU.add)
            dve.drain()
            for b in range(B):
                last = dve.tensor_scalar(F["pick"][:, b, :], cst("iota"), F["slot"][:, b:b + 1], None, ALU.is_equal)
            last.then_inc(S["F_pick"], 1)
            dve.wait_ge(S["F_ew"], 1)
            dve.tensor_tensor(F["e"], F["e"], F["keep"], ALU.mult).then_inc(S["F_keep"], 1)
            dve.wait_ge(S["F_esum"], 1)
            dve.reciprocal(F["esum"], PS[:, 7, 0:B])
            dve.drain()
            dve.tensor_tensor(F["w"], F["e"], F["esum"], ALU.mult)
            dve.tensor_scalar(F["R"], X[:, :, :], 2.0, None, ALU.mult)
            dve.wait_ge(S["F_pickT"], 1)
            dve.tensor_copy(F["pickT"].rearrange("p b n -> p (b n)"), PS[:, 4:6, :].rearrange("p k n -> p (k n)"))\
                .then_inc(S["F_pickT_sb"], 1)
            dve.wait_ge(S["F_down"], 1)
            dve.tensor_tensor(F["ol"], PS[:, 6, 0:C], b2, ALU.add).then_inc(S["F_ol"], 1)
            for b in range(B):
                dve.wait_ge(S["F_back"], b + 1)
                dve.scalar_tensor_tensor(F["R"][:, b, :], PS[:, b, 0:C], F["w"][:, b:b + 1],
                                         F["R"][:, b, :], ALU.mult, ALU.add)
            dve.drain()
            for b in range(B):
                dve.bn_stats(F["st"][:, b, :], F["R"][:, b, :])
            dve.drain()
            for b in range(B):
                dve.bn_aggr(F["mv"][:, b, :], F["st"][:, b, :]).then_inc(S["F_stats"], 1)
            dve.wait_ge(S["F_rstd"], 1)
            for b in range(B):
                dve.tensor_scalar(X[:, b, :], F["R"][:, b, :], F["mv"][:, b, 0:1], F["rstd"][:, b:b + 1],
                                  ALU.subtract, ALU.mult).then_inc(S["F_out"], 1)

        @block.scalar
        def _(act):
            def copy(dst, src):
                return act.activation(dst, src, ACT.Copy)

            act.dma_start(const[:, :], a["const"]).then_inc(const_in, 16)
            act.sem_inc(conv_out, 2)
            act.sem_inc(normed, 2)

            def normalise(j, p, s):
                act.wait_ge(ln_scale, nth(j, p, before=B * s))
                act.activation(X[:, j * 2 + p, :], R[:, p, :], ACT.Identity, bias=shift[:, p, :], scale=rstd[:, p, :])\
                    .then_inc(normed, 1)

            def conv_copies(j, cs):
                for c in cs:
                    for l in range(2):
                        act.wait_ge(conv_half if l == 0 else conv_mm, head(j, c, before=2 * l))
                        copy(Y[:, l, :, :].rearrange("p b (h n) -> p b h n", h=HS)[:, :, j * HEADS_A_TURN + c, :],
                             bank(l, 3).rearrange("p (b n) -> p b n", b=B)).then_inc(conv_out, 1)

            act.wait_ge(qkv_in, 16)
            act.dma_start(ctxT, a["ctxT"]).then_inc(ctxT_in, 16)
            act.activation(qkv_sign, qkv_w, ACT.Sign)
            act.wait_ge(w0_in, 64)
            act.dma_start(gu_w[:, :, :], a["gu_w"]).then_inc(w2_in, 16)
            act.activation(proj_sign, proj_w, ACT.Sign).then_inc(w_signed, 1)
            def copy_xqT(j, p, made, copied):
                act.wait_ge(made, nth(j, p))
                copy(xqT[:, p, :, :].rearrange("p k t -> p (k t)"),
                     bank(p, 0 if made is S["A_xqT"] else 1)[:, 0:P].bitcast(BF16)).then_inc(copied, 1)

            def turn(new, old, older):
                if new:
                    copy_xqT(*new, S["A_xqT"], S["A_xqT_sb"])
                if older:
                    normalise(*older, 0)
                if old:
                    conv_copies(old[0], (2 * old[1] + 1,))
                if new:
                    j, p = new
                    act.wait_ge(S["A_sub"], nth(j, p))
                    act.activation(probs(p), probs(p), ACT.Exp, scale=D0 ** -0.5).then_inc(S["A_exp"], 1)
                    conv_copies(new[0], (2 * new[1],))
                if old:
                    copy_xqT(*old, S["A_xq2T"], S["A_xq2T_sb"])

            staggered3(act, turn)

            def turn(new, old):
                if old:
                    normalise(*old, 1)

            staggered(act, turn)

            def xt_copy(j, p, stage):
                act.wait_ge(S[f"{stage}_xT"], nth(j, p))
                copy(XT[:, p, :, :].rearrange("p k t -> p (k t)"), bank(p, 0)[:, 0:C]).then_inc(S[f"{stage}_xT_sb"], 1)

            NU = NE + 1
            def silu(j, p, units):
                for e in units:
                    act.wait_ge(S["C_gu"], nth(j, p, NU, e + 1))
                    n = FE if e < NE else FSH
                    at = NE if e == 0 else 0
                    act.activation(WK[0][:, p, e * FE:e * FE + n], bank(p, e % 4)[:, at:at + n], ACT.Silu).then_inc(S["C_silu"], 1)

            def copy_aT(j, p):
                for i in range(4):
                    act.wait_ge(S["C_aT"], nth(j, p, 4, i + 1))
                    if i < 3:
                        last = copy(WK[2][:, p, i * 512:(i + 1) * 512], bank(p, i))
                    else:
                        copy(WK[2][:, p, 1536:1664], bank(p, 3)[:, 0:P])
                        last = copy(WK[2][0:NF - 13 * P, p, 1664:1792], bank(p, 3)[0:NF - 13 * P, P:2 * P])
                last.then_inc(S["C_aT_sb"], 1)

            def turn(new, old):
                if new:
                    xt_copy(*new, "C")
                if old:
                    copy_aT(*old)
                if new:
                    act.wait_ge(S["C_dl"], nth(*new))
                    silu(*new, range(NU))

            staggered(act, turn)
            def copy_kT(j, p):
                act.wait_ge(S["D_qkT"], nth(j, p, 5, 1))
                copy(WK[3][:, p, 512:512 + P], bank(p, 0)[:, 0:P]).then_inc(S["D_qkT_sb"], 1)

            def copy_qT(j, p):
                for i in range(4):
                    act.wait_ge(S["D_qkT"], nth(j, p, 5, i + 2))
                    copy(WK[2][:, p, i * 512:(i + 1) * 512], bank(p, (i + 1) % 4)).then_inc(S["D_qkT_sb"], 1)

            def exponentials(j, p):
                for i in range(4):
                    act.wait_ge(S["D_max"], nth(j, p, 4, i + 1))
                    for n in range(4):
                        h = 4 * i + n
                        last = act.activation(WK[1][:, p, h * T:(h + 1) * T], bank(p, (i + 1) % 4)[:, n * T:(n + 1) * T],
                                              ACT.Exp, bias=nmx[:, p, h:h + 1], scale=D1 ** -0.5,
                                              accum_out=msq[:, p, h:h + 1])
                    last.then_inc(S["D_exp"], 1)

            def copy_pT(j, p):
                for i in range(2):
                    act.wait_ge(S["D_pT"], nth(j, p, 4, i + 1))
                    copy(PT3(p, i), bank(p, i + 1)).then_inc(S["D_pT_sa"], 1)

            def copy_o(j, p):
                for i in range(4):
                    act.wait_ge(S["D_o"], nth(j, p, 4, i + 1))
                    copy(WK[0][:, p, i * 512:(i + 1) * 512], bank(p, (i + 1) % 4)).then_inc(S["D_o_sb"], 1)

            def turn(new, old):
                if new:
                    xt_copy(*new, "D")
                if old:
                    exponentials(*old)
                if old:
                    copy_pT(*old)
                if new:
                    copy_kT(*new)
                if old:
                    copy_o(*old)
                if new:
                    copy_qT(*new)

            staggered(act, turn)
            def squares(j, p):
                act.wait_ge(S["E_qkv"], nth(j, p, before=2))
                act.activation(WK[2][:, p, 0:512], bank(p, 1), ACT.Square, scale=D2 ** -0.5)
                copy(VP(p)[:, :, 0:D2],
                     bank(p, 0)[:, C:2 * C].rearrange("p (h d) -> p h d", d=D2)).then_inc(S["E_sq"], 1)

            def copy_qT(j, p):
                for i in range(2):
                    act.wait_ge(S["E_qkT"], nth(j, p, 4, i + 1))
                    last = copy(ET(p, i), bank(p, i).bitcast(BF16))
                last.then_inc(S["E_qT_sb"], 1)

            def exponentials(j, p, rd):
                for n in range(4 * rd, 4 * rd + 4):
                    act.wait_ge(S["E_s"], nth(j, p, 8, n + 1))
                    act.activation(WK[1 + n // 4][:, p, (n % 4) * 512:(n % 4 + 1) * 512], bank(p, n % 4), ACT.Exp,
                                   scale=D2 ** -0.5).then_inc(S["E_exp"], 1)

            def copy_oT(j, p):
                for i in range(2):
                    act.wait_ge(S["E_oT"], nth(j, p, 2, i + 1))
                    copy(OT(p)[:, i * 512:(i + 1) * 512], bank(p, i)).then_inc(S["E_oT_sb"], 1)

            def turn(new, old):
                if new:
                    xt_copy(*new, "E")
                    squares(*new)
                if old:
                    exponentials(*old, 0)
                    exponentials(*old, 1)
                    copy_oT(*old)
                if new:
                    copy_qT(*new)

            staggered(act, turn)
            act.wait_ge(S["F_rank"], 1)
            act.activation(F["e"], F["e"], ACT.Exp).then_inc(S["F_ew"], 1)
            act.activation(sm[:, 0, 15:16], cst("ones", 1), ACT.Gelu)
            act.wait_ge(S["F_gath"], 1)
            for k in range(KC):
                last = copy(F["gath"][:, k, :], PS[:, 2 + k, 0:P])
            last.then_inc(S["F_gath_sb"], 1)
            act.wait_ge(w5_in, 96)
            for f in range(NFF):
                act.wait_ge(S["F_up"], f + 1)
                act.activation(F["hid"][:, f, :], PS[:, f % 4, 0:P], ACT.Gelu,
                               bias=b1[:, f:f + 1]).then_inc(S["F_gelu"], 1)

        @block.tensor
        def _(pe):
            def turn_x(j, p, s, stage):
                pe.wait_ge(x_in[p], j * 16 + (s * 64 + 16))
                for k in range(KC):
                    last = pe.transpose(bank(p, 0)[:, k * P:(k + 1) * P], Xc[:, p, k * P:(k + 1) * P], ident)
                last.then_inc(S[f"{stage}_xT"], 1)

            pe.sem_inc(conv_mm, 2)
            pe.sem_inc(S["E_qkv"], 2)
            pe.wait_ge(const_in, 16)
            pe.wait_ge(bf_made, 1)
            pe.wait_ge(w_abs, 1)
            pe.matmul(bank(1, 3)[:, 0:2], ones, wsc[:, 0:2], start=True, stop=True).then_inc(w_abs_sum, 1)
            def conv_heads(j, cs):
                for c in cs:
                    near, far = toep[:, c % 2, 0:P], toep[:, c % 2, P:2 * P]
                    pe.wait_ge(conv_w, head(j, c))
                    pe.wait_ge(conv_kv, head(j, c))
                    pe.wait_ge(conv_out, j * (2 * HEADS_A_TURN) + (2 * c + 1))
                    pe.matmul(bank(0, 3), near, conv_kv_tile(c, 0), start=True, stop=True).then_inc(conv_half, 1)
                    pe.wait_ge(conv_out, j * (2 * HEADS_A_TURN) + (2 * c + 2))
                    pe.matmul(bank(1, 3), near, conv_kv_tile(c, 1), start=True, stop=False)
                    pe.matmul(bank(1, 3), far, conv_kv_tile(c, 0), start=False, stop=True).then_inc(conv_mm, 1)

            pe.wait_ge(w_signed, 1)
            def transpose_xq(j, p, xq_p, k0, made, done):
                pe.wait_ge(made, nth(j, p))
                for k in range(KC):
                    last = pe.transpose(bank(p, k0)[:, 0:P].bitcast(BF16)[:, k * P:(k + 1) * P], xq_p[:, k * P:(k + 1) * P], ident_bf[:, :])
                last.then_inc(done, 1)

            def qkv(j, p):
                pe.wait_ge(S["A_xqT_sb"], nth(j, p))
                for n, (lo, hi) in enumerate(((0, 512), (512, 768))):
                    for k in range(KC):
                        last = pe.matmul(bank(p, 1 + n)[:, 0:hi - lo], xqT[:, p, k, :], qkv_sign[:, k, lo:hi],
                                         start=(k == 0), stop=(k == KC - 1))
                last.then_inc(S["A_qkv"], 1)

            def pv_sums(j, p):
                for half, made in enumerate((S["A_pv_lo"], S["A_pv_hi"])):
                    pe.wait_ge(made, nth(j, p))
                    for g in range(H0):
                        last = pe.matmul(bank(p, 1)[:, half * P:(half + 1) * P], ident,
                                         WK[1 + half][:, p, :].rearrange("p (n g) -> p g n", g=H0)[:, g, :],
                                         start=(g == 0), stop=(g == H0 - 1))
                last.then_inc(S["A_att"], 1)

            def project(j, p):
                pe.wait_ge(S["A_xq2T_sb"], nth(j, p))
                for k in range(KC):
                    last = pe.matmul(bank(p, 2)[:, 0:C], xqT[:, p, k, :], proj_sign[:, k, :], start=(k == 0), stop=(k == KC - 1))
                last.then_inc(S["A_y"], 1)

            def turn(new, old, older):
                if new:
                    transpose_xq(*new, xq[:, new[1], :], 0, S["A_xq"], S["A_xqT"])
                if older:
                    pe.wait_ge(stats, nth(*older))
                if new:
                    qkv(*new)
                if old:
                    conv_heads(old[0], (2 * old[1] + 1,))
                    pv_sums(*old)
                if new:
                    conv_heads(new[0], (2 * new[1],))
                if old:
                    transpose_xq(*old, att_q(old[1]), 1, S["A_xq2"], S["A_xq2T"])
                    project(*old)

            staggered3(pe, turn)

            def gated_sums(j, p):
                for l in range(2):
                    pe.wait_ge(S["B_g"], nth(j, p, 2, l + 1))
                    for i in range(DS):
                        c = l * 1024 + i * P
                        last = pe.matmul(bank(p, 1)[:, l * P:(l + 1) * P], WK[0][:, p, c:c + P], ident,
                                         start=(i == 0), stop=(i == DS - 1))
                last.then_inc(S["B_o"], 1)

            def turn(new, old):
                if new:
                    turn_x(*new, 1, "B")
                if old:
                    gated_sums(*old)

            staggered(pe, turn)

            NU = NE + 1
            pe.wait_ge(w2_in, 32)
            def gates(j, p, units):
                for e in units:
                    lo = NE + e * 2 * FE if e else 0
                    hi = NE + (e + 1) * 2 * FE
                    if e >= 4:
                        pe.wait_ge(S["C_act"], nth(j, p, NU, e - 3))
                    for k in range(KC):
                        last = pe.matmul(bank(p, e % 4)[:, 0:hi - lo], XT[:, p, k, :], gu_w[:, k, lo:hi],
                                         start=(k == 0), stop=(k == KC - 1))
                    last.then_inc(S["C_gu"], 1)

            def shared_gates(j, p):
                pe.wait_ge(S["C_act"], nth(j, p, NU, 6))
                for n in range(2):
                    c = NE + 2 * FE * NE + n * FSH
                    for k in range(KC):
                        last = pe.matmul(bank(p, n)[:, 0:FSH], XT[:, p, k, :], gu_w[:, k, c:c + FSH],
                                         start=(k == 0), stop=(k == KC - 1))
                last.then_inc(S["C_gu"], 1)

            def transpose_act(j, p):
                pe.wait_ge(S["C_act"], nth(j, p, NU, NU))
                for i in range(4):
                    for f in range(4 * i, min(4 * i + 4, NFT)):
                        w = min(P, NF - f * P)
                        last = pe.transpose(bank(p, i)[0:w, (f % 4) * P:(f % 4 + 1) * P], WK[1][:, p, f * P:f * P + w], ident)
                    last.then_inc(S["C_aT"], 1)

            def project_down(j, p):
                pe.wait_ge(S["C_aT_sb"], nth(j, p))
                for f in range(NFT):
                    w = min(P, NF - f * P)
                    last = pe.matmul(bank(p, 0)[:, 0:C], WK[2][0:w, p, f * P:(f + 1) * P], down_w[0:w, f, :],
                                     start=(f == 0), stop=(f == NFT - 1))
                last.then_inc(S["C_y"], 1)

            def turn(new, old):
                if new:
                    pe.wait_ge(stats, nth(new[0] - 1, new[1], before=2 * B))
                    turn_x(*new, 2, "C")
                if old:
                    transpose_act(*old)
                if new:
                    pe.wait_ge(S["C_xT_sb"], nth(*new))
                    gates(*new, (0,))
                if old:
                    project_down(*old)
                if new:
                    gates(*new, range(1, NE))
                    shared_gates(*new)

            staggered(pe, turn)
            pe.wait_ge(w3_in, 96)
            def keys_values(j, p):
                pe.wait_ge(S["D_xT_sb"], nth(j, p))
                for k in range(KC):
                    last = pe.matmul(bank(p, 0)[:, 0:2 * D1], XT[:, p, k, :], wkv[:, k, :], start=(k == 0), stop=(k == KC - 1))
                last.then_inc(S["D_kv"], 1)

            def queries(j, p):
                pe.wait_ge(stats, nth(j - 1, p, before=3 * B))
                for i in range(4):
                    if i == 3:
                        pe.wait_ge(S["D_kvb"], nth(j, p))
                    for k in range(KC):
                        last = pe.matmul(bank(p, (i + 1) % 4), XT[:, p, k, :], wq[:, k, i * 512:(i + 1) * 512],
                                         start=(k == 0), stop=(k == KC - 1))
                    last.then_inc(S["D_q"], 1)

            def transpose_k(j, p):
                pe.wait_ge(S["D_qb"], nth(j, p, 4, 4))
                pe.transpose(bank(p, 0)[:, 0:P], WK[3][:, p, 0:D1], ident).then_inc(S["D_qkT"], 1)

            def transpose_q(j, p, chunks):
                for i in chunks:
                    pe.wait_ge(S["D_rot"], nth(j, p, 4, i + 1))
                    if i == 3:
                        pe.wait_ge(S["D_qkT_sb"], nth(j, p, 5, 1))
                    for n in range(4):
                        c = (4 * i + n) * D1
                        last = pe.transpose(bank(p, (i + 1) % 4)[:, n * T:(n + 1) * T], WK[0][:, p, c:c + D1], ident)
                    last.then_inc(S["D_qkT"], 1)

            def scores(j, p):
                for i in range(4):
                    b = (i + 1) % 4
                    pe.wait_ge(S["D_qkT_sb"], nth(j, p, 5, i + 2))
                    pe.matmul(bank(p, b), ident_bf[:, :], causal_bf[:, :].unsqueeze(1).broadcast_to([P, 4, P]), start=True, stop=True)
                    for n in range(4):
                        c = (4 * i + n) * T
                        last = pe.matmul(bank(p, b)[:, n * T:(n + 1) * T], WK[2][:, p, c:c + T], WK[3][:, p, 512:512 + P],
                                         start=False, stop=True, skip_group_check=True)
                    last.then_inc(S["D_s"], 1)

            def transpose_p(j, p):
                for i in range(4):
                    pe.wait_ge(S["D_pn"], nth(j, p, 4, i + 1))
                    for n in range(4):
                        c = (4 * i + n) * T
                        last = pe.transpose(bank(p, (i + 1) % 4)[:, n * T:(n + 1) * T], WK[1][:, p, c:c + T], ident)
                    last.then_inc(S["D_pT"], 1)

            def heads_out(j, p):
                for i in range(4):
                    pe.wait_ge(S["D_pT_sa" if i < 2 else "D_pT_sv"], nth(j, p, 2, i % 2 + 1))
                    pe.matmul(bank(p, (i + 1) % 4), WK[3][:, p, D1:2 * D1], PT3(p, i), start=True, stop=True).then_inc(S["D_o"], 1)

            def project(j, p):
                for i in range(4):
                    pe.wait_ge(S["D_o_sb"], nth(j, p, 4, i + 1))
                    for h in range(4 * i, 4 * i + 4):
                        last = pe.matmul(bank(p, 1)[:, 0:C], WK[0][:, p, h * T:(h + 1) * T], wo[:, h, :],
                                         start=(h == 0), stop=(h == H1 - 1))
                last.then_inc(S["D_y"], 1)

            def turn(new, old):
                if new:
                    turn_x(*new, 3, "D")
                if old:
                    scores(*old)
                if new:
                    keys_values(*new)
                    queries(*new)
                if old:
                    transpose_p(*old)
                if new:
                    transpose_k(*new)
                if old:
                    heads_out(*old)
                if new:
                    transpose_q(*new, range(4))
                if old:
                    project(*old)

            staggered(pe, turn)
            pe.wait_ge(w4_in, 32)
            def keys_values(j, p):
                pe.wait_ge(ctx_in[p], j * 16 + 16)
                for k in range(KC):
                    pe.matmul(bank(p, 1)[:, C:2 * C], CT[:, p, k, :], xwkv[:, k, 0:C], start=(k == 0), stop=(k == KC - 1))
                for k in range(KC):
                    pe.matmul(bank(p, 0)[:, C:2 * C], CT[:, p, k, :], xwkv[:, k, C:2 * C], start=(k == 0), stop=(k == KC - 1))

            def queries(j, p):
                pe.wait_ge(S["E_xT_sb"], nth(j, p))
                for k in range(KC):
                    last = pe.matmul(bank(p, 1)[:, 0:C], XT[:, p, k, :], xwq[:, k, :], start=(k == 0), stop=(k == KC - 1))
                last.then_inc(S["E_qkv"], 1)

            def transpose_qk(j, p):
                pe.wait_ge(pads_clear, 1 + p)
                pe.wait_ge(S["E_pad"], nth(j, p))
                for i in range(4):
                    for n in range(8):
                        c = (8 * i + n) * P
                        last = pe.transpose(bank(p, i).bitcast(BF16)[:, n * P:(n + 1) * P], WK[0][:, p, :].bitcast(BF16)[:, c:c + P],
                                            ident_bf[:, :])
                    last.then_inc(S["E_qkT"], 1)

            def scores(j, p, rd):
                for r in range(4):
                    if rd:
                        pe.wait_ge(S["E_exp"], nth(j, p, 8, r + 1))
                    at = slice(64 * (r % 2), 64 * (r % 2) + 6 * D2)
                    for g in range(4):
                        c = (2 * g + r // 2) * P
                        last = pe.matmul(bank(p, r)[:, g * P:(g + 1) * P], ET(p, 2 + rd)[at, c:c + P],
                                         ET(p, rd)[at, c:c + P], start=True, stop=True)
                    last.then_inc(S["E_s"], 1)

            def heads_out(j, p, i):
                pe.wait_ge(S["E_exp"], nth(j, p, 8, 8 if i else 5))
                for g in range(4):
                    for r in range(4):
                        h = 16 * i + 4 * g + r
                        last = pe.matmul(bank(p, i)[PAD * r:PAD * (r + 1), g * P:(g + 1) * P], VP(p)[:, h, :],
                                         WK[1 + i][:, p, (4 * r + g) * P:(4 * r + g + 1) * P], start=True, stop=True)
                last.then_inc(S["E_oT"], 1)

            def transpose_o(j, p):
                for i in range(2):
                    pe.wait_ge(S["E_oT_sb"], nth(j, p, 2, i + 1))
                    for g in range(4):
                        last = pe.transpose(bank(p, 2 + i)[:, g * P:(g + 1) * P], OT(p)[:, (4 * i + g) * P:(4 * i + g + 1) * P], ident)
                last.then_inc(S["E_o"], 1)

            def turn(new, old, coming):
                if new:
                    turn_x(*new, 4, "E")
                    queries(*new)
                if old:
                    pe.wait_ge(S["E_qT_sb"], nth(*old))
                    pe.wait_ge(S["E_kT_sb"], nth(*old))
                    scores(*old, 0)
                    scores(*old, 1)
                    heads_out(*old, 0)
                    heads_out(*old, 1)
                    transpose_o(*old)
                if coming:
                    keys_values(*coming)
                if new:
                    transpose_qk(*new)

            pe.wait_ge(stats, 4 * B)
            keys_values(0, 0)
            turn((0, 0), None, (0, 1))
            turn((0, 1), (0, 0), (1, 0))
            with pe.Fori(1, PAIRS - 1) as j:
                turn((j, 0), (j - 1, 1), (j, 1))
                turn((j, 1), (j, 0), (j + 1, 0))
            turn((PAIRS - 1, 0), (PAIRS - 2, 1), (PAIRS - 1, 1))
            turn((PAIRS - 1, 1), (PAIRS - 1, 0), None)
            turn(None, (PAIRS - 1, 1), None)
            pe.wait_ge(S["F_diag"], 1)
            for b in range(B):
                last = pe.matmul(PS[:, b // 4, (b % 4) * P:(b % 4 + 1) * P], ones, F["diag"][:, b, :], start=True, stop=True)
            last.then_inc(S["F_row"], 1)
            pe.wait_ge(S["F_pick"], 1)
            for k in range(KC):
                for b in range(B):
                    last = pe.matmul(PS[:, 2 + k, 0:P], X[:, b, k * P:(k + 1) * P], F["pick"][:, b, :], start=(b == 0), stop=(b == B - 1))
            last.then_inc(S["F_gath"], 1)
            for b in range(B):
                last = pe.transpose(PS[:, 4 + b // 4, (b % 4) * P:(b % 4 + 1) * P], F["pick"][:, b, :], ident)
            last.then_inc(S["F_pickT"], 1)
            pe.wait_ge(S["F_keep"], 1)
            pe.matmul(PS[:, 7, 0:B], ones, F["e"], start=True, stop=True).then_inc(S["F_esum"], 1)
            pe.wait_ge(S["F_gath_sb"], 1)
            pe.wait_ge(w5_in, 96)
            for f in range(NFF):
                if f >= 4:
                    pe.wait_ge(S["F_gelu"], f - 3)
                for k in range(KC):
                    last = pe.matmul(PS[:, f % 4, 0:P], w1[:, k, f * P:(f + 1) * P], F["gath"][:, k, :],
                                     start=(k == 0), stop=(k == KC - 1))
                last.then_inc(S["F_up"], 1)
            for f in range(NFF):
                pe.wait_ge(S["F_gelu"], f + 1)
                last = pe.matmul(PS[:, 6, 0:C], F["hid"][:, f, :], w2[:, f, :], start=(f == 0), stop=(f == NFF - 1))
            last.then_inc(S["F_down"], 1)
            pe.wait_ge(S["F_pickT_sb"], 1)
            pe.wait_ge(S["F_ol"], 1)
            for b in range(B):
                pe.matmul(PS[:, b, 0:C], F["pickT"][:, b, :], F["ol"], start=True, stop=True)\
                    .then_inc(S["F_back"], 1)


def constants():
    c = np.zeros((P, NCONST), np.float32)

    def put(name, value):
        c[:, CONST_AT[name][0]:CONST_AT[name][1]] = value

    t = np.arange(P)
    put("ident", np.eye(P))
    put("ones", 1.0)
    put("before", t[None, :] < t[:, None])
    put("iota", t[None, :])
    put("causal", np.where(t[None, :] <= t[:, None], 0.0, -1e30))
    inv_freq = (1.0 / np.float32(10000.0) ** (np.arange(0, D1, 2, dtype=np.float32) / np.float32(D1))).astype(np.float32)
    ang = (t.astype(np.float32)[:, None] * inv_freq[None, :]).astype(np.float32)
    put("cos", np.tile(np.cos(ang), (1, 2)))
    put("sin", np.concatenate([-np.sin(ang), np.sin(ang)], axis=1))
    put("minus_half", -0.5)
    put("ln_eps", LN_EPS)
    put("minus_one", -1.0)
    put("euler", np.e)
    put("first_slot", TOPK * np.arange(B)[None, :])
    return c


def kernel(**inputs):
    import concourse.bacc as _bacc
    from concourse.bass_utils import run_bass_kernel_spmd as _run

    g = {k: np.asarray(v) for k, v in inputs.items()}

    def tiles(w):
        n = -(-w.shape[0] // P)
        if n * P != w.shape[0]:
            w = np.concatenate([w, np.zeros((n * P - w.shape[0], w.shape[1]), w.dtype)])
        return w.reshape(n, P, -1).transpose(1, 0, 2)

    halves = np.concatenate([np.arange(0, D1, 2), np.arange(1, D1, 2)])
    qcols = (np.arange(H1)[:, None] * D1 + halves[None, :]).ravel()
    xkv = np.concatenate([g["L1_xattn_Wk"], g["L1_xattn_Wv"]])
    taps = g["L0_xattn_ssm_kernel"]
    taps = np.concatenate([np.zeros((HS, P - 1), taps.dtype), taps], axis=1)
    toep = np.lib.stride_tricks.sliding_window_view(taps, C, axis=1)[:, ::-1, :]
    down = g["L0_ffn_down_weights"].transpose(0, 2, 1).reshape(NE * FE, C)
    gu = g["L0_ffn_gate_up_weights"].reshape(NE * 2 * FE, C)
    arrays = {
        "x": g["x"],
        "const": constants(),
        "ctxT": g["ctx_2048"].reshape(B, T, KC, P).transpose(3, 0, 2, 1),
        "d_skip": g["L0_xattn_D"],
        "toep": toep,
        "qkv_w": tiles(g["L0_attn_qkv_w"].T), "qkv_b": g["L0_attn_qkv_b"],
        "proj_w": tiles(g["L0_attn_proj_w"].T), "proj_b": g["L0_attn_proj_b"],
        "norm_w": g["L0_attn_norm_w"],
        "gu_w": tiles(np.concatenate([g["L0_ffn_gate_weight"], gu, g["L0_ffn_shared_gate_up"]]).T),
        "down_w": tiles(np.concatenate([down, g["L0_ffn_shared_down"].T])),
        "wq": tiles(g["L1_attn_Wq"][:, qcols]), "bq": g["L1_attn_bq"][qcols],
        "wkv": tiles(np.concatenate([g["L1_attn_Wk"][:, halves], g["L1_attn_Wv"]], axis=1)),
        "bkv": np.concatenate([g["L1_attn_bk"][halves], g["L1_attn_bv"]]),
        "wo": tiles(g["L1_attn_Wo"]), "bo": g["L1_attn_bo"],
        "xwq": tiles(g["L1_xattn_Wq"].T),
        "xwkv": tiles(np.concatenate([xkv[0::2], xkv[1::2]]).T),
        "wr": g["L1_ffn_Wr"][:, 0], "br": g["L1_ffn_br"],
        "w1": tiles(g["L1_ffn_W1"]), "b1": g["L1_ffn_b1"].reshape(NFF, P).T,
        "w2": tiles(g["L1_ffn_W2"]), "b2": g["L1_ffn_b2"],
    }
    arrays = {f"in_{k}": np.ascontiguousarray(v) for k, v in arrays.items()}
    nc = _bacc.Bacc("TRN2", target_bir_lowering=False, num_devices=1)
    a = {k[3:]: nc.dram_tensor(k, v.shape, F32, kind="ExternalInput").ap() for k, v in arrays.items()}
    a["out"] = nc.dram_tensor("out_0", (B, T, C), F32, kind="ExternalOutput").ap()
    build(nc, a)
    r = _run(nc, [arrays], core_ids=[0])
    return r.results[0]["out_0"]
```
